# Optimizing a Trainium2 kernel written in Bass

```python
import numpy as np
import jax
import jax.numpy as jnp

def _softmax(x, axis=-1):
    return jax.nn.softmax(x, axis=axis)

def _gelu(x):
    return jax.nn.gelu(x, approximate=True)

def _silu(x):
    return jax.nn.silu(x)

def _sigmoid(x):
    return jax.nn.sigmoid(x)

def _layernorm(x, axis=-1, eps=1e-05):
    m = jnp.mean(x, axis=axis, keepdims=True)
    v = jnp.var(x, axis=axis, keepdims=True)
    return (x - m) / jnp.sqrt(v + eps)

def _scatter_add(tgt, idx, src, axis=0):
    return tgt.at[idx].add(src)

def _segment_sum(src, seg, n):
    return jax.ops.segment_sum(src, seg, n)
kernel_name = 'mk_adj_resnorm_d4_adj_r2_d38b7b'

def setup_inputs(seed: int=0):
    np.random.seed(seed)
    _w = jnp.asarray

    def _rec_inputs():
        import jax
        import jax.numpy as jnp
        _gk = jax.random.key(seed)
        x = -9.806e-05 + 1 * jax.random.normal(jax.random.fold_in(_gk, 1), (4096, 128), jnp.float32)
        _a = jax.random.bernoulli(jax.random.fold_in(_gk, 2), 0.000976562, (4096, 4096))
        _a = jnp.logical_or(_a, jnp.eye(4096, dtype=bool))
        _af = _a.astype(jnp.float32)
        _af = _af * jax.random.uniform(jax.random.fold_in(_gk, 3), (4096, 4096), jnp.float32, 0.05, 1)
        adj = _af
        return (x, adj)
    x, adj = _rec_inputs()

    def _L0_gnn_setup():
        import jax, jax.numpy as jnp
        import numpy as np

        def _lap_mul(A, x):
            d = 1.0 / jnp.sqrt(jnp.sum(A, axis=-1))
            return d[:, None] * (A @ (d[:, None] * x))
        key = jax.random.key(seed)
        k1, k2, k3, k4, k5, k6 = jax.random.split(key, 6)
        N, D_IN, D_OUT = (2048, 128, 128)
        x = jax.random.normal(k1, (N, D_IN), dtype=jnp.float32)
        A = jax.random.uniform(k2, (N, N), dtype=jnp.float32)
        s1 = 1.0 / np.sqrt(D_IN)
        W1 = jax.random.uniform(k3, (D_IN, D_OUT), minval=-s1, maxval=s1, dtype=jnp.float32)
        b1 = jax.random.uniform(k4, (D_OUT,), minval=-s1, maxval=s1, dtype=jnp.float32)
        W2 = jax.random.uniform(k5, (D_IN, D_OUT), minval=-s1, maxval=s1, dtype=jnp.float32)
        b2 = jax.random.uniform(k6, (D_OUT,), minval=-s1, maxval=s1, dtype=jnp.float32)
        return {'x': x, 'A': A, 'W1': W1, 'b1': b1, 'W2': W2, 'b2': b2, 'sigma': 1, 'k': 4}
    _L0_gnn_all = _L0_gnn_setup()
    _L0_gnn_in = {k: v for k, v in _L0_gnn_all.items() if k in ('W1', 'b1', 'W2', 'b2')}
    del _L0_gnn_all

    def _L1_gnn_setup():
        import jax, jax.numpy as jnp
        import numpy as np
        N, IN, H, C = (2048, 128, 4, 32)
        HC = H * C
        EDGE_P = 0.008

        def _linear_params(key, fan_in, fan_out, bias=True):
            k1, k2 = jax.random.split(key)
            lim = 1.0 / np.sqrt(fan_in)
            W = jax.random.uniform(k1, (fan_in, fan_out), jnp.float32, -lim, lim)
            if not bias:
                return W
            b = jax.random.uniform(k2, (fan_out,), jnp.float32, -lim, lim)
            return (W, b)

        def _transformer_conv(x, adj, Wq, bq, Wk, bk, Wv, bv, Ws, bs, Wb):
            n = x.shape[0]
            q = (x @ Wq + bq).reshape(n, H, C)
            k = (x @ Wk + bk).reshape(n, H, C)
            v = (x @ Wv + bv).reshape(n, H, C)
            attn = jnp.einsum('nhc,mhc->hnm', q, k) / np.float32(np.sqrt(C))
            mask = adj == 0.0
            neg = jnp.where(mask[None], -jnp.inf, attn)
            m = jnp.max(neg, axis=-1, keepdims=True)
            all_inf = jnp.isneginf(m)
            e = jnp.where(mask[None], 0.0, jnp.exp(neg - jnp.where(all_inf, 0.0, m)))
            denom = jnp.sum(e, axis=-1, keepdims=True)
            alpha = e / jnp.where(denom == 0.0, 1.0, denom)
            out = jnp.einsum('hnm,mhc->hnc', alpha, v)
            out = jnp.transpose(out, (1, 2, 0)).reshape(n, C * H)
            x_r = x @ Ws + bs
            beta = jax.nn.sigmoid(jnp.concatenate([out, x_r, out - x_r], axis=-1) @ Wb)
            return beta * x_r + (1.0 - beta) * out
        key = jax.random.key(seed)
        ks = jax.random.split(key, 7)
        x = jax.random.normal(ks[0], (N, IN), jnp.float32)
        adj = (jax.random.uniform(ks[1], (N, N)) < EDGE_P).astype(jnp.float32)
        Wq, bq = _linear_params(ks[2], IN, HC)
        Wk, bk = _linear_params(ks[3], IN, HC)
        Wv, bv = _linear_params(ks[4], IN, HC)
        Ws, bs = _linear_params(ks[5], IN, HC)
        Wb = _linear_params(ks[6], 3 * HC, 1, bias=False)
        return dict(x=x, adj=adj, Wq=Wq, bq=bq, Wk=Wk, bk=bk, Wv=Wv, bv=bv, Ws=Ws, bs=bs, Wb=Wb)
    _L1_gnn_all = _L1_gnn_setup()
    _L1_gnn_in = {k: v for k, v in _L1_gnn_all.items() if k in ('Wq', 'bq', 'Wk', 'bk', 'Wv', 'bv', 'Ws', 'bs', 'Wb')}
    del _L1_gnn_all

    def _L2_gnn_setup():
        import jax, jax.numpy as jnp
        import numpy as np
        N = 8192
        U = 128
        AVG_DEGREE = 32
        key = jax.random.key(seed)
        kx, ka, kw = jax.random.split(key, 3)
        x = jax.random.normal(kx, (N, U), dtype=jnp.float32)
        adj = (jax.random.uniform(ka, (N, N)) < AVG_DEGREE / N).astype(jnp.float32)
        W = jax.random.normal(kw, (U, U), dtype=jnp.float32) * 0.05
        b = jnp.zeros((U,), dtype=jnp.float32)
        return {'x': x, 'adj': adj, 'W': W, 'b': b}
    _L2_gnn_all = _L2_gnn_setup()
    _L2_gnn_in = {k: v for k, v in _L2_gnn_all.items() if k in ('W', 'b')}
    del _L2_gnn_all

    def _L3_gnn_setup():
        import jax, jax.numpy as jnp
        import numpy as np
        IN_F, OUT_F = (128, 128)
        R, LEV, N = (2, 2, 4096)
        JD = (R - 1) * LEV + 1
        key = jax.random.key(seed)
        ks = jax.random.split(key, 7)
        x = jax.random.normal(ks[0], (N, IN_F), dtype=jnp.float32)
        d_list = jax.random.uniform(ks[1], (JD, N), dtype=jnp.float32)
        U = jax.random.normal(ks[2], (N, N), dtype=jnp.float32)
        Vt = jax.random.normal(ks[3], (N, N), dtype=jnp.float32)
        bound = float(np.sqrt(6.0 / (IN_F + OUT_F)))
        weight = jax.random.uniform(ks[4], (IN_F, OUT_F), dtype=jnp.float32, minval=-bound, maxval=bound)
        filt = jax.random.uniform(ks[5], (JD, N), dtype=jnp.float32, minval=0.9, maxval=1.1)
        bias = jnp.zeros((OUT_F,), dtype=jnp.float32)
        return {'x': x, 'd_list': d_list, 'U': U, 'Vt': Vt, 'weight': weight, 'filt': filt, 'bias': bias}
    _L3_gnn_all = _L3_gnn_setup()
    _L3_gnn_in = {k: v for k, v in _L3_gnn_all.items() if k in ('d_list', 'weight', 'filt', 'bias')}
    del _L3_gnn_all
    return {'x': x, 'adj': adj, 'L0_gnn_W1': _L0_gnn_in['W1'], 'L0_gnn_b1': _L0_gnn_in['b1'], 'L0_gnn_W2': _L0_gnn_in['W2'], 'L0_gnn_b2': _L0_gnn_in['b2'], 'L1_gnn_Wq': _L1_gnn_in['Wq'], 'L1_gnn_bq': _L1_gnn_in['bq'], 'L1_gnn_Wk': _L1_gnn_in['Wk'], 'L1_gnn_bk': _L1_gnn_in['bk'], 'L1_gnn_Wv': _L1_gnn_in['Wv'], 'L1_gnn_bv': _L1_gnn_in['bv'], 'L1_gnn_Ws': _L1_gnn_in['Ws'], 'L1_gnn_bs': _L1_gnn_in['bs'], 'L1_gnn_Wb': _L1_gnn_in['Wb'], 'L2_gnn_W': _L2_gnn_in['W'], 'L2_gnn_b': _L2_gnn_in['b'], 'L3_gnn_d_list': _L3_gnn_in['d_list'], 'L3_gnn_weight': _L3_gnn_in['weight'], 'L3_gnn_filt': _L3_gnn_in['filt'], 'L3_gnn_bias': _L3_gnn_in['bias']}

def reference(x, adj, L0_gnn_W1, L0_gnn_b1, L0_gnn_W2, L0_gnn_b2, L1_gnn_Wq, L1_gnn_bq, L1_gnn_Wk, L1_gnn_bk, L1_gnn_Wv, L1_gnn_bv, L1_gnn_Ws, L1_gnn_bs, L1_gnn_Wb, L2_gnn_W, L2_gnn_b, L3_gnn_d_list, L3_gnn_weight, L3_gnn_filt, L3_gnn_bias):
    import jax
    import jax.numpy as jnp

    def _L0_gnn_ref(x, A, W1, b1, W2, b2, sigma, k):
        import jax, jax.numpy as jnp
        import numpy as np

        def _lap_mul(A, x):
            d = 1.0 / jnp.sqrt(jnp.sum(A, axis=-1))
            return d[:, None] * (A @ (d[:, None] * x))
        z = _lap_mul(A, x) @ W1 + b1
        z = jax.nn.leaky_relu(z, negative_slope=0.1)
        sq = jnp.sum(z * z, axis=-1)
        d2 = sq[:, None] + sq[None, :] - 2.0 * (z @ z.T)
        d2 = jnp.maximum(d2, 0.0)
        S = jnp.sqrt(d2 + 1e-10)
        S = jnp.exp(-S / (2.0 * sigma))
        order = jnp.argsort(-S, axis=-1)
        ranks = jnp.argsort(order, axis=-1)
        S = jnp.where(ranks < k, S, 0.0)
        A2 = S + A
        out = _lap_mul(A2, x) @ W2 + b2
        return out

    def _L1_gnn_ref(x, adj, Wq, bq, Wk, bk, Wv, bv, Ws, bs, Wb):
        import jax, jax.numpy as jnp
        import numpy as np
        N, IN, H, C = (2048, 128, 4, 32)
        HC = H * C
        EDGE_P = 0.008

        def _linear_params(key, fan_in, fan_out, bias=True):
            k1, k2 = jax.random.split(key)
            lim = 1.0 / np.sqrt(fan_in)
            W = jax.random.uniform(k1, (fan_in, fan_out), jnp.float32, -lim, lim)
            if not bias:
                return W
            b = jax.random.uniform(k2, (fan_out,), jnp.float32, -lim, lim)
            return (W, b)

        def _transformer_conv(x, adj, Wq, bq, Wk, bk, Wv, bv, Ws, bs, Wb):
            n = x.shape[0]
            q = (x @ Wq + bq).reshape(n, H, C)
            k = (x @ Wk + bk).reshape(n, H, C)
            v = (x @ Wv + bv).reshape(n, H, C)
            attn = jnp.einsum('nhc,mhc->hnm', q, k) / np.float32(np.sqrt(C))
            mask = adj == 0.0
            neg = jnp.where(mask[None], -jnp.inf, attn)
            m = jnp.max(neg, axis=-1, keepdims=True)
            all_inf = jnp.isneginf(m)
            e = jnp.where(mask[None], 0.0, jnp.exp(neg - jnp.where(all_inf, 0.0, m)))
            denom = jnp.sum(e, axis=-1, keepdims=True)
            alpha = e / jnp.where(denom == 0.0, 1.0, denom)
            out = jnp.einsum('hnm,mhc->hnc', alpha, v)
            out = jnp.transpose(out, (1, 2, 0)).reshape(n, C * H)
            x_r = x @ Ws + bs
            beta = jax.nn.sigmoid(jnp.concatenate([out, x_r, out - x_r], axis=-1) @ Wb)
            return beta * x_r + (1.0 - beta) * out
        return _transformer_conv(x, adj, Wq, bq, Wk, bk, Wv, bv, Ws, bs, Wb)

    def _L2_gnn_ref(x, adj, W, b):
        import jax, jax.numpy as jnp
        import numpy as np
        N = 8192
        U = 128
        AVG_DEGREE = 32
        adj = jax.lax.stop_gradient(adj)
        neigh1 = adj @ x
        x1 = jax.nn.swish(neigh1 @ W + b)
        neigh2 = adj @ x1
        x2 = jax.nn.swish(neigh2 @ W + b)
        return x2

    def _L3_gnn_ref(x, d_list, U, Vt, weight, filt, bias):
        import jax, jax.numpy as jnp
        import numpy as np
        IN_F, OUT_F = (128, 128)
        R, LEV, N = (2, 2, 4096)
        JD = (R - 1) * LEV + 1
        xw = x @ weight
        Vxw = Vt @ xw
        scale = jnp.sum(d_list * filt * d_list, axis=0)
        out = U @ (scale[:, None] * Vxw)
        return out + bias
    x = _layernorm(x + _L0_gnn_ref(x, adj, L0_gnn_W1, L0_gnn_b1, L0_gnn_W2, L0_gnn_b2, 1, 4), axis=-1)
    x = _layernorm(x + _L1_gnn_ref(x, adj, L1_gnn_Wq, L1_gnn_bq, L1_gnn_Wk, L1_gnn_bk, L1_gnn_Wv, L1_gnn_bv, L1_gnn_Ws, L1_gnn_bs, L1_gnn_Wb), axis=-1)
    x = _layernorm(x + _L2_gnn_ref(x, adj, L2_gnn_W, L2_gnn_b), axis=-1)
    x = _layernorm(x + _L3_gnn_ref(x, L3_gnn_d_list, adj, adj, L3_gnn_weight, L3_gnn_filt, L3_gnn_bias), axis=-1)
    return x

_drawn_inputs = setup_inputs


def setup_inputs(seed=0):
    import zlib

    import numpy as np

    out = dict(_drawn_inputs(seed))
    spreads = {'L2_gnn_b': (0.0, 0.1), 'L3_gnn_bias': (0.0, 0.1)}
    factors = {'L1_gnn_bq': 8.0, 'L1_gnn_bk': 8.0}
    for name, (base, spread) in spreads.items():
        noise = np.random.default_rng([zlib.crc32(name.encode()), seed]).standard_normal(out[name].shape)
        drawn = base * np.exp(spread * noise) if base else spread * noise
        out[name] = jnp.asarray(drawn.astype(out[name].dtype))
    for name, factor in factors.items():
        out[name] = (out[name] * factor).astype(out[name].dtype)
    return out
```

```python
from contextlib import ExitStack

import concourse.bass as bass
from concourse import mybir
from concourse.alu_op_type import AluOpType as ALU

ds = bass.ds
N, F, P = 4096, 128, 128
NB = N // P
CH = 512
BPC = CH // P
NCH = N // CH
TQ = 4
TC = NB // TQ
K_NEAR = 4
HEADS, C = 4, 32
JD = 3
LN_EPS = 1e-5
MASKED = -1e30
ATT_SCALE = 1.0 / float(C) ** 0.5
GRP = 1024
NG = N // GRP
STEPS = NB // 2
ACT_STEPS = [0, 1, 2, 3, 4, 5, 6, 7, 14, 15]
DVE_STEPS = [t for t in range(STEPS) if t not in ACT_STEPS]

K_AGG1, K_AGG2, K_HOP1, K_HOP2, K_FRM1, K_FRM2 = range(6)


class Count:

    def __init__(self, eng, sem):
        self.eng, self.sem, self.base, self.turn, self.n = eng, sem, 0, None, 0

    def link(self, ins):
        self.n += 1
        ins.then_inc(self.sem, 1)
        self.eng.wait_ge(self.sem, self.value())

    def value(self):
        if self.turn is None:
            return self.base + self.n
        i, first, per_turn = self.turn
        return i * per_turn + (self.base + self.n - first * per_turn)

    def enter(self, i, first, per_turn):
        self.base, self.n, self.turn = self.base + self.n, 0, (i, first, per_turn)

    def leave(self, turns):
        _, _, per_turn = self.turn
        assert self.n == per_turn, (self.n, per_turn)
        self.base, self.n, self.turn = self.base + turns * per_turn, 0, None


def graph_layers_kernel(nc, x, adj, W1, b1, W2, b2, Wq, bq, Wk, bk, Wv, bv, Ws, bs, Wb, Wh, bh,
                        d_list, Wf, filt, bf, out):
    f32, bf16, f16, u32 = mybir.dt.float32, mybir.dt.bfloat16, mybir.dt.float16, mybir.dt.uint32
    ACT = mybir.ActivationFunctionType
    X_AX = mybir.AxisListType.X

    adjT = nc.dram_tensor("adjT_tiles", (NCH * TQ * P, TC * CH), f32).ap()
    gtab = nc.dram_tensor("scaled_x_rows", (N, F), f32).ap()

    ctx = ExitStack()
    with ctx:
        def sb(name, shape, dt=f32):
            return ctx.enter_context(nc.sbuf_tensor(name, shape, dt))

        def sem(name):
            return ctx.enter_context(nc.semaphore(name))

        xres = sb("xres", [P, NB * F])
        XA = sb("XA", [P, NB * F])
        tiles = sb("tiles", [P, 4, TC * CH])
        R2 = sb("R2", [P, 2 * N])
        adj_rows = sb("adj_rows", [P, N])
        maskb = sb("maskb", [P, 2, N], bf16)
        yT_sb = sb("yT_sb", [P, 2, CH])
        ident = sb("ident", [P, P])
        w_sb = sb("w_sb", [P, 8, F])
        wq4 = sb("wq4", [P, HEADS, 4, C])
        wk4 = sb("wk4", [P, HEADS, 4, C])
        bq4 = sb("bq4", [P, HEADS])
        bk4 = sb("bk4", [P, HEADS])
        bias_sb = sb("bias_sb", [P, 6, F])
        wb_sb = sb("wb_sb", [P, 3 * F])
        eps_ln = sb("eps_ln", [P, 1])
        zero1 = sb("zero1", [P, 1])
        neg_half = sb("neg_half", [P, JD])
        lo_q = sb("lo_q", [P, 1])
        lo_k = sb("lo_k", [P, 1])
        frm = adj_rows[0:NB, 0:2 * JD * P].rearrange("b (a i p) -> b a i p", a=2, i=JD)
        frm_t = adj_rows[0:NB, 2 * JD * P:3 * JD * P].rearrange("b (i p) -> b i p", i=JD)
        fscale = sb("fscale", [P, NB])
        rs_part = sb("rs_part", [P, TQ, NB])
        rowsum = sb("rowsum", [P, NB])
        deg = sb("deg", [P, NB])
        rdeg = sb("rdeg", [P, NB])
        zc = adj_rows[:, 0:2 * CH].rearrange("p (s n) -> p s n", s=2)
        zsq = adj_rows[:, 2 * CH:3 * CH]
        sqn = sb("sqn", [P, NB])
        sqz = adj_rows[:, 3 * CH:5 * CH].rearrange("p (s n) -> p s n", s=2)
        sq_h = sb("sq_h", [JD, CH], bf16)
        sq_m = sb("sq_m", [JD, CH], bf16)
        sq_r = adj_rows[0:JD, 5 * CH:6 * CH]
        sq_c = adj_rows[0:JD, 6 * CH:7 * CH]
        sq3 = maskb[0:JD, 0, :]
        ones3 = sb("ones3", [JD, P], bf16)
        zst = sb("zst", [P, 2, P])
        top8 = sb("top8", [P, 2, 8])
        idx8 = sb("idx8", [P, 2, 8], u32)
        near_key = sb("near_key", [P, NB * K_NEAR])
        near_idx = sb("near_idx", [P, NB * K_NEAR], u32)
        near_s = sb("near_s", [P, NB * K_NEAR])
        near_t = sb("near_t", [P, NB * K_NEAR])
        rdeg2 = sb("rdeg2", [P, NB])
        idx_st = sb("idx_st", [P, 2, K_NEAR], u32)
        gat = adj_rows[:, 0:2 * K_NEAR * F].rearrange("p (s n f) -> p s n f", s=2, n=K_NEAR)
        near_u = adj_rows[:, 2 * CH:4 * CH].rearrange("p (b f) -> p b f", f=F)
        e_tx = sb("e_tx", [P, 2 * CH])
        e_t, e_exp = e_tx[:, 0:CH], e_tx[:, CH:2 * CH]
        e_cq = sb("e_cq", [P, 2 * CH])
        e_c, e_q = e_cq[:, 0:CH], e_cq[:, CH:2 * CH]
        e_sum = sb("e_sum", [P, BPC])
        e_var = sb("e_var", [P, BPC])
        e_std = sb("e_std", [P, BPC])
        oc = sb("oc", [P, 2, CH])
        xst = sb("xst", [P, 2, F])
        xTst = sb("xTst", [P, 2, P])
        q_full = sb("q_full", [P, 2, P])
        q_hi = sb("q_hi", [P, 2, P], f16)
        qst = sb("qst", [P, 2, HEADS, P], f16)
        pts = e_cq[:, :].rearrange("p (s n) -> p s n", s=2)
        mx_part = sb("mx_part", [P, 2, NG])
        mx4 = sb("mx4", [P, 2, HEADS])
        nbias = sb("nbias", [P, HEADS])
        den = sb("den", [P, 2, HEADS, NG])
        den4 = sb("den4", [P, HEADS])
        rden4 = sb("rden4", [P, HEADS])
        oTs = sb("oTs", [P, 2, P])
        cat = e_tx[:, 0:6 * F].rearrange("p (s n) -> p s n", s=2)
        cat_t = oc[:, 0, 0:3 * F]
        gate_z = sb("gate_z", [P, 1])
        gate_e = sb("gate_e", [P, 1])
        gate_b = sb("gate_b", [P, 1])
        att = sb("att", [P, F])
        xr_new = oc[:, 1, 0:F]
        st6 = sb("st6", [P, 6])
        mv = sb("mv", [P, 2])
        a_std = sb("a_std", [P, 1])
        a_rstd = sb("a_rstd", [P, 1])

        PS = ctx.enter_context(nc.psum_tensor("PS", [P, 8 * CH], f32))

        def bank(b):
            return PS[:, b * CH:(b + 1) * CH]

        zT = R2[:, 0:N]
        kst = R2[:, :].bitcast(f16).rearrange("p (h n) -> p h n", h=HEADS)
        key_rows = [tiles[:, 2, :], tiles[:, 3, :]]
        att_w = [[tiles[:, 2 * pr + hh, :] for hh in range(2)] for pr in range(2)]
        V = XA
        W_1, W_2, W_H, W_F, W_Q, W_K, W_V, W_S = (w_sb[:, i, :] for i in range(8))
        B_1, B_2, B_H, B_F, B_V, B_S = (bias_sb[:, i, :] for i in range(6))
        weight_of = [W_1, W_2, W_H, W_H, W_F, ident[:, :]]
        operand_of = [XA, XA, xres, XA, xres, XA]

        def by_block(ap):
            return ap.rearrange("p (b f) -> p b f", f=F)

        def over_blocks(vec):
            return vec.unsqueeze(1).to_broadcast([P, BPC, F])

        def over_features(vec, n=BPC, f=F):
            return vec.unsqueeze(2).to_broadcast([P, n, f])

        consts_in = sem("consts_in")
        made = sem("made")
        fs_summed = sem("fs_summed")
        fs_turned = sem("fs_turned")
        rows_in = [sem(f"rows_in{i}") for i in range(2)]
        bank_turned = sem("bank_turned")
        bank_copied = sem("bank_copied")
        rows_summed = sem("rows_summed")
        adjT_out = [sem(f"adjT_out{i}") for i in range(2)]
        deg_ready = sem("deg_ready")
        deg_root = sem("deg_root")
        x_ready = [sem(f"x_ready{k}") for k in range(6)]
        tile_in = [sem(f"tile_in{q}") for q in range(TQ)]
        tile_used = [sem(f"tile_used{q}") for q in range(TQ)]
        y_ready = sem("y_ready")
        y_copied = sem("y_copied")
        e_ready = sem("e_ready")
        e_taken = sem("e_taken")
        z_ready = sem("z_ready")
        zT_turned = sem("zT_turned")
        zT_ready = sem("zT_ready")
        sq_ready = sem("sq_ready")
        sq_split = sem("sq_split")
        zst_ready = sem("zst_ready")
        keys_ready = sem("keys_ready")
        keys_copied = sem("keys_copied")
        near_found = sem("near_found")
        d_near = sem("d_near")
        s_near = sem("s_near")
        deg2_ready = sem("deg2_ready")
        deg2_root = sem("deg2_root")
        table_out = sem("table_out")
        idx_staged = sem("idx_staged")
        rows_gathered = [sem(f"rows_gathered{i}") for i in range(2)]
        u_ready = sem("u_ready")
        var_ready = sem("var_ready")
        std_ready = sem("std_ready")
        swish_in = sem("swish_in")
        swish_exp = sem("swish_exp")
        out_ready = sem("out_ready")
        out_stored = [sem(f"out_stored{i}") for i in range(2)]
        kx_staged = sem("kx_staged")
        kx_turned = sem("kx_turned")
        kx_copied = sem("kx_copied")
        v_ready = sem("v_ready")
        v_taken = sem("v_taken")
        k_ready = sem("k_ready")
        k_halved = sem("k_halved")
        k_stacked = sem("k_stacked")
        mask_rows_in = sem("mask_rows_in")
        mask_ready = sem("mask_ready")
        xst_ready = sem("xst_ready")
        xT_turned = sem("xT_turned")
        xT_copied = sem("xT_copied")
        xr_ready = sem("xr_ready")
        xr_taken = sem("xr_taken")
        q_ready = sem("q_ready")
        q_halved = sem("q_halved")
        q_stacked = sem("q_stacked")
        s_ready = sem("s_ready")
        s_taken = sem("s_taken")
        max_ready = sem("max_ready")
        exp_done = sem("exp_done")
        pt_ready = sem("pt_ready")
        pt_by_act = sem("pt_by_act")
        pt_by_dve = sem("pt_by_dve")
        o_ready = sem("o_ready")
        o_copied = sem("o_copied")
        o_turned = sem("o_turned")
        gate_in = sem("gate_in")
        gate_exp = sem("gate_exp")
        avar_ready = sem("avar_ready")
        astd_ready = sem("astd_ready")
        att_done = sem("att_done")
        passed = sem("passed")
        act_link = sem("act_link")
        dve_link = sem("dve_link")

        N_CONSTS = 0
        consts = []

        consts.append((by_block(xres[:, :]), x.rearrange("(b p) f -> p b f", p=P)))
        for i, w in enumerate((W1, W2, Wh, Wf, Wq, Wk, Wv, Ws)):
            consts.append((w_sb[:, i, :], w))
        for i, b in enumerate((b1, b2, bh, bf, bv, bs)):
            consts.append((bias_sb[:, i, :], b.rearrange("(a n) -> a n", a=1).to_broadcast([P, F])))
        consts.append((wb_sb[:, :], Wb.rearrange("n a -> a n").to_broadcast([P, 3 * F])))
        for r in range(4):
            consts.append((bq4[C * r:C * (r + 1), :], bq.rearrange("(h c) -> c h", c=C)))
            consts.append((bk4[C * r:C * (r + 1), :], bk.rearrange("(h c) -> c h", c=C)))
        consts.append((frm[:, 0, :, :], d_list.rearrange("i (b p) -> b i p", p=P)))
        consts.append((frm[:, 1, :, :], filt.rearrange("i (b p) -> b i p", p=P)))
        N_CONSTS = 16 * len(consts)

        N_MADE = 14

        def apart(eng):
            eng.sem_inc(passed, 1)

        block = ctx.enter_context(nc.Block())

        @block.sync
        def _(sp):
            with nc.allow_non_contiguous_dma(reason="biases by partition, once"):
                for dst, src in consts:
                    sp.dma_start(dst, src).then_inc(consts_in, 16)

            def load_rows(j, q):
                src = adj[ds(j * CH, CH), q * TC * P:(q + 1) * TC * P]
                sp.dma_start(tiles[:, q % 2, :].rearrange("p (b m) -> p b m", b=BPC),
                             src.rearrange("(b p) m -> p b m", p=P)).then_inc(rows_in[q % 2], 16)

            for q in range(TQ):
                if q >= 2:
                    sp.wait_ge(bank_turned, (q - 1) * TC)
                    sp.wait_ge(rows_summed, q - 1)
                load_rows(0, q)
            with sp.Fori(1, NCH) as j:
                for q in range(TQ):
                    sp.wait_ge(bank_turned, j * (TQ * TC) + (q - 1) * TC)
                    apart(sp)
                    sp.wait_ge(rows_summed, j * TQ + (q - 1))
                    apart(sp)
                    load_rows(j, q)

            def load_tile(j, q):
                sp.dma_start(tiles[:, q, :], adjT[ds((j * TQ + q) * P, P), :]).then_inc(tile_in[q], 16)

            def load_product(k):
                lo = 0
                if k in (K_AGG1, K_AGG2, K_HOP1):
                    for q in range(TQ):
                        if k > 0:
                            sp.wait_ge(tile_used[q], NCH * k)
                        load_tile(0, q)
                    lo = 1
                with sp.Fori(lo, NCH) as j:
                    for q in range(TQ):
                        sp.wait_ge(tile_used[q], j + NCH * k)
                        apart(sp)
                        load_tile(j, q)

            for i in range(2):
                sp.wait_ge(adjT_out[i], 16 * NCH * TQ // 2)
            sp.wait_ge(bank_turned, NCH * TQ * TC)
            sp.wait_ge(rows_summed, NCH * TQ)
            load_product(K_AGG1)
            sp.wait_ge(near_found, NB)
            load_product(K_AGG2)

            def load_mask_rows(b):
                sp.dma_start(adj_rows[:, :], adj[ds(b * P, P), :]).then_inc(mask_rows_in, 16)

            sp.wait_ge(att_done, 1)
            load_mask_rows(0)
            with sp.Fori(1, NB) as b:
                sp.wait_ge(mask_ready, b)
                apart(sp)
                load_mask_rows(b)
            sp.wait_ge(pt_ready, 2 * NB * STEPS)
            for k in (K_HOP1, K_HOP2, K_FRM1, K_FRM2):
                load_product(k)
            for s in range(2):
                sp.wait_ge(out_stored[s], 16 * NCH // 2)

        @block.gpsimd
        def _(pool):
            pool.memset(ident[:, :], 0.0).then_inc(made, 1)
            pool.wait_ge(made, 1)
            pool.affine_select(out=ident[:, :], in_=ident[:, :], compare_op=ALU.not_equal, fill=1.0,
                               base=0, pattern=[[-1, P]], channel_multiplier=1).then_inc(made, 1)
            fills = [(eps_ln, LN_EPS), (zero1, 0.0), (neg_half, -0.5), (ones3, 1.0)]
            fills += [(lo_q[C * r:C * (r + 1)], -1.0 if r >= 2 else 0.0) for r in range(4)]
            fills += [(lo_k[C * r:C * (r + 1)], -1.0 if r % 2 else 0.0) for r in range(4)]
            for n, (t, value) in enumerate(fills):
                pool.wait_ge(made, n + 2)
                pool.memset(t[:, :], value).then_inc(made, 1)

            pool.wait_ge(zT_ready, NCH)

            def stage_z(b, s):
                pool.tensor_copy(zst[:, s, :], zT[:, ds(b * P, P)]).then_inc(zst_ready, 1)

            stage_z(0, 0)
            stage_z(1, 1)
            with pool.Fori(1, NB // 2) as i:
                for s in range(2):
                    pool.wait_ge(keys_ready, i * (2 * NG) + (s - 1) * NG)
                    stage_z(i * 2 + s, s)

            pool.wait_ge(table_out, 16)

            def gather(b, s):
                pool.tensor_copy(idx_st[:, s, :], near_idx[:, ds(b * K_NEAR, K_NEAR)])\
                    .then_inc(idx_staged, 1)
                pool.wait_ge(idx_staged, b + 1)
                apart(pool)
                for n in range(K_NEAR):
                    pool.indirect_dma_start(
                        out=gat[:, s, n, :], out_offset=None, in_=gtab[:, :],
                        in_offset=bass.IndirectOffsetOnAxis(ap=idx_st[:, s, n:n + 1], axis=0),
                    ).then_inc(rows_gathered[s], 16)

            gather(0, 0)
            gather(1, 1)
            with pool.Fori(1, NB // 2) as i:
                for s in range(2):
                    b = i * 2 + s
                    pool.wait_ge(u_ready, b - 1)
                    pool.wait_ge(rows_gathered[s], i * (16 * K_NEAR))
                    gather(b, s)

            pool.wait_ge(k_stacked, NCH * HEADS)

            def stage_x(b, s):
                pool.tensor_copy(xst[:, s, :], xres[:, ds(b * F, F)]).then_inc(xst_ready, 1)

            stage_x(0, 0)
            stage_x(1, 1)
            with pool.Fori(1, NB // 2) as i:
                for s in range(2):
                    pool.wait_ge(xT_turned, i * 2 + (s - 1))
                    stage_x(i * 2 + s, s)

        @block.tensor
        def _(pe):
            pe.wait_ge(made, N_MADE)
            pe.wait_ge(fs_summed, 1)
            pe.transpose(PS[:, 0:NB], frm_t[:, 0, :], ident[0:NB, 0:NB]).then_inc(fs_turned, 1)
            pe.wait_ge(deg_ready, 1)

            def turn_tile(j, q, first):
                pe.wait_ge(rows_in[q % 2], j * 32 + 16 * (q // 2 + 1))
                for c in range(TC):
                    if not first:
                        pe.wait_ge(bank_copied, j * (TQ * TC) + ((q - 1) * TC + c + 1))
                    for b in range(BPC):
                        src = tiles[:, q % 2, (b * TC + c) * P:(b * TC + c + 1) * P]
                        ins = pe.transpose(PS[:, c * CH + b * P:c * CH + (b + 1) * P], src, ident[:, :])
                    ins.then_inc(bank_turned, 1)

            def turn_chunk(j, first):
                for q in range(TQ):
                    turn_tile(j, q, first and q == 0)

            turn_chunk(0, True)
            with pe.Fori(1, NCH) as j:
                turn_chunk(j, False)
            pe.wait_ge(bank_copied, NCH * TQ * TC)

            def product(k):
                X = operand_of[k]
                first_c = NCH * k

                def quarter(j, s, q, head):
                    if head:
                        pe.wait_ge(x_ready[k], 2 * q + 2)
                    pe.wait_ge(tile_in[q], j * 16 + 16 * (first_c + 1))
                    for c in range(TC):
                        m = q * TC + c
                        ins = pe.matmul(bank(s), X[:, m * F:(m + 1) * F],
                                        tiles[:, q, c * CH:(c + 1) * CH], start=(m == 0),
                                        stop=(m == NB - 1 and k != K_AGG2), skip_group_check=True)
                    ins.then_inc(tile_used[q], 1)

                def weigh(j, s, fresh=False):
                    if not fresh:
                        pe.wait_ge(e_taken, j + first_c)
                    pe.wait_ge(y_copied, j + (first_c + 1))
                    for b in range(BPC):
                        ins = pe.matmul(bank(2 + s)[:, b * P:(b + 1) * P], yT_sb[:, s, b * P:(b + 1) * P],
                                        weight_of[k], start=True, stop=True)
                    ins.then_inc(e_ready, 1)

                def turn_z(j, s):
                    pe.wait_ge(z_ready, j + 1)
                    for b in range(BPC):
                        ins = pe.transpose(bank(4 + s)[:, b * P:(b + 1) * P],
                                           zc[:, s, b * P:(b + 1) * P], ident[:, :])
                    ins.then_inc(zT_turned, 1)

                def sum_z(j, s):
                    pe.wait_ge(zT_ready, j + 1)
                    pe.matmul(PS[0:JD, 6 * CH:7 * CH], neg_half[:, :], sqz[:, s, :], start=True,
                              stop=True).then_inc(sq_ready, 1)

                def add_near(j, s):
                    pe.wait_ge(u_ready, j * BPC + BPC)
                    for b in range(BPC):
                        ins = pe.matmul(bank(s)[:, b * P:(b + 1) * P], near_u[:, s * BPC + b, :],
                                        ident[:, :], start=False, stop=(b == BPC - 1),
                                        skip_group_check=True)
                    ins.then_inc(y_ready, 1)

                def chunk(j, s, head, after, head_next=False):
                    for q in range(TQ):
                        quarter(j, s, q, head)
                        if after and q == 0:
                            weigh(j - 1, 1 - s, k == K_AGG1 and head_next)
                        if after and q == 2 and k == K_AGG1:
                            turn_z(j - 1, 1 - s)
                    if k == K_AGG2:
                        add_near(j, s)
                    if k == K_AGG1 and after:
                        sum_z(j - 1, 1 - s)

                chunk(0, 0, True, False)
                chunk(1, 1, False, True, True)
                with pe.Fori(1, NCH // 2) as i:
                    chunk(i * 2, 0, False, True, False)
                    chunk(i * 2 + 1, 1, False, True)
                weigh(NCH - 1, 1)
                if k == K_AGG1:
                    turn_z(NCH - 1, 1)
                    sum_z(NCH - 1, 1)

            product(K_AGG1)

            pe.wait_ge(sq_split, NCH)
            pe.wait_ge(e_taken, NCH)

            def keys(b, s, first):
                pe.wait_ge(zst_ready, b + 1)
                for g in range(NG):
                    if not first:
                        pe.wait_ge(keys_copied, b * NG + (g + 1 - NG))
                    for h in range(GRP // CH):
                        o = g * GRP + h * CH
                        pe.matmul(PS[:, o:o + CH], zst[:, s, :], zT[:, o:o + CH], start=True, stop=False)
                        ins = pe.matmul(PS[:, o:o + CH], ones3[:, :], sq3[:, o:o + CH], start=False,
                                        stop=True)
                    ins.then_inc(keys_ready, 1)

            keys(0, 0, True)
            keys(1, 1, False)
            with pe.Fori(1, NB // 2) as i:
                keys(i * 2, 0, False)
                keys(i * 2 + 1, 1, False)
            pe.wait_ge(keys_copied, NB * NG)

            product(K_AGG2)

            def kv_chunk(j, s, first):
                pe.wait_ge(kx_staged, j + 1)
                for b in range(BPC):
                    ins = pe.transpose(bank(4 + s)[:, b * P:(b + 1) * P], oc[:, s, b * P:(b + 1) * P],
                                       ident[:, :])
                ins.then_inc(kx_turned, 1)
                pe.wait_ge(kx_copied, j + 1)
                if not first:
                    pe.wait_ge(v_taken, j - 1)
                for b in range(BPC):
                    ins = pe.matmul(bank(6 + s)[:, b * P:(b + 1) * P], yT_sb[:, s, b * P:(b + 1) * P],
                                    W_V, start=True, stop=True)
                ins.then_inc(v_ready, 1)
                for h in range(HEADS):
                    if not (first and s == 0):
                        pe.wait_ge(k_halved, j * HEADS + (h + 1 - HEADS))
                    pe.matmul(bank(h), wk4[:, h, :, :].rearrange("p r c -> p (r c)"), yT_sb[:, s, :],
                              start=True, stop=True).then_inc(k_ready, 1)

            pe.wait_ge(att_done, 1)
            kv_chunk(0, 0, True)
            kv_chunk(1, 1, True)
            with pe.Fori(1, NCH // 2) as i:
                kv_chunk(i * 2, 0, False)
                kv_chunk(i * 2 + 1, 1, False)
            pe.wait_ge(k_stacked, NCH * HEADS)
            pe.wait_ge(v_taken, NCH)

            OUT = 6 * CH
            MISC = 7 * CH

            def turn_x(b, s, prev):
                pe.wait_ge(xst_ready, b + 1)
                if prev:
                    pe.wait_ge(gate_in, b - 2)
                pe.transpose(PS[:, MISC:MISC + P], xst[:, s, :], ident[:, :]).then_inc(xT_turned, 1)

            def queries(b, s, pr):
                if pr == 0:
                    pe.wait_ge(xT_copied, b + 1)
                    pe.matmul(PS[:, MISC:MISC + F], xTst[:, s, :], W_S, start=True,
                              stop=True).then_inc(xr_ready, 1)
                else:
                    pe.wait_ge(xr_taken, b + 1)
                for hh in range(2):
                    o = MISC + P + hh * P
                    ins = pe.matmul(PS[:, o:o + P], wq4[:, 2 * pr + hh, :, :].rearrange("p r c -> p (r c)"),
                                    xTst[:, s, :], start=True, stop=True)
                ins.then_inc(q_ready, 1)

            def scores(u, s, pr, i, first):
                if i == 0:
                    pe.wait_ge(q_stacked, u + 1)
                if not (first and i < 2):
                    pe.wait_ge(s_taken, u * 8 + (i - 1))
                for h in range(GRP // CH):
                    o = (i % NG) * GRP + h * CH
                    p_o = (i % 2) * GRP + h * CH
                    ins = pe.matmul(PS[:, p_o:p_o + CH], qst[:, s, 2 * pr + i // NG, :],
                                    kst[:, 2 * pr + i // NG, o:o + CH], start=True, stop=True)
                ins.then_inc(s_ready, 1)

            def turn_weights(u, pr, t):
                if t % 4 == 0:
                    pe.wait_ge(exp_done, u * 8 + (NG + t // 4 + 1))
                for m in range(2):
                    for hh in range(2):
                        col = (2 * t + m) * P
                        o = (4 + t % 2) * CH + (m * 2 + hh) * P
                        ins = pe.transpose(PS[:, o:o + P], att_w[pr][hh][:, col:col + P], ident[:, :])
                ins.then_inc(pt_ready, 1)

            def weigh_values(b, u, s, pr, t, prev):
                if t in ACT_STEPS:
                    pe.wait_ge(pt_by_act, u * len(ACT_STEPS) + (ACT_STEPS.index(t) + 1))
                else:
                    pe.wait_ge(pt_by_dve, u * len(DVE_STEPS) + (DVE_STEPS.index(t) + 1))
                if t == 0 and pr == 0 and prev:
                    pe.wait_ge(o_copied, b)
                for m in range(2):
                    for hh in range(2):
                        h, blk = 2 * pr + hh, 2 * t + m
                        ins = pe.matmul(PS[C * h:C * (h + 1), OUT:OUT + P],
                                        V[:, blk * F + C * h:blk * F + C * (h + 1)],
                                        pts[:, t % 2, (m * 2 + hh) * P:(m * 2 + hh + 1) * P],
                                        start=(blk == 0), stop=(blk == NB - 1), skip_group_check=True)
                if t == STEPS - 1 and pr == 1:
                    ins.then_inc(o_ready, 1)

            def turn_out(b, s, asked):
                pe.wait_ge(o_copied, b + 1)
                if asked:
                    pe.wait_ge(q_halved, b * 2 + 6)
                pe.transpose(PS[:, MISC + 3 * P:MISC + 4 * P], oTs[:, s, :], ident[:, :])\
                    .then_inc(o_turned, 1)

            def phase(b, s, pr, prev, prevprev, nxt):
                u = b * 2 + pr
                for t in range(STEPS):
                    turn_weights(u, pr, t)
                    if t > 0:
                        weigh_values(b, u, s, pr, t - 1, prev)
                    if t < 8 and (pr == 0 or nxt):
                        scores(u + 1, s if pr == 0 else 1 - s, 1 - pr, t, False)
                    if pr == 0 and nxt:
                        if t == 0:
                            turn_x(b + 1, 1 - s, prevprev)
                        if t == 2:
                            queries(b + 1, 1 - s, 0)
                        if t == 5:
                            queries(b + 1, 1 - s, 1)
                    if pr == 0 and prev and t == 8:
                        turn_out(b - 1, 1 - s, nxt)
                weigh_values(b, u, s, pr, STEPS - 1, prev)

            turn_x(0, 0, False)
            queries(0, 0, 0)
            queries(0, 0, 1)
            for i in range(8):
                scores(0, 0, 0, i, True)
            for s in range(2):
                for pr in range(2):
                    phase(s, s, pr, s > 0, False, True)
            with pe.Fori(1, NB // 2 - 1) as i:
                for s in range(2):
                    for pr in range(2):
                        phase(i * 2 + s, s, pr, True, True, True)
            for s in range(2):
                for pr in range(2):
                    phase(NB - 2 + s, s, pr, True, True, s == 0)
            turn_out(NB - 1, 1, False)
            pe.wait_ge(att_done, NB + 1)

            for k in (K_HOP1, K_HOP2, K_FRM1, K_FRM2):
                product(k)

        @block.scalar
        def _(act):
            chain = Count(act, act_link)
            act.wait_ge(made, N_MADE)

            def copy_tile(j, q, first):
                if not first:
                    act.wait_ge(adjT_out[q % 2], j * 32 + 16 * (q // 2))
                for c in range(TC):
                    act.wait_ge(bank_turned, j * (TQ * TC) + (q * TC + c + 1))
                    act.activation(tiles[:, 2 + q % 2, c * CH:(c + 1) * CH], bank(c), ACT.Copy)\
                        .then_inc(bank_copied, 1)
                act.wait_ge(bank_copied, j * (TQ * TC) + (q + 1) * TC)
                act.dma_start(adjT[ds((j * TQ + q) * P, P), :], tiles[:, 2 + q % 2, :])\
                    .then_inc(adjT_out[q % 2], 16)

            for q in range(TQ):
                copy_tile(0, q, q < 2)
            with act.Fori(1, NCH) as j:
                for q in range(TQ):
                    copy_tile(j, q, False)

            act.wait_ge(deg_ready, 2)
            act.activation(deg[:, :], rowsum[:, :], ACT.Sqrt, bias=zero1[:, :]).then_inc(deg_root, 1)

            def product(k):
                first_c = NCH * k

                def chunk(j, s, n_ln, n_sw):
                    if k == K_AGG2:
                        act.wait_ge(y_ready, j + 1)
                    else:
                        act.wait_ge(tile_used[TQ - 1], j + (first_c + 1))
                    act.activation(yT_sb[:, s, :], bank(s), ACT.Copy).then_inc(y_copied, 1)
                    if k == K_AGG1:
                        act.wait_ge(zT_turned, j + 1)
                        act.activation(zT[:, ds(j * CH, CH)], bank(4 + s), ACT.Copy).then_inc(act_link, 1)
                        act.activation(sqz[:, s, :], bank(4 + s), ACT.Square, bias=zero1[:, :])\
                            .then_inc(act_link, 1)
                        act.wait_ge(act_link, j * 2 + 2)
                        act.sem_inc(zT_ready, 1)
                    if k in (K_HOP1, K_HOP2):
                        act.wait_ge(swish_in, j + (n_sw + 1))
                        act.activation(e_exp[:, :], e_t[:, :], ACT.Exp, scale=-1.0, bias=zero1[:, :])\
                            .then_inc(swish_exp, 1)
                    if k in (K_AGG2, K_HOP2, K_FRM2):
                        act.wait_ge(var_ready, j + (n_ln + 1))
                        act.activation(e_std[:, :], e_var[:, :], ACT.Sqrt, scale=1.0 / F,
                                       bias=eps_ln[:, :]).then_inc(std_ready, 1)
                    if k == K_FRM2:
                        act.wait_ge(out_ready, j + 1)
                        act.dma_start(out[ds(j * CH, CH), :].rearrange("(b p) f -> p b f", p=P),
                                      by_block(oc[:, s, :])).then_inc(out_stored[s], 16)

                n_ln = {K_AGG2: 0, K_HOP2: NCH, K_FRM2: 2 * NCH}.get(k)
                n_sw = {K_HOP1: 0, K_HOP2: NCH}.get(k)
                with act.Fori(0, NCH // 2) as i:
                    for s in range(2):
                        chunk(i * 2 + s, s, n_ln, n_sw)

            product(K_AGG1)

            def keys(b, s, first):
                if not first:
                    act.wait_ge(near_found, b - 1)
                for g in range(NG):
                    act.wait_ge(keys_ready, b * NG + (g + 1))
                    act.activation(key_rows[s][:, g * GRP:(g + 1) * GRP], PS[:, g * GRP:(g + 1) * GRP],
                                   ACT.Copy).then_inc(keys_copied, 1)

            act.wait_ge(tile_used[2], NCH)
            act.wait_ge(y_copied, NCH)
            keys(0, 0, True)
            keys(1, 1, True)
            with act.Fori(1, NB // 2) as i:
                keys(i * 2, 0, False)
                keys(i * 2 + 1, 1, False)

            act.wait_ge(d_near, 1)
            act.activation(near_t[:, :], near_s[:, :], ACT.Sqrt, bias=zero1[:, :]).then_inc(s_near, 1)
            act.wait_ge(s_near, 1)
            act.activation(near_s[:, :], near_t[:, :], ACT.Exp, scale=-0.5, bias=zero1[:, :])\
                .then_inc(s_near, 1)
            act.wait_ge(deg2_ready, 1)
            act.activation(deg[:, :], rdeg2[:, :], ACT.Sqrt, bias=zero1[:, :]).then_inc(deg2_root, 1)
            act.wait_ge(x_ready[K_AGG2], NCH)
            act.dma_start(gtab.rearrange("(b p) f -> p b f", p=P), by_block(XA[:, :]))\
                .then_inc(table_out, 16)

            product(K_AGG2)

            def kv_chunk(j, s, first):
                act.wait_ge(kx_turned, j + 1)
                if not first:
                    act.wait_ge(k_ready, j * HEADS - HEADS)
                act.activation(yT_sb[:, s, :], bank(4 + s), ACT.Copy).then_inc(kx_copied, 1)
                for h in range(HEADS):
                    r = h % 2
                    act.wait_ge(k_ready, j * HEADS + (h + 1))
                    if not (first and s == 0 and h < 2):
                        act.wait_ge(k_stacked, j * HEADS + (h - 1))
                    act.activation(pts[:, r, :], bank(h), ACT.Identity, bias=bk4[:, h:h + 1])\
                        .then_inc(act_link, 1)
                    act.activation(khi[:, r, :], bank(h), ACT.Identity, bias=bk4[:, h:h + 1])\
                        .then_inc(k_halved, 1)

            khi = maskb[:, 0, 0:2 * CH].bitcast(f16).rearrange("p (r n) -> p r n", r=2)
            kv_chunk(0, 0, True)
            kv_chunk(1, 1, True)
            with act.Fori(1, NCH // 2) as i:
                kv_chunk(i * 2, 0, False)
                kv_chunk(i * 2 + 1, 1, False)

            def copy_xT(b, s):
                act.wait_ge(xT_turned, b + 1)
                act.activation(xTst[:, s, :], PS[:, 7 * CH:7 * CH + P], ACT.Copy).then_inc(xT_copied, 1)

            def halve_queries(b, s, pr, first):
                act.wait_ge(q_ready, b * 2 + (pr + 1))
                if not (first and pr == 0):
                    act.wait_ge(q_stacked, b * 2 + pr)
                for hh in range(2):
                    h = 2 * pr + hh
                    src = PS[:, 7 * CH + P + hh * P:7 * CH + P + (hh + 1) * P]
                    act.activation(q_full[:, hh, :], src, ACT.Identity, bias=bq4[:, h:h + 1])\
                        .then_inc(act_link, 1)
                    ins = act.activation(q_hi[:, hh, :], src, ACT.Identity, bias=bq4[:, h:h + 1])
                ins.then_inc(q_halved, 1)

            def exponentials(u, s, pr, i):
                hh, g = i // NG, i % NG
                h = 2 * pr + hh
                if g == 0:
                    act.wait_ge(max_ready, u * 2 + (hh + 1))
                w = att_w[pr][hh][:, g * GRP:(g + 1) * GRP]
                act.activation(w, w, ACT.Exp, bias=nbias[:, h:h + 1], scale=ATT_SCALE,
                               accum_out=den[:, s, h, g:g + 1]).then_inc(exp_done, 1)

            def copy_turned(u, t):
                act.wait_ge(pt_ready, u * STEPS + (t + 1))
                act.activation(pts[:, t % 2, :], bank(4 + t % 2), ACT.Copy).then_inc(pt_by_act, 1)

            def copy_out(b, s):
                act.wait_ge(o_ready, b + 1)
                act.activation(oTs[:, s, :], PS[:, 6 * CH:6 * CH + P], ACT.Copy)\
                    .then_inc(o_copied, 1)

            def gate(b):
                act.wait_ge(gate_in, b + 1)
                act.activation(gate_e[:, :], gate_z[:, :], ACT.Exp, scale=-1.0, bias=zero1[:, :])\
                    .then_inc(gate_exp, 1)

            def root(b):
                act.wait_ge(avar_ready, b + 1)
                act.activation(a_std[:, :], mv[:, 1:2], ACT.Sqrt, bias=eps_ln[:, :]).then_inc(astd_ready, 1)

            def phase(b, s, pr, prev, prevprev, nxt):
                u = b * 2 + pr
                ns, npr = (s, 1) if pr == 0 else (1 - s, 0)
                ahead = pr == 0 or nxt
                for t in range(STEPS):
                    if t in ACT_STEPS:
                        copy_turned(u, t)
                    if pr == 0:
                        if t == 0 and prev:
                            copy_out(b - 1, 1 - s)
                        if t == 1 and nxt:
                            copy_xT(b + 1, 1 - s)
                        if t == 3 and nxt:
                            halve_queries(b + 1, 1 - s, 0, False)
                        if t == 5 and nxt:
                            halve_queries(b + 1, 1 - s, 1, False)
                    elif prev:
                        if t == 3:
                            gate(b - 1)
                        if t == 7:
                            root(b - 1)
                    if ahead and 5 <= t <= 12:
                        exponentials(u + 1, ns, npr, t - 5)

            copy_xT(0, 0)
            halve_queries(0, 0, 0, True)
            halve_queries(0, 0, 1, True)
            for i in range(8):
                exponentials(0, 0, 0, i)
            for s in range(2):
                for pr in range(2):
                    phase(s, s, pr, s > 0, False, True)
            with act.Fori(1, NB // 2 - 1) as i:
                for s in range(2):
                    for pr in range(2):
                        phase(i * 2 + s, s, pr, True, True, True)
            for s in range(2):
                for pr in range(2):
                    phase(NB - 2 + s, s, pr, True, True, s == 0)
            copy_out(NB - 1, 1)
            gate(NB - 1)
            root(NB - 1)

            for k in (K_HOP1, K_HOP2, K_FRM1, K_FRM2):
                product(k)

        @block.vector
        def _(dve):
            chain = Count(dve, dve_link)
            link = chain.link

            dve.wait_ge(consts_in, N_CONSTS)
            dve.wait_ge(made, N_MADE)
            link(dve.tensor_tensor(frm_t[:, :, :], frm[:, 0, :, :], frm[:, 1, :, :], ALU.mult))
            link(dve.tensor_tensor(frm_t[:, :, :], frm_t[:, :, :], frm[:, 0, :, :], ALU.mult))
            link(dve.tensor_tensor(frm_t[:, 0, :], frm_t[:, 0, :], frm_t[:, 1, :], ALU.add))
            dve.tensor_tensor(frm_t[:, 0, :], frm_t[:, 0, :], frm_t[:, 2, :], ALU.add).then_inc(fs_summed, 1)
            for h in range(HEADS):
                for w4, w in ((wq4, W_Q), (wk4, W_K)):
                    link(dve.tensor_copy(w4[:, h, :, :], w[:, C * h:C * (h + 1)].unsqueeze(1)
                                         .to_broadcast([P, 4, C])))
            dve.wait_ge(fs_turned, 1)
            dve.tensor_copy(fscale[:, :], PS[:, 0:NB]).then_inc(deg_ready, 1)

            def sum_rows(j, q):
                dve.wait_ge(rows_in[q % 2], j * 32 + 16 * (q // 2 + 1))
                dve.tensor_reduce(rs_part[:, q, ds(j * BPC, BPC)],
                                  tiles[:, q % 2, :].rearrange("p (b m) -> p b m", b=BPC),
                                  X_AX, ALU.add).then_inc(rows_summed, 1)

            with dve.Fori(0, NCH) as j:
                for q in range(TQ):
                    sum_rows(j, q)
            dve.wait_ge(rows_summed, NCH * TQ)
            dve.tensor_reduce(rowsum[:, :], rs_part[:, :, :].rearrange("p q n -> p n q"), X_AX, ALU.add)\
                .then_inc(deg_ready, 1)
            dve.wait_ge(deg_root, 1)
            link(dve.reciprocal(rdeg[:, :], deg[:, :]))

            def scale_x(k, r):
                for j in range(NCH):
                    dve.tensor_tensor(by_block(XA[:, j * CH:(j + 1) * CH]),
                                      by_block(xres[:, j * CH:(j + 1) * CH]),
                                      over_features(r[:, j * BPC:(j + 1) * BPC]), ALU.mult)\
                        .then_inc(x_ready[k], 1)

            scale_x(K_AGG1, rdeg)

            def layernorm(j, s, k, count):
                link(dve.tensor_reduce(e_sum[:, :], by_block(e_t[:, :]), X_AX, ALU.add))
                link(dve.tensor_scalar(e_sum[:, :], e_sum[:, :], 1.0 / F, None, ALU.mult))
                link(dve.tensor_tensor(by_block(e_c[:, :]), by_block(e_t[:, :]),
                                       over_features(e_sum[:, :]), ALU.subtract))
                link(dve.tensor_tensor(e_q[:, :], e_c[:, :], e_c[:, :], ALU.mult))
                dve.tensor_reduce(e_var[:, :], by_block(e_q[:, :]), X_AX, ALU.add).then_inc(var_ready, 1)
                dve.wait_ge(std_ready, count)
                link(dve.reciprocal(e_std[:, :], e_std[:, :]))

            def product(k):
                first_c = NCH * k

                def epilogue(j, s):
                    eps = by_block(bank(2 + s))
                    e_b, x_b = by_block(e_t[:, :]), by_block(xres[:, ds(j * CH, CH)])
                    dve.wait_ge(e_ready, j + (first_c + 1))
                    if k == K_AGG1:
                        link(dve.tensor_tensor(e_b, eps, over_features(rdeg[:, ds(j * BPC, BPC)]), ALU.mult))
                        dve.sem_inc(e_taken, 1)
                        link(dve.tensor_tensor(e_b, e_b, over_blocks(B_1), ALU.add))
                        link(dve.scalar_tensor_tensor(zc[:, s, :], e_t[:, :], 0.1, e_t[:, :], ALU.mult, ALU.max))
                        dve.sem_inc(z_ready, 1)
                        link(dve.tensor_tensor(zsq[:, :], zc[:, s, :], zc[:, s, :], ALU.mult))
                        link(dve.tensor_reduce(sqn[:, ds(j * BPC, BPC)], by_block(zsq[:, :]), X_AX, ALU.add))
                        ps = PS[0:JD, 6 * CH:7 * CH]
                        dve.wait_ge(sq_ready, j + 1)
                        link(dve.tensor_copy(sq_h[:, :], ps))
                        link(dve.tensor_tensor(sq_r[:, :], ps, sq_h[:, :], ALU.subtract))
                        link(dve.tensor_copy(sq_m[:, :], sq_r[:, :]))
                        link(dve.tensor_tensor(sq_r[:, :], sq_r[:, :], sq_m[:, :], ALU.subtract))
                        link(dve.tensor_scalar(sq_c[:, :], sq_h[:, :], ident[0:JD, 0:1], None, ALU.mult))
                        link(dve.scalar_tensor_tensor(sq_c[:, :], sq_m[:, :], ident[0:JD, 1:2], sq_c[:, :],
                                                      ALU.mult, ALU.add))
                        dve.scalar_tensor_tensor(sq3[:, ds(j * CH, CH)], sq_r[:, :], ident[0:JD, 2:3],
                                                 sq_c[:, :], ALU.mult, ALU.add).then_inc(sq_split, 1)
                    elif k == K_AGG2:
                        link(dve.tensor_tensor(e_b, eps, over_features(rdeg2[:, ds(j * BPC, BPC)]), ALU.mult))
                        dve.sem_inc(e_taken, 1)
                        link(dve.tensor_tensor(e_b, e_b, over_blocks(B_2), ALU.add))
                        link(dve.tensor_tensor(e_b, e_b, x_b, ALU.add))
                        layernorm(j, s, k, j + 1)
                        link(dve.tensor_tensor(x_b, by_block(e_c[:, :]), over_features(e_std[:, :]), ALU.mult))
                    elif k in (K_HOP1, K_HOP2):
                        n_sw = 0 if k == K_HOP1 else NCH
                        dve.tensor_tensor(e_b, eps, over_blocks(B_H), ALU.add).then_inc(swish_in, 1)
                        dve.wait_ge(swish_exp, j + (n_sw + 1))
                        dve.sem_inc(e_taken, 1)
                        link(dve.tensor_scalar(e_exp[:, :], e_exp[:, :], 1.0, None, ALU.add))
                        link(dve.reciprocal(e_exp[:, :], e_exp[:, :]))
                        if k == K_HOP1:
                            dve.tensor_tensor(XA[:, ds(j * CH, CH)], e_t[:, :], e_exp[:, :], ALU.mult)\
                                .then_inc(x_ready[K_HOP2], 1)
                            dve.wait_ge(x_ready[K_HOP2], j + 1)
                        else:
                            link(dve.tensor_tensor(e_t[:, :], e_t[:, :], e_exp[:, :], ALU.mult))
                            link(dve.tensor_tensor(e_b, e_b, x_b, ALU.add))
                            layernorm(j, s, k, j + (NCH + 1))
                            dve.tensor_tensor(x_b, by_block(e_c[:, :]), over_features(e_std[:, :]), ALU.mult)\
                                .then_inc(x_ready[K_FRM1], 1)
                            dve.wait_ge(x_ready[K_FRM1], j + 1)
                    elif k == K_FRM1:
                        dve.tensor_tensor(by_block(XA[:, ds(j * CH, CH)]), eps,
                                          over_features(fscale[:, ds(j * BPC, BPC)]), ALU.mult)\
                            .then_inc(x_ready[K_FRM2], 1)
                        dve.wait_ge(x_ready[K_FRM2], j + 1)
                        dve.sem_inc(e_taken, 1)
                    else:
                        link(dve.tensor_tensor(e_b, eps, over_blocks(B_F), ALU.add))
                        dve.sem_inc(e_taken, 1)
                        link(dve.tensor_tensor(e_b, e_b, x_b, ALU.add))
                        layernorm(j, s, k, j + (2 * NCH + 1))
                        dve.tensor_tensor(by_block(oc[:, s, :]), by_block(e_c[:, :]),
                                          over_features(e_std[:, :]), ALU.mult).then_inc(out_ready, 1)

                def sum_near(j, s):
                    for b in range(BPC):
                        r = b % 2
                        dve.wait_ge(rows_gathered[r], j * (2 * 16 * K_NEAR) + 16 * K_NEAR * (b // 2 + 1))
                        u = near_u[:, s * BPC + b, :]
                        w0 = (j * BPC + b) * K_NEAR
                        link(dve.tensor_scalar(u, gat[:, r, 0, :], near_s[:, ds(w0, 1)], None, ALU.mult))
                        for n in range(1, K_NEAR):
                            ins = dve.scalar_tensor_tensor(u, gat[:, r, n, :], near_s[:, ds(w0 + n, 1)], u,
                                                           ALU.mult, ALU.add)
                            if n < K_NEAR - 1:
                                link(ins)
                        ins.then_inc(u_ready, 1)

                per = {K_AGG1: 11, K_AGG2: 9 + 12, K_HOP1: 2, K_HOP2: 9, K_FRM1: 0, K_FRM2: 7}[k]

                if k == K_AGG2:
                    sum_near(0, 0)
                    sum_near(1, 1)
                    epilogue(0, 0)
                    n0 = chain.base + chain.n
                    with dve.Fori(1, NCH // 2) as i:
                        chain.enter(i, 1, 2 * per)
                        sum_near(i * 2, 0)
                        epilogue(i * 2 - 1, 1)
                        sum_near(i * 2 + 1, 1)
                        epilogue(i * 2, 0)
                    chain.leave(NCH // 2 - 1)
                    epilogue(NCH - 1, 1)
                    dve.sem_inc(att_done, 1)
                elif k == K_FRM2:
                    epilogue(0, 0)
                    epilogue(1, 1)
                    with dve.Fori(1, NCH // 2) as i:
                        chain.enter(i, 1, 2 * per)
                        for s in range(2):
                            dve.wait_ge(out_stored[s], i * 16)
                            epilogue(i * 2 + s, s)
                    chain.leave(NCH // 2 - 1)
                else:
                    with dve.Fori(0, NCH // 2) as i:
                        chain.enter(i, 0, 2 * per)
                        for s in range(2):
                            epilogue(i * 2 + s, s)
                    chain.leave(NCH // 2)

            product(K_AGG1)

            def search(b, s):
                dve.wait_ge(keys_copied, b * NG + NG)
                apart(dve)
                link(dve.max(top8[:, s, :], key_rows[s]))
                apart(dve)
                dve.max_index(idx8[:, s, :], top8[:, s, :], key_rows[s]).then_inc(near_found, 1)
                dve.tensor_copy(near_key[:, ds(b * K_NEAR, K_NEAR)], top8[:, s, 0:K_NEAR])
                dve.wait_ge(near_found, b + 1)
                link(dve.tensor_copy(near_idx[:, ds(b * K_NEAR, K_NEAR)], idx8[:, s, 0:K_NEAR]))

            with dve.Fori(0, NB // 2) as i:
                chain.enter(i, 0, 4)
                search(i * 2, 0)
                search(i * 2 + 1, 1)
            chain.leave(NB // 2)

            nk = near_key[:, :].rearrange("p (b n) -> p b n", n=K_NEAR)
            ns = near_s[:, :].rearrange("p (b n) -> p b n", n=K_NEAR)
            link(dve.scalar_tensor_tensor(ns, nk, -2.0, over_features(sqn[:, :], NB, K_NEAR), ALU.mult, ALU.add))
            dve.tensor_scalar(near_s[:, :], near_s[:, :], 0.0, 1e-10, ALU.max, ALU.add).then_inc(d_near, 1)
            dve.wait_ge(s_near, 2)
            link(dve.tensor_reduce(rdeg2[:, :], ns, X_AX, ALU.add))
            dve.tensor_tensor(rdeg2[:, :], rdeg2[:, :], rowsum[:, :], ALU.add).then_inc(deg2_ready, 1)
            dve.wait_ge(deg2_root, 1)
            link(dve.reciprocal(rdeg2[:, :], deg[:, :]))
            scale_x(K_AGG2, rdeg2)

            product(K_AGG2)

            khi = maskb[:, 0, 0:2 * CH].bitcast(f16).rearrange("p (r n) -> p r n", r=2)

            def stage_chunk(j, s):
                dve.tensor_copy(oc[:, s, :], xres[:, ds(j * CH, CH)]).then_inc(kx_staged, 1)

            def kv_chunk(j, s, nxt):
                if nxt:
                    dve.wait_ge(kx_turned, j + 1)
                    stage_chunk(j + 2, s)
                dve.wait_ge(v_ready, j + 1)
                dve.tensor_tensor(by_block(V[:, ds(j * CH, CH)]), by_block(bank(6 + s)), over_blocks(B_V),
                                  ALU.add).then_inc(v_taken, 1)
                for h in range(HEADS):
                    dve.wait_ge(k_halved, j * HEADS + (h + 1))
                    dve.scalar_tensor_tensor(kst[:, h, ds(j * CH, CH)], khi[:, h % 2, :], lo_k[:, :],
                                             pts[:, h % 2, :], ALU.mult, ALU.add).then_inc(k_stacked, 1)

            stage_chunk(0, 0)
            stage_chunk(1, 1)
            with dve.Fori(0, NCH // 2 - 1) as i:
                kv_chunk(i * 2, 0, True)
                kv_chunk(i * 2 + 1, 1, True)
            kv_chunk(NCH - 2, 0, False)
            kv_chunk(NCH - 1, 1, False)
            dve.wait_ge(k_stacked, NCH * HEADS)

            def mask(b, s):
                dve.wait_ge(mask_rows_in, b * 16 + 16)
                dve.tensor_scalar(maskb[:, s, :], adj_rows[:, :], 0.0, MASKED, ALU.is_equal, ALU.mult)\
                    .then_inc(mask_ready, 1)

            def take_scores(u, b, s, pr, i):
                hh, g = i // NG, i % NG
                h = 2 * pr + hh
                if pr == 0 and i == 0:
                    dve.wait_ge(mask_ready, b + 1)
                dve.wait_ge(s_ready, u * 8 + (i + 1))
                apart(dve)
                o = (i % 2) * GRP
                dve.tensor_tensor_reduce(
                    out=att_w[pr][hh][:, g * GRP:(g + 1) * GRP], in0=PS[:, o:o + GRP],
                    in1=maskb[:, s, g * GRP:(g + 1) * GRP], scale=1.0, scalar=-3.0e38, op0=ALU.add,
                    op1=ALU.max, accum_out=mx_part[:, hh, g:g + 1]).then_inc(s_taken, 1)
                if g == NG - 1:
                    dve.wait_ge(s_taken, u * 8 + (i + 1))
                    link(dve.tensor_reduce(mx4[:, s, h:h + 1], mx_part[:, hh, :], X_AX, ALU.max))
                    dve.tensor_scalar(nbias[:, h:h + 1], mx4[:, s, h:h + 1], -ATT_SCALE, None, ALU.mult)\
                        .then_inc(max_ready, 1)

            def stack_queries(b, s, pr):
                dve.wait_ge(q_halved, b * 2 + (pr + 1))
                dve.scalar_tensor_tensor(qst[:, s, 2 * pr:2 * pr + 2, :], q_hi[:, :, :], lo_q[:, :],
                                         q_full[:, :, :], ALU.mult, ALU.add).then_inc(q_stacked, 1)

            def take_xr(b, s):
                dve.wait_ge(xr_ready, b + 1)
                dve.tensor_tensor(xr_new[:, :], PS[:, 7 * CH:7 * CH + F], B_S, ALU.add)\
                    .then_inc(xr_taken, 1)

            def keep_xr(b, s):
                dve.wait_ge(xr_taken, b + 1)
                link(dve.tensor_copy(cat[:, s, F:2 * F], xr_new[:, :]))

            def copy_turned(u, t):
                dve.wait_ge(pt_ready, u * STEPS + (t + 1))
                dve.tensor_copy(pts[:, t % 2, :], bank(4 + t % 2)).then_inc(pt_by_dve, 1)

            def normalise(b, s):
                dve.wait_ge(o_turned, b + 1)
                link(dve.tensor_reduce(den4[:, :], den[:, s, :, :], X_AX, ALU.add))
                link(dve.reciprocal(rden4[:, :], den4[:, :]))
                link(dve.scalar_tensor_tensor(rden4[:, :], mx4[:, s, :], MASKED / 10, rden4[:, :],
                                              ALU.is_gt, ALU.mult))
                link(dve.tensor_tensor(cat[:, s, 0:F].rearrange("p (c h) -> p h c", h=HEADS),
                                       PS[:, 7 * CH + 3 * P:8 * CH].rearrange("p (h c) -> p h c", h=HEADS),
                                       over_features(rden4[:, :], HEADS, C), ALU.mult))
                link(dve.tensor_tensor(cat[:, s, 2 * F:3 * F], cat[:, s, 0:F], cat[:, s, F:2 * F],
                                       ALU.subtract))
                link(dve.tensor_tensor_reduce(out=cat_t[:, :], in0=cat[:, s, :], in1=wb_sb[:, :], scale=1.0,
                                              scalar=0.0, op0=ALU.mult, op1=ALU.add,
                                              accum_out=gate_z[:, :]))
                dve.sem_inc(gate_in, 1)

            def blend(b, s):
                dve.wait_ge(gate_exp, b + 1)
                link(dve.tensor_scalar(gate_b[:, :], gate_e[:, :], 1.0, None, ALU.add))
                link(dve.reciprocal(gate_b[:, :], gate_b[:, :]))
                link(dve.tensor_scalar(gate_b[:, :], gate_b[:, :], -1.0, None, ALU.mult))
                link(dve.scalar_tensor_tensor(att[:, :], cat[:, s, 2 * F:3 * F], gate_b[:, :],
                                              cat[:, s, 0:F], ALU.mult, ALU.add))
                link(dve.tensor_tensor(att[:, :], att[:, :], xres[:, ds(b * F, F)], ALU.add))
                link(dve.bn_stats(st6[:, :], att[:, :]))
                apart(dve)
                link(dve.bn_aggr(mv[:, :], st6[:, :]))
                dve.sem_inc(avar_ready, 1)

            def finish(b, s):
                dve.wait_ge(astd_ready, b + 1)
                link(dve.reciprocal(a_rstd[:, :], a_std[:, :]))
                dve.tensor_scalar(xres[:, ds(b * F, F)], att[:, :], mv[:, 0:1], a_rstd[:, :], ALU.subtract,
                                  ALU.mult).then_inc(att_done, 1)

            def phase(b, s, pr, prev, nxt):
                u = b * 2 + pr
                ahead = pr == 0 or nxt
                nb, nsl, npr = (b, s, 1) if pr == 0 else (b + 1, 1 - s, 0)
                for i in range(8):
                    if ahead:
                        take_scores(u + 1, nb, nsl, npr, i)
                    if i == 3 and pr == 0 and nxt:
                        stack_queries(b + 1, 1 - s, 0)
                        take_xr(b + 1, 1 - s)
                    if i == 3 and pr == 1 and prev:
                        blend(b - 1, 1 - s)
                if pr == 0 and nxt:
                    stack_queries(b + 1, 1 - s, 1)
                for t in DVE_STEPS:
                    copy_turned(u, t)
                if pr == 0:
                    if prev:
                        normalise(b - 1, 1 - s)
                    if nxt:
                        keep_xr(b + 1, 1 - s)
                        mask(b + 1, 1 - s)
                elif prev:
                    finish(b - 1, 1 - s)

            mask(0, 0)
            stack_queries(0, 0, 0)
            take_xr(0, 0)
            stack_queries(0, 0, 1)
            keep_xr(0, 0)
            for i in range(8):
                take_scores(0, 0, 0, 0, i)
            for s in range(2):
                for pr in range(2):
                    phase(s, s, pr, s > 0, True)
            with dve.Fori(1, NB // 2 - 1) as i:
                chain.enter(i, 1, 2 * (4 + 6 + 7 + 1 + 1))
                for s in range(2):
                    for pr in range(2):
                        phase(i * 2 + s, s, pr, True, True)
            chain.leave(NB // 2 - 2)
            for s in range(2):
                for pr in range(2):
                    phase(NB - 2 + s, s, pr, True, s == 0)
            normalise(NB - 1, 1)
            blend(NB - 1, 1)
            finish(NB - 1, 1)
            dve.wait_ge(att_done, NB + 1)
            dve.sem_inc(x_ready[K_HOP1], NCH)

            for k in (K_HOP1, K_HOP2, K_FRM1, K_FRM2):
                product(k)


_INS = ['x', 'adj', 'L0_gnn_W1', 'L0_gnn_b1', 'L0_gnn_W2', 'L0_gnn_b2', 'L1_gnn_Wq', 'L1_gnn_bq',
        'L1_gnn_Wk', 'L1_gnn_bk', 'L1_gnn_Wv', 'L1_gnn_bv', 'L1_gnn_Ws', 'L1_gnn_bs', 'L1_gnn_Wb',
        'L2_gnn_W', 'L2_gnn_b', 'L3_gnn_d_list', 'L3_gnn_weight', 'L3_gnn_filt', 'L3_gnn_bias']
_OUTS = [((4096, 128), 'float32')]


def kernel(**inputs):
    import numpy as _np
    import concourse.bacc as _bacc
    from concourse import mybir as _mybir
    from concourse.bass_utils import run_bass_kernel_spmd as _run

    nc = _bacc.Bacc("TRN2", target_bir_lowering=False, num_devices=1)
    arrays, args = {}, []
    for name in _INS:
        a = _np.ascontiguousarray(inputs[name])
        arrays[f"in_{name}_dram"] = a
        args.append(nc.dram_tensor(f"in_{name}_dram", a.shape, _mybir.dt.from_np(a.dtype), kind="ExternalInput").ap())
    for i, (shape, dtype) in enumerate(_OUTS):
        dt = _mybir.dt.from_np(_np.dtype(dtype))
        args.append(nc.dram_tensor(f"out_{i}_dram", shape, dt, kind="ExternalOutput").ap())
    graph_layers_kernel(nc, *args)
    r = _run(nc, [arrays], core_ids=[0])
    got = tuple(r.results[0][f"out_{i}_dram"] for i in range(len(_OUTS)))
    return got[0]
```

```python
from contextlib import ExitStack

import concourse.bass as bass
from concourse import mybir
from concourse.alu_op_type import AluOpType as ALU

ds = bass.ds
N, F, P = 4096, 128, 128
NB = N // P
CH = 512
BPC = CH // P
NCH = N // CH
TQ = 4
TC = NB // TQ
K_NEAR = 4
HEADS, C = 4, 32
JD = 3
LN_EPS = 1e-5
SPLIT = 64.0
MASKED = -1e30
ATT_SCALE = 1.0 / float(C) ** 0.5
GRP = 1024
NG = N // GRP
EXP = 1024
STEPS = NB // 4
DVE_STEPS = [2, 5]
ACT_STEPS = [t for t in range(STEPS) if t not in DVE_STEPS]
S_RING = 2
T_RING = 4
LAG = 3

K_AGG1, K_AGG2, K_HOP1, K_HOP2, K_FRM1, K_FRM2 = range(6)


class Count:

    def __init__(self, eng, sem):
        self.eng, self.sem, self.base, self.turn, self.n = eng, sem, 0, None, 0

    def link(self, ins):
        self.n += 1
        ins.then_inc(self.sem, 1)
        self.eng.wait_ge(self.sem, self.value())

    def mark(self, ins):
        self.n += 1
        return ins.then_inc(self.sem, 1)

    def settle(self):
        self.eng.wait_ge(self.sem, self.value())

    def value(self):
        if self.turn is None:
            return self.base + self.n
        i, first, per_turn = self.turn
        return i * per_turn + (self.base + self.n - first * per_turn)

    def enter(self, i, first, per_turn):
        self.base, self.n, self.turn = self.base + self.n, 0, (i, first, per_turn)

    def leave(self, turns):
        _, _, per_turn = self.turn
        assert self.n == per_turn, (self.n, per_turn)
        self.base, self.n, self.turn = self.base + turns * per_turn, 0, None


def graph_layers_kernel(nc, x, adj, W1, b1, W2, b2, Wq, bq, Wk, bk, Wv, bv, Ws, bs, Wb, Wh, bh,
                        d_list, Wf, filt, bf, out):
    f32, bf16, f16, u32 = mybir.dt.float32, mybir.dt.bfloat16, mybir.dt.float16, mybir.dt.uint32
    ACT = mybir.ActivationFunctionType
    X_AX = mybir.AxisListType.X

    adjT = nc.dram_tensor("adjT_tiles", (NCH * TQ * P, 2 * TC * CH), f16).ap()
    gtab = nc.dram_tensor("scaled_x_rows", (N, F), f32).ap()

    ctx = ExitStack()
    with ctx:
        def sb(name, shape, dt=f32):
            return ctx.enter_context(nc.sbuf_tensor(name, shape, dt))

        def sem(name):
            return ctx.enter_context(nc.semaphore(name))

        RES = TQ - 1
        xres = sb("xres", [P, NB * F])
        XA = sb("XA", [P, NB * F])
        tiles = sb("tiles", [P, 4, TC * CH])
        R2 = sb("R2", [P, 2 * N])
        adj_rows = sb("adj_rows", [P, N])
        maskb = sb("maskb", [P, 2, N], bf16)
        yT_sb = sb("yT_sb", [P, 2, CH])
        ident = sb("ident", [P, P])
        w_sb = sb("w_sb", [P, 8, F])
        tiles16 = tiles[:, :, :].rearrange("p s n -> p (s n)").bitcast(f16)\
            .rearrange("p (s a c n) -> p s a c n", s=4, a=2, c=TC)
        wq4 = sb("wq4", [P, HEADS, 4, C])
        wk4 = sb("wk4", [P, HEADS, 4, C])
        bq4 = sb("bq4", [P, HEADS])
        bk4 = sb("bk4", [P, HEADS])
        bias_sb = sb("bias_sb", [P, 6, F])
        wb_sb = sb("wb_sb", [P, 3 * F])
        eps_ln = sb("eps_ln", [P, 1])
        zero1 = sb("zero1", [P, 1])
        neg_half = sb("neg_half", [P, JD])
        lo_q = sb("lo_q", [P, 1])
        lo_k = sb("lo_k", [P, 1])
        frm = adj_rows[0:NB, 0:2 * JD * P].rearrange("b (a i p) -> b a i p", a=2, i=JD)
        frm_t = adj_rows[0:NB, 2 * JD * P:3 * JD * P].rearrange("b (i p) -> b i p", i=JD)
        fscale = sb("fscale", [P, NB])
        rs_part = sb("rs_part", [P, TQ, NB])
        rowsum = sb("rowsum", [P, NB])
        deg = sb("deg", [P, NB])
        rdeg = sb("rdeg", [P, NB])
        zc = adj_rows[:, 0:2 * CH].rearrange("p (s n) -> p s n", s=2)
        zsq = adj_rows[:, 2 * CH:3 * CH]
        sqn = sb("sqn", [P, NB])
        sqz = adj_rows[:, 3 * CH:5 * CH].rearrange("p (s n) -> p s n", s=2)
        sq_h = sb("sq_h", [JD, CH], bf16)
        sq_m = sb("sq_m", [JD, CH], bf16)
        sq_r = adj_rows[0:JD, 5 * CH:6 * CH]
        sq_c = adj_rows[0:JD, 6 * CH:7 * CH]
        sq3 = maskb[0:JD, 0, :]
        ones3 = sb("ones3", [JD, P], bf16)
        top8 = sb("top8", [P, 2, 8])
        idx8 = sb("idx8", [P, 2, 8], u32)
        near_key = sb("near_key", [P, NB * K_NEAR])
        near_idx = sb("near_idx", [P, NB * K_NEAR], u32)
        near_s = sb("near_s", [P, NB * K_NEAR])
        near_t = sb("near_t", [P, NB * K_NEAR])
        rdeg2 = sb("rdeg2", [P, NB])
        idx_st = sb("idx_st", [P, 2, K_NEAR], u32)
        gat = adj_rows[:, 0:2 * K_NEAR * F].rearrange("p (s n f) -> p s n f", s=2, n=K_NEAR)
        near_u = adj_rows[:, 2 * CH:4 * CH].rearrange("p (b f) -> p b f", f=F)
        e_tx = sb("e_tx", [P, 2 * CH])
        e_t, e_exp = e_tx[:, 0:CH], e_tx[:, CH:2 * CH]
        e_cq = sb("e_cq", [P, 2 * CH])
        e_c, e_q = e_cq[:, 0:CH], e_cq[:, CH:2 * CH]
        e_sum = sb("e_sum", [P, BPC])
        e_var = sb("e_var", [P, BPC])
        e_std = sb("e_std", [P, BPC])
        oc = sb("oc", [P, 2, CH])
        xst = sb("xst", [P, 2, F])
        xTst = sb("xTst", [P, 2, P])
        q_full = sb("q_full", [P, 2, P])
        q_hi = sb("q_hi", [P, 2, P], f16)
        qst = sb("qst", [P, 2, HEADS, P], f16)
        pts = [e_c, e_q, yT_sb[:, 0, :], yT_sb[:, 1, :]]
        mx_part = sb("mx_part", [P, 2, STEPS])
        mx4 = sb("mx4", [P, 2, HEADS])
        nbias = sb("nbias", [P, HEADS])
        den = sb("den", [P, 2, HEADS, N // EXP])
        den4 = sb("den4", [P, HEADS])
        rden4 = sb("rden4", [P, HEADS])
        oTs = sb("oTs", [P, HEADS, P])
        cat = e_tx[:, 0:6 * F].rearrange("p (s n) -> p s n", s=2)
        cat_t = oc[:, 0, 0:3 * F]
        gate_z = sb("gate_z", [P, 1])
        gate_e = sb("gate_e", [P, 1])
        gate_b = sb("gate_b", [P, 1])
        att = sb("att", [P, F])
        xr_new = oc[:, 1, 0:F]
        o_sum = oc[:, 1, F:2 * F]
        st6 = sb("st6", [P, 6])
        mv = sb("mv", [P, 2])
        mv_all = sb("mv_all", [P, NB, 2])
        a_std = sb("a_std", [P, NB])
        a_rstd = sb("a_rstd", [P, NB])

        PS = ctx.enter_context(nc.psum_tensor("PS", [P, 8 * CH], f32))

        def bank(b):
            return PS[:, b * CH:(b + 1) * CH]

        R2h = R2[:, :].bitcast(f16)
        zT = [R2h[:, 0:N], R2h[:, N:2 * N]]
        scaled_x = R2[:, N:2 * N]
        XA16 = XA[:, :].bitcast(f16)
        XB16 = maskb[:, :, :].rearrange("p s n -> p (s n)").bitcast(f16)
        op_A = [XA16[:, 0:N], XA16[:, N:2 * N]]
        op_B = [XB16[:, 0:N], XB16[:, N:2 * N]]
        kept = [t.bitcast(f16).rearrange("p (a c n) -> p a c n", a=2, c=TC)
                for t in (adj_rows[:, :], R2[:, 0:N], R2[:, N:2 * N])]
        kst = R2[:, :].bitcast(f16).rearrange("p (h n) -> p h n", h=HEADS)
        key_rows = [tiles[:, 2, :], tiles[:, 3, :]]
        att_w = [tiles[:, h, :] for h in range(HEADS)]
        V = XA
        W_1, W_2, W_H, W_F, W_Q, W_K, W_V, W_S = (w_sb[:, i, :] for i in range(8))
        B_1, B_2, B_H, B_F, B_V, B_S = (bias_sb[:, i, :] for i in range(6))
        weight_of = [W_1, W_2, W_H, W_H, W_F, ident[:, :]]
        operand_of = [op_A, op_A, op_A, op_B, op_A, op_B]

        def by_block(ap):
            return ap.rearrange("p (b f) -> p b f", f=F)

        def over_blocks(vec):
            return vec.unsqueeze(1).to_broadcast([P, BPC, F])

        def over_features(vec, n=BPC, f=F):
            return vec.unsqueeze(2).to_broadcast([P, n, f])

        consts_in = sem("consts_in")
        made = sem("made")
        fs_summed = sem("fs_summed")
        fs_turned = sem("fs_turned")
        rows_in = [sem(f"rows_in{i}") for i in range(2)]
        bank_turned = sem("bank_turned")
        bank_copied = sem("bank_copied")
        bank_split = sem("bank_split")
        rows_summed = sem("rows_summed")
        adjT_out = [sem(f"adjT_out{i}") for i in range(2)]
        deg_ready = sem("deg_ready")
        deg_root = sem("deg_root")
        x_ready = [sem(f"x_ready{k}") for k in range(6)]
        tile_in = [sem(f"tile_in{q}") for q in range(TQ)]
        tile_used = [sem(f"tile_used{q}") for q in range(RES)]
        kept_in = [sem(f"kept_in{q}") for q in range(RES)]
        y_ready = sem("y_ready")
        y_copied = sem("y_copied")
        e_ready = sem("e_ready")
        e_taken = sem("e_taken")
        z_ready = sem("z_ready")
        zT_turned = sem("zT_turned")
        zT_ready = sem("zT_ready")
        zT_split = sem("zT_split")
        sq_ready = sem("sq_ready")
        sq_split = sem("sq_split")
        keys_ready = sem("keys_ready")
        keys_copied = sem("keys_copied")
        near_found = sem("near_found")
        d_near = sem("d_near")
        s_near = sem("s_near")
        deg2_ready = sem("deg2_ready")
        deg2_root = sem("deg2_root")
        table_out = sem("table_out")
        idx_staged = sem("idx_staged")
        rows_gathered = [sem(f"rows_gathered{i}") for i in range(2)]
        u_ready = sem("u_ready")
        var_ready = sem("var_ready")
        std_ready = sem("std_ready")
        swish_in = sem("swish_in")
        swish_exp = sem("swish_exp")
        out_ready = sem("out_ready")
        out_stored = [sem(f"out_stored{i}") for i in range(2)]
        kx_staged = sem("kx_staged")
        kx_turned = sem("kx_turned")
        kx_copied = sem("kx_copied")
        v_ready = sem("v_ready")
        v_taken = sem("v_taken")
        k_ready = sem("k_ready")
        k_halved = sem("k_halved")
        k_stacked = sem("k_stacked")
        mask_rows_in = sem("mask_rows_in")
        mask_ready = sem("mask_ready")
        xst_ready = sem("xst_ready")
        xT_turned = sem("xT_turned")
        xT_copied = sem("xT_copied")
        xr_taken = sem("xr_taken")
        q_ready = sem("q_ready")
        q_halved = sem("q_halved")
        q_stacked = sem("q_stacked")
        s_ready = sem("s_ready")
        s_taken = sem("s_taken")
        max_ready = sem("max_ready")
        exp_done = sem("exp_done")
        pt_ready = sem("pt_ready")
        pt_by_act = sem("pt_by_act")
        pt_by_dve = sem("pt_by_dve")
        o_ready = sem("o_ready")
        o_copied = sem("o_copied")
        o_turned = sem("o_turned")
        gate_in = sem("gate_in")
        gate_exp = sem("gate_exp")
        avar_ready = sem("avar_ready")
        astd_ready = sem("astd_ready")
        att_done = sem("att_done")
        att_kept = sem("att_kept")
        passed = sem("passed")
        act_link = sem("act_link")
        dve_link = sem("dve_link")

        def loads_before(k, q):
            return NCH * k if k <= K_HOP1 or q >= RES else NCH * K_HOP1 + (NCH - 1) * (k - K_HOP1)

        def is_kept(k, q):
            return k >= K_HOP1 and q < RES

        N_CONSTS = 0
        consts = []

        consts.append((by_block(xres[:, :]), x.rearrange("(b p) f -> p b f", p=P)))
        for i, w in enumerate((W1, W2, Wh, Wf, Wq, Wk, Wv, Ws)):
            consts.append((w_sb[:, i, :], w))
        for i, b in enumerate((b1, b2, bh, bf, bv, bs)):
            consts.append((bias_sb[:, i, :], b.rearrange("(a n) -> a n", a=1).to_broadcast([P, F])))
        consts.append((wb_sb[:, :], Wb.rearrange("n a -> a n").to_broadcast([P, 3 * F])))
        for r in range(4):
            consts.append((bq4[C * r:C * (r + 1), :], bq.rearrange("(h c) -> c h", c=C)))
            consts.append((bk4[C * r:C * (r + 1), :], bk.rearrange("(h c) -> c h", c=C)))
        consts.append((frm[:, 0, :, :], d_list.rearrange("i (b p) -> b i p", p=P)))
        consts.append((frm[:, 1, :, :], filt.rearrange("i (b p) -> b i p", p=P)))
        N_CONSTS = 16 * len(consts)

        N_MADE = 14

        def apart(eng):
            eng.sem_inc(passed, 1)

        block = ctx.enter_context(nc.Block())

        @block.sync
        def _(sp):
            with nc.allow_non_contiguous_dma(reason="biases by partition, once"):
                for dst, src in consts:
                    sp.dma_start(dst, src).then_inc(consts_in, 16)

            def load_rows(j, q):
                src = adj[ds(j * CH, CH), q * TC * P:(q + 1) * TC * P]
                sp.dma_start(tiles[:, q % 2, :].rearrange("p (b m) -> p b m", b=BPC),
                             src.rearrange("(b p) m -> p b m", p=P)).then_inc(rows_in[q % 2], 16)

            for q in range(TQ):
                if q >= 2:
                    sp.wait_ge(bank_turned, (q - 1) * TC)
                    sp.wait_ge(rows_summed, q - 1)
                load_rows(0, q)
            with sp.Fori(1, NCH) as j:
                for q in range(TQ):
                    sp.wait_ge(bank_turned, j * (TQ * TC) + (q - 1) * TC)
                    apart(sp)
                    sp.wait_ge(rows_summed, j * TQ + (q - 1))
                    apart(sp)
                    load_rows(j, q)

            def load_tile(j, q):
                sp.dma_start(tiles16[:, q, :, :, :].rearrange("p a c n -> p (a c n)"),
                             adjT[ds((j * TQ + q) * P, P), :]).then_inc(tile_in[q], 16)

            def slot_free(k, j, q):
                if q < RES:
                    sp.wait_ge(tile_used[q], j + (loads_before(k, q) - (1 if is_kept(k, q) else 0)))
                else:
                    sp.wait_ge(y_ready, j + NCH * k)

            def load_rest(k):
                with sp.Fori(1, NCH) as j:
                    for q in range(TQ):
                        slot_free(k, j, q)
                        apart(sp)
                        load_tile(j, q)

            sp.wait_ge(bank_turned, (NCH * TQ - 1) * TC)
            sp.wait_ge(rows_summed, NCH * TQ - 1)
            sp.wait_ge(adjT_out[0], 16)
            load_tile(0, 0)
            sp.wait_ge(bank_turned, NCH * TQ * TC)
            sp.wait_ge(rows_summed, NCH * TQ)
            sp.wait_ge(adjT_out[1], 16)
            load_tile(0, 1)
            for i in range(2):
                sp.wait_ge(adjT_out[i], 16 * NCH * TQ // 2)
                load_tile(0, 2 + i)
            load_rest(K_AGG1)
            for q in range(TQ):
                slot_free(K_AGG2, 0, q)
                if q >= 2:
                    sp.wait_ge(near_found, NB)
                load_tile(0, q)
            load_rest(K_AGG2)

            def load_mask_rows(b):
                sp.dma_start(adj_rows[:, :], adj[ds(b * P, P), :]).then_inc(mask_rows_in, 16)

            sp.wait_ge(att_done, 1)
            load_mask_rows(0)
            with sp.Fori(1, NB) as b:
                sp.wait_ge(mask_ready, b)
                apart(sp)
                load_mask_rows(b)
            def keep_tile(q):
                sp.dma_start(kept[q].rearrange("p a c n -> p (a c n)"), adjT[q * P:(q + 1) * P, :])\
                    .then_inc(kept_in[q], 16)

            sp.wait_ge(mask_ready, NB)
            keep_tile(0)
            sp.wait_ge(s_ready, NB * HEADS * STEPS)
            keep_tile(1)
            keep_tile(2)
            sp.wait_ge(pt_ready, NB * HEADS * STEPS)
            for k in (K_HOP1, K_HOP2, K_FRM1, K_FRM2):
                slot_free(k, 0, RES)
                load_tile(0, RES)
                load_rest(k)
            for s in range(2):
                sp.wait_ge(out_stored[s], 16 * NCH // 2)

        @block.gpsimd
        def _(pool):
            pool.memset(ident[:, :], 0.0).then_inc(made, 1)
            pool.wait_ge(made, 1)
            pool.affine_select(out=ident[:, :], in_=ident[:, :], compare_op=ALU.not_equal, fill=1.0,
                               base=0, pattern=[[-1, P]], channel_multiplier=1).then_inc(made, 1)
            fills = [(eps_ln, LN_EPS), (zero1, 0.0), (neg_half, -0.5 * SPLIT ** 2), (ones3, 1.0)]
            fills += [(lo_q[C * r:C * (r + 1)], -1.0 if r >= 2 else 0.0) for r in range(4)]
            fills += [(lo_k[C * r:C * (r + 1)], -1.0 if r % 2 else 0.0) for r in range(4)]
            for n, (t, value) in enumerate(fills):
                pool.wait_ge(made, n + 2)
                pool.memset(t[:, :], value).then_inc(made, 1)

            pool.wait_ge(table_out, 16)

            def gather(b, s):
                pool.tensor_copy(idx_st[:, s, :], near_idx[:, ds(b * K_NEAR, K_NEAR)])\
                    .then_inc(idx_staged, 1)
                pool.wait_ge(idx_staged, b + 1)
                apart(pool)
                for n in range(K_NEAR):
                    pool.indirect_dma_start(
                        out=gat[:, s, n, :], out_offset=None, in_=gtab[:, :],
                        in_offset=bass.IndirectOffsetOnAxis(ap=idx_st[:, s, n:n + 1], axis=0),
                    ).then_inc(rows_gathered[s], 16)

            gather(0, 0)
            gather(1, 1)
            with pool.Fori(1, NB // 2) as i:
                for s in range(2):
                    b = i * 2 + s
                    pool.wait_ge(u_ready, b - 1)
                    pool.wait_ge(rows_gathered[s], i * (16 * K_NEAR))
                    gather(b, s)

            pool.wait_ge(k_stacked, NCH * HEADS)

            def stage_x(b, s):
                pool.tensor_copy(xst[:, s, :], xres[:, ds(b * F, F)]).then_inc(xst_ready, 1)

            def mask(b, s):
                pool.wait_ge(mask_rows_in, b * 16 + 16)
                apart(pool)
                pool.tensor_scalar(maskb[:, s, :], adj_rows[:, :], 0.0, MASKED, ALU.is_equal, ALU.mult)\
                    .then_inc(mask_ready, 1)

            for s in range(2):
                stage_x(s, s)
            mask(1, 1)
            with pool.Fori(1, NB // 2) as i:
                for s in range(2):
                    b = i * 2 + s
                    pool.wait_ge(xT_turned, b - 1)
                    stage_x(b, s)
                    pool.wait_ge(s_taken, (b - 1) * (HEADS * STEPS))
                    mask(b, s)

        @block.tensor
        def _(pe):
            pe.wait_ge(made, N_MADE)
            pe.wait_ge(fs_summed, 1)
            pe.transpose(PS[:, 0:NB], frm_t[:, 0, :], ident[0:NB, 0:NB]).then_inc(fs_turned, 1)
            pe.wait_ge(deg_ready, 1)

            def turn_tile(j, q, first):
                pe.wait_ge(rows_in[q % 2], j * 32 + 16 * (q // 2 + 1))
                for c in range(TC):
                    if not first:
                        pe.wait_ge(bank_split, j * (TQ * TC) + ((q - 1) * TC + c + 1))
                    for b in range(BPC):
                        src = tiles[:, q % 2, (b * TC + c) * P:(b * TC + c + 1) * P]
                        ins = pe.transpose(PS[:, c * CH + b * P:c * CH + (b + 1) * P], src, ident[:, :])
                    ins.then_inc(bank_turned, 1)

            def turn_chunk(j, first):
                for q in range(TQ):
                    turn_tile(j, q, first and q == 0)

            turn_chunk(0, True)
            with pe.Fori(1, NCH) as j:
                turn_chunk(j, False)
            pe.wait_ge(bank_split, NCH * TQ * TC)

            def product(k):
                X = operand_of[k]
                first_c = NCH * k

                def quarter(j, s, q, head):
                    if head:
                        pe.wait_ge(x_ready[k], 2 * q + 2)
                    if head and is_kept(k, q):
                        pe.wait_ge(kept_in[q], 16)
                        tile = kept[q]
                    else:
                        n = loads_before(k, q) + (0 if is_kept(k, q) else 1)
                        pe.wait_ge(tile_in[q], j * 16 + 16 * n)
                        tile = tiles16[:, q]
                    for c in range(TC):
                        m = q * TC + c
                        x_hi, x_lo = (part[:, m * F:(m + 1) * F] for part in X)
                        t_hi, t_lo = tile[:, 0, c, :], tile[:, 1, c, :]
                        pe.matmul(bank(s), x_hi, t_hi, start=(m == 0), stop=False, skip_group_check=True)
                        pe.matmul(bank(s), x_hi, t_lo, start=False, stop=False, skip_group_check=True)
                        ins = pe.matmul(bank(s), x_lo, t_hi, start=False,
                                        stop=(m == NB - 1 and k != K_AGG2), skip_group_check=True)
                    if q == RES:
                        if k != K_AGG2:
                            ins.then_inc(y_ready, 1)
                    elif not (head and is_kept(k, q)):
                        ins.then_inc(tile_used[q], 1)

                def weigh(j, s, fresh=False):
                    if not fresh:
                        pe.wait_ge(e_taken, j + first_c)
                    pe.wait_ge(y_copied, j + (first_c + 1))
                    for b in range(BPC):
                        ins = pe.matmul(bank(2 + s)[:, b * P:(b + 1) * P], yT_sb[:, s, b * P:(b + 1) * P],
                                        weight_of[k], start=True, stop=True)
                    ins.then_inc(e_ready, 1)

                def turn_z(j, s):
                    pe.wait_ge(z_ready, j + 1)
                    for b in range(BPC):
                        ins = pe.transpose(bank(4 + s)[:, b * P:(b + 1) * P],
                                           zc[:, s, b * P:(b + 1) * P], ident[:, :])
                    ins.then_inc(zT_turned, 1)

                def sum_z(j, s):
                    pe.wait_ge(zT_ready, j + 1)
                    pe.matmul(PS[0:JD, 6 * CH:7 * CH], neg_half[:, :], sqz[:, s, :], start=True,
                              stop=True).then_inc(sq_ready, 1)

                def add_near(j, s):
                    pe.wait_ge(u_ready, j * BPC + BPC)
                    for b in range(BPC):
                        ins = pe.matmul(bank(s)[:, b * P:(b + 1) * P], near_u[:, s * BPC + b, :],
                                        ident[:, :], start=False, stop=(b == BPC - 1),
                                        skip_group_check=True)
                    ins.then_inc(y_ready, 1)

                def chunk(j, s, head, after, head_next=False):
                    for q in range(TQ):
                        quarter(j, s, q, head)
                        if after and q == 0:
                            weigh(j - 1, 1 - s, k == K_AGG1 and head_next)
                        if after and q == 2 and k == K_AGG1:
                            turn_z(j - 1, 1 - s)
                    if k == K_AGG2:
                        add_near(j, s)
                    if k == K_AGG1 and after:
                        sum_z(j - 1, 1 - s)

                chunk(0, 0, True, False)
                chunk(1, 1, False, True, True)
                with pe.Fori(1, NCH // 2) as i:
                    chunk(i * 2, 0, False, True, False)
                    chunk(i * 2 + 1, 1, False, True)
                weigh(NCH - 1, 1)
                if k == K_AGG1:
                    turn_z(NCH - 1, 1)
                    sum_z(NCH - 1, 1)

            product(K_AGG1)

            pe.wait_ge(sq_split, NCH)
            pe.wait_ge(zT_split, NCH)
            pe.wait_ge(e_taken, NCH)

            def keys(b, first):
                z_hi, z_lo = (part[:, ds(b * P, P)] for part in zT)
                for g in range(NG):
                    if not first:
                        pe.wait_ge(keys_copied, b * NG + (g + 1 - NG))
                    for h in range(GRP // CH):
                        o = g * GRP + h * CH
                        hi, lo = (part[:, o:o + CH] for part in zT)
                        pe.matmul(PS[:, o:o + CH], z_hi, hi, start=True, stop=False)
                        pe.matmul(PS[:, o:o + CH], z_hi, lo, start=False, stop=False)
                        pe.matmul(PS[:, o:o + CH], z_lo, hi, start=False, stop=False)
                        ins = pe.matmul(PS[:, o:o + CH], ones3[:, :], sq3[:, o:o + CH], start=False,
                                        stop=True)
                    ins.then_inc(keys_ready, 1)

            keys(0, True)
            with pe.Fori(1, NB) as b:
                keys(b, False)
            pe.wait_ge(keys_copied, NB * NG)

            product(K_AGG2)

            def kv_chunk(j, s, first):
                pe.wait_ge(kx_staged, j + 1)
                for b in range(BPC):
                    ins = pe.transpose(bank(4 + s)[:, b * P:(b + 1) * P], oc[:, s, b * P:(b + 1) * P],
                                       ident[:, :])
                ins.then_inc(kx_turned, 1)
                pe.wait_ge(kx_copied, j + 1)
                if not first:
                    pe.wait_ge(v_taken, j - 1)
                for b in range(BPC):
                    ins = pe.matmul(bank(6 + s)[:, b * P:(b + 1) * P], yT_sb[:, s, b * P:(b + 1) * P],
                                    W_V, start=True, stop=True)
                ins.then_inc(v_ready, 1)
                for h in range(HEADS):
                    if not (first and s == 0):
                        pe.wait_ge(k_halved, j * HEADS + (h + 1 - HEADS))
                    pe.matmul(bank(h), wk4[:, h, :, :].rearrange("p r c -> p (r c)"), yT_sb[:, s, :],
                              start=True, stop=True).then_inc(k_ready, 1)

            pe.wait_ge(att_done, 1)
            kv_chunk(0, 0, True)
            kv_chunk(1, 1, True)
            with pe.Fori(1, NCH // 2) as i:
                kv_chunk(i * 2, 0, False)
                kv_chunk(i * 2 + 1, 1, False)
            pe.wait_ge(k_stacked, NCH * HEADS)
            pe.wait_ge(v_taken, NCH)

            def turn_x(b, s, m):
                pe.wait_ge(xst_ready, b + 1)
                pe.transpose(bank(m)[:, 0:P], xst[:, s, :], ident[:, :]).then_inc(xT_turned, 1)

            def queries(b, s, pr, m):
                if pr == 0:
                    pe.wait_ge(xT_copied, b + 1)
                    pe.matmul(bank(m)[:, 0:F], xTst[:, s, :], W_S, start=True, stop=True)
                else:
                    pe.wait_ge(q_halved, b * 2 + 1)
                for hh in range(2):
                    o = P + hh * P
                    ins = pe.matmul(bank(m)[:, o:o + P],
                                    wq4[:, 2 * pr + hh, :, :].rearrange("p r c -> p (r c)"),
                                    xTst[:, s, :], start=True, stop=True)
                ins.then_inc(q_ready, 1)

            def scores(v, qb, s, h, t, first):
                if t == 0 and h % 2 == 0:
                    pe.wait_ge(q_stacked, qb * 2 + (h // 2 + 1))
                if not (first and t < S_RING):
                    pe.wait_ge(s_taken, v * STEPS + (t - S_RING + 1))
                pe.matmul(bank(t % S_RING), qst[:, s, h, :], kst[:, h, t * CH:(t + 1) * CH],
                          start=True, stop=True).then_inc(s_ready, 1)

            def turn_weights(v, h, t):
                if t % (EXP // CH) == 0:
                    pe.wait_ge(exp_done, v * (N // EXP) + (t // (EXP // CH) + 1))
                for r in range(4):
                    col = (4 * t + r) * P
                    ins = pe.transpose(bank(S_RING + t % T_RING)[:, r * P:(r + 1) * P],
                                       att_w[h][:, col:col + P], ident[:, :])
                ins.then_inc(pt_ready, 1)

            def weigh_values(b, s, v, h, t, prev, prevprev):
                if t in ACT_STEPS:
                    pe.wait_ge(pt_by_act, v * len(ACT_STEPS) + (ACT_STEPS.index(t) + 1))
                else:
                    pe.wait_ge(pt_by_dve, v * len(DVE_STEPS) + (DVE_STEPS.index(t) + 1))
                if t == 0 and h == 0 and prev:
                    if prevprev:
                        pe.wait_ge(gate_in, b - 1)
                    else:
                        pe.wait_ge(q_halved, 4)
                for r in range(4):
                    m = 4 * t + r
                    ins = pe.matmul(bank(6 + s)[C * r:C * (r + 1), h * P:(h + 1) * P],
                                    V[:, m * F + C * h:m * F + C * (h + 1)],
                                    pts[t % T_RING][:, r * P:(r + 1) * P], start=(t == 0),
                                    stop=(t == STEPS - 1), skip_group_check=True,
                                    tile_position=(0, C * r))
                if t == STEPS - 1 and h == HEADS - 1:
                    ins.then_inc(o_ready, 1)

            def turn_out(b, m, asked):
                pe.wait_ge(o_copied, b + 1)
                if asked:
                    pe.wait_ge(q_halved, b * 2 + 6)
                for h in range(HEADS):
                    ins = pe.transpose(bank(m)[:, h * P:(h + 1) * P], oTs[:, h, :], ident[:, :])
                ins.then_inc(o_turned, 1)

            def phase(b, s, h, prev, prevprev, nxt):
                v = b * HEADS + h
                for t in range(STEPS):
                    if t >= LAG:
                        weigh_values(b, s, v, h, t - LAG, prev, prevprev)
                    elif h > 0:
                        weigh_values(b, s, v - 1, h - 1, STEPS + t - LAG, prev, prevprev)
                    elif prev:
                        weigh_values(b - 1, 1 - s, v - 1, HEADS - 1, STEPS + t - LAG, True, True)
                    turn_weights(v, h, t)
                    if h < 2 or nxt:
                        scores(v + 2, b if h < 2 else b + 1, s if h < 2 else 1 - s, (h + 2) % HEADS,
                               t, False)
                    if nxt and h == 0 and t == 5:
                        if prev:
                            pe.wait_ge(o_copied, b)
                        else:
                            pe.wait_ge(q_halved, 2)
                        turn_x(b + 1, 1 - s, 7 - s)
                    if nxt and h == 1 and t % 4 == 0:
                        queries(b + 1, 1 - s, t // 4, 7 - s)
                    if prev and h == 2 and t == 0:
                        turn_out(b - 1, 7 - s, nxt)

            turn_x(0, 0, 7)
            queries(0, 0, 0, 7)
            queries(0, 0, 1, 7)
            for v in range(2):
                for t in range(STEPS):
                    scores(v, 0, 0, v, t, v == 0)
            for s in range(2):
                for h in range(HEADS):
                    phase(s, s, h, s > 0, False, True)
            with pe.Fori(1, NB // 2 - 1) as i:
                for s in range(2):
                    for h in range(HEADS):
                        phase(i * 2 + s, s, h, True, True, True)
            for s in range(2):
                for h in range(HEADS):
                    phase(NB - 2 + s, s, h, True, True, s == 0)
            for t in range(STEPS - LAG, STEPS):
                weigh_values(NB - 1, 1, NB * HEADS - 1, HEADS - 1, t, True, True)
            turn_out(NB - 1, 7, False)
            pe.wait_ge(att_done, NB + 1)

            for k in (K_HOP1, K_HOP2, K_FRM1, K_FRM2):
                product(k)

        @block.scalar
        def _(act):
            chain = Count(act, act_link)
            act.wait_ge(made, N_MADE)

            def store_tile(t, q):
                act.wait_ge(bank_split, t * TC + TC)
                act.dma_start(adjT[ds(t * P, P), :],
                              tiles16[:, 2 + q % 2, :, :, :].rearrange("p a c n -> p (a c n)"))\
                    .then_inc(adjT_out[q % 2], 16)

            def copy_tile(j, q, first, fresh):
                if not fresh:
                    act.wait_ge(adjT_out[q % 2], j * 32 + 16 * (q // 2))
                for c in range(TC):
                    act.wait_ge(bank_turned, j * (TQ * TC) + (q * TC + c + 1))
                    act.activation(tiles16[:, 2 + q % 2, 0, c, :], bank(c), ACT.Copy, scale=SPLIT)\
                        .then_inc(bank_copied, 1)
                    if c == TC // 2 and not first:
                        store_tile(j * TQ + (q - 1), q - 1)

            for q in range(TQ):
                copy_tile(0, q, q < 1, q < 2)
            with act.Fori(1, NCH) as j:
                for q in range(TQ):
                    copy_tile(j, q, False, False)
            store_tile(NCH * TQ - 1, TQ - 1)

            act.wait_ge(deg_ready, 2)
            act.activation(deg[:, :], rowsum[:, :], ACT.Sqrt, bias=zero1[:, :]).then_inc(deg_root, 1)

            def product(k):
                first_c = NCH * k

                def chunk(j, s, n_ln, n_sw):
                    act.wait_ge(y_ready, j + (first_c + 1))
                    act.activation(yT_sb[:, s, :], bank(s), ACT.Copy, scale=1.0 / SPLIT ** 2)\
                        .then_inc(y_copied, 1)
                    if k == K_AGG1:
                        act.wait_ge(zT_turned, j + 1)
                        act.activation(zT[0][:, ds(j * CH, CH)], bank(4 + s), ACT.Copy, scale=SPLIT)\
                            .then_inc(act_link, 1)
                        act.activation(sqz[:, s, :], bank(4 + s), ACT.Square, bias=zero1[:, :])\
                            .then_inc(act_link, 1)
                        act.wait_ge(act_link, j * 2 + 2)
                        act.sem_inc(zT_ready, 1)
                    if k in (K_HOP1, K_HOP2):
                        act.wait_ge(swish_in, j + (n_sw + 1))
                        act.activation(e_exp[:, :], e_t[:, :], ACT.Exp, scale=-1.0, bias=zero1[:, :])\
                            .then_inc(swish_exp, 1)
                    if k in (K_AGG2, K_HOP2, K_FRM2):
                        act.wait_ge(var_ready, j + (n_ln + 1))
                        act.activation(e_std[:, :], e_var[:, :], ACT.Sqrt, scale=1.0 / F,
                                       bias=eps_ln[:, :]).then_inc(std_ready, 1)
                    if k == K_FRM2:
                        act.wait_ge(out_ready, j + 1)
                        act.dma_start(out[ds(j * CH, CH), :].rearrange("(b p) f -> p b f", p=P),
                                      by_block(oc[:, s, :])).then_inc(out_stored[s], 16)

                n_ln = {K_AGG2: 0, K_HOP2: NCH, K_FRM2: 2 * NCH}.get(k)
                n_sw = {K_HOP1: 0, K_HOP2: NCH}.get(k)
                with act.Fori(0, NCH // 2) as i:
                    for s in range(2):
                        chunk(i * 2 + s, s, n_ln, n_sw)

            product(K_AGG1)

            def keys(b, s, first):
                if not first:
                    act.wait_ge(near_found, b - 1)
                for g in range(NG):
                    act.wait_ge(keys_ready, b * NG + (g + 1))
                    act.activation(key_rows[s][:, g * GRP:(g + 1) * GRP], PS[:, g * GRP:(g + 1) * GRP],
                                   ACT.Copy).then_inc(keys_copied, 1)

            act.wait_ge(y_ready, NCH)
            act.wait_ge(y_copied, NCH)
            keys(0, 0, True)
            keys(1, 1, True)
            with act.Fori(1, NB // 2) as i:
                keys(i * 2, 0, False)
                keys(i * 2 + 1, 1, False)

            act.wait_ge(d_near, 1)
            act.activation(near_t[:, :], near_s[:, :], ACT.Sqrt, bias=zero1[:, :]).then_inc(s_near, 1)
            act.wait_ge(s_near, 1)
            act.activation(near_s[:, :], near_t[:, :], ACT.Exp, scale=-0.5, bias=zero1[:, :])\
                .then_inc(s_near, 1)
            act.wait_ge(deg2_ready, 1)
            act.activation(deg[:, :], rdeg2[:, :], ACT.Sqrt, bias=zero1[:, :]).then_inc(deg2_root, 1)
            act.wait_ge(x_ready[K_AGG2], NCH)
            act.dma_start(gtab.rearrange("(b p) f -> p b f", p=P), by_block(scaled_x))\
                .then_inc(table_out, 16)

            product(K_AGG2)

            def kv_chunk(j, s, first):
                act.wait_ge(kx_turned, j + 1)
                if not first:
                    act.wait_ge(k_ready, j * HEADS - HEADS)
                act.activation(yT_sb[:, s, :], bank(4 + s), ACT.Copy).then_inc(kx_copied, 1)
                for h in range(HEADS):
                    r = h % 2
                    act.wait_ge(k_ready, j * HEADS + (h + 1))
                    if not (first and s == 0 and h < 2):
                        act.wait_ge(k_stacked, j * HEADS + (h - 1))
                    act.activation(pts[r], bank(h), ACT.Identity, bias=bk4[:, h:h + 1],
                                   scale=SPLIT)\
                        .then_inc(act_link, 1)
                    act.activation(khi[:, r, :], bank(h), ACT.Identity, bias=bk4[:, h:h + 1],
                                   scale=SPLIT)\
                        .then_inc(k_halved, 1)

            khi = maskb[:, 0, 0:2 * CH].bitcast(f16).rearrange("p (r n) -> p r n", r=2)
            kv_chunk(0, 0, True)
            kv_chunk(1, 1, True)
            with act.Fori(1, NCH // 2) as i:
                kv_chunk(i * 2, 0, False)
                kv_chunk(i * 2 + 1, 1, False)

            def copy_xT(b, s, m):
                act.wait_ge(xT_turned, b + 1)
                act.activation(xTst[:, s, :], bank(m)[:, 0:P], ACT.Copy).then_inc(xT_copied, 1)

            def halve_queries(b, s, pr, m, first):
                act.wait_ge(q_ready, b * 2 + (pr + 1))
                if pr == 0:
                    act.wait_ge(xr_taken, b + 1)
                if not (first and pr == 0):
                    act.wait_ge(q_stacked, b * 2 + pr)
                for hh in range(2):
                    h = 2 * pr + hh
                    src = bank(m)[:, P + hh * P:P + (hh + 1) * P]
                    act.activation(q_full[:, hh, :], src, ACT.Identity, bias=bq4[:, h:h + 1],
                                   scale=SPLIT)\
                        .then_inc(act_link, 1)
                    ins = act.activation(q_hi[:, hh, :], src, ACT.Identity, bias=bq4[:, h:h + 1],
                                   scale=SPLIT)
                ins.then_inc(q_halved, 1)

            def exponentials(v, s, h, i):
                if i == 0:
                    act.wait_ge(max_ready, v + 1)
                w = att_w[h][:, i * EXP:(i + 1) * EXP]
                act.activation(w, w, ACT.Exp, bias=nbias[:, h:h + 1], scale=ATT_SCALE / SPLIT ** 2,
                               accum_out=den[:, s, h, i:i + 1]).then_inc(exp_done, 1)

            def copy_turned(v, t):
                act.wait_ge(pt_ready, v * STEPS + (t + 1))
                act.activation(pts[t % T_RING], bank(S_RING + t % T_RING), ACT.Copy).then_inc(pt_by_act, 1)

            def copy_out(b, m):
                act.wait_ge(o_ready, b + 1)
                act.activation(oTs[:, :, :].rearrange("p r n -> p (r n)"), bank(m), ACT.Copy)\
                    .then_inc(o_copied, 1)

            def gate(b):
                act.wait_ge(gate_in, b + 1)
                act.activation(gate_e[:, :], gate_z[:, :], ACT.Exp, scale=-1.0, bias=zero1[:, :])\
                    .then_inc(gate_exp, 1)

            def phase(b, s, h, prev, nxt):
                v = b * HEADS + h
                for t in range(STEPS):
                    if prev and h == 0 and t == LAG:
                        copy_out(b - 1, 7 - s)
                    if t in ACT_STEPS:
                        copy_turned(v, t)
                    if nxt and h == 0 and t == 6:
                        copy_xT(b + 1, 1 - s, 7 - s)
                    if nxt and h == 1 and t % 4 == 2:
                        halve_queries(b + 1, 1 - s, t // 4, 7 - s, False)
                    if prev and h == 3 and t == 0:
                        gate(b - 1)
                    if t == 0:
                        exponentials(v, s, h, N // EXP - 1)
                    elif t % 2 == 0 and (h < HEADS - 1 or nxt):
                        exponentials(v + 1, s if h < HEADS - 1 else 1 - s, (h + 1) % HEADS, t // 2 - 1)

            copy_xT(0, 0, 7)
            halve_queries(0, 0, 0, 7, True)
            halve_queries(0, 0, 1, 7, True)
            for i in range(N // EXP - 1):
                exponentials(0, 0, 0, i)
            for s in range(2):
                for h in range(HEADS):
                    phase(s, s, h, s > 0, True)
            with act.Fori(1, NB // 2 - 1) as i:
                for s in range(2):
                    for h in range(HEADS):
                        phase(i * 2 + s, s, h, True, True)
            for s in range(2):
                for h in range(HEADS):
                    phase(NB - 2 + s, s, h, True, s == 0)
            copy_out(NB - 1, 7)
            gate(NB - 1)
            act.wait_ge(avar_ready, NB)
            act.activation(a_std[:, :], mv_all[:, :, 1], ACT.Sqrt, bias=eps_ln[:, :]).then_inc(astd_ready, 1)

            for k in (K_HOP1, K_HOP2, K_FRM1, K_FRM2):
                product(k)

        @block.vector
        def _(dve):
            chain = Count(dve, dve_link)
            link = chain.link
            mark, settle = chain.mark, chain.settle

            dve.wait_ge(consts_in, N_CONSTS)
            dve.wait_ge(made, N_MADE)
            link(dve.tensor_tensor(frm_t[:, :, :], frm[:, 0, :, :], frm[:, 1, :, :], ALU.mult))
            link(dve.tensor_tensor(frm_t[:, :, :], frm_t[:, :, :], frm[:, 0, :, :], ALU.mult))
            link(dve.tensor_tensor(frm_t[:, 0, :], frm_t[:, 0, :], frm_t[:, 1, :], ALU.add))
            dve.tensor_tensor(frm_t[:, 0, :], frm_t[:, 0, :], frm_t[:, 2, :], ALU.add).then_inc(fs_summed, 1)
            for h in range(HEADS):
                for w4, w in ((wq4, W_Q), (wk4, W_K)):
                    link(dve.tensor_copy(w4[:, h, :, :], w[:, C * h:C * (h + 1)].unsqueeze(1)
                                         .to_broadcast([P, 4, C])))
            link(dve.tensor_scalar(bq4[:, :], bq4[:, :], SPLIT, None, ALU.mult))
            link(dve.tensor_scalar(bk4[:, :], bk4[:, :], SPLIT, None, ALU.mult))
            dve.wait_ge(fs_turned, 1)
            dve.tensor_copy(fscale[:, :], PS[:, 0:NB]).then_inc(deg_ready, 1)

            def split_tile(j, q):
                for c in range(TC):
                    dve.wait_ge(bank_copied, j * (TQ * TC) + (q * TC + c + 1))
                    dve.scalar_tensor_tensor(tiles16[:, 2 + q % 2, 1, c, :], bank(c), SPLIT,
                                             tiles16[:, 2 + q % 2, 0, c, :], ALU.mult, ALU.subtract)\
                        .then_inc(bank_split, 1)

            def sum_rows(j, q):
                dve.wait_ge(rows_in[q % 2], j * 32 + 16 * (q // 2 + 1))
                dve.tensor_reduce(rs_part[:, q, ds(j * BPC, BPC)],
                                  tiles[:, q % 2, :].rearrange("p (b m) -> p b m", b=BPC),
                                  X_AX, ALU.add).then_inc(rows_summed, 1)

            with dve.Fori(0, NCH) as j:
                for q in range(TQ):
                    split_tile(j, q)
                    sum_rows(j, q)
            dve.wait_ge(rows_summed, NCH * TQ)
            dve.tensor_reduce(rowsum[:, :], rs_part[:, :, :].rearrange("p q n -> p n q"), X_AX, ALU.add)\
                .then_inc(deg_ready, 1)
            dve.wait_ge(deg_root, 1)
            link(dve.reciprocal(rdeg[:, :], deg[:, :]))

            def split(k, j, src):
                hi, lo = (part[:, ds(j * CH, CH)] for part in operand_of[k])
                link(dve.tensor_scalar(hi, src, SPLIT, None, ALU.mult))
                dve.scalar_tensor_tensor(lo, src, SPLIT, hi, ALU.mult, ALU.subtract).then_inc(x_ready[k], 1)
                dve.wait_ge(x_ready[k], j + 1)

            def scale_x(k, r):
                for j in range(NCH):
                    g = scaled_x[:, j * CH:(j + 1) * CH]
                    link(dve.tensor_tensor(by_block(g), by_block(xres[:, j * CH:(j + 1) * CH]),
                                           over_features(r[:, j * BPC:(j + 1) * BPC]), ALU.mult))
                    split(k, j, g)

            scale_x(K_AGG1, rdeg)

            def layernorm(j, s, k, count):
                link(dve.tensor_reduce(e_sum[:, :], by_block(e_t[:, :]), X_AX, ALU.add))
                link(dve.tensor_scalar(e_sum[:, :], e_sum[:, :], 1.0 / F, None, ALU.mult))
                link(dve.tensor_tensor(by_block(e_c[:, :]), by_block(e_t[:, :]),
                                       over_features(e_sum[:, :]), ALU.subtract))
                link(dve.tensor_tensor(e_q[:, :], e_c[:, :], e_c[:, :], ALU.mult))
                dve.tensor_reduce(e_var[:, :], by_block(e_q[:, :]), X_AX, ALU.add).then_inc(var_ready, 1)
                dve.wait_ge(std_ready, count)
                link(dve.reciprocal(e_std[:, :], e_std[:, :]))

            def product(k):
                first_c = NCH * k

                def epilogue(j, s):
                    eps = by_block(bank(2 + s))
                    e_b, x_b = by_block(e_t[:, :]), by_block(xres[:, ds(j * CH, CH)])
                    dve.wait_ge(e_ready, j + (first_c + 1))
                    if k == K_AGG1:
                        link(dve.tensor_tensor(e_b, eps, over_features(rdeg[:, ds(j * BPC, BPC)]), ALU.mult))
                        dve.sem_inc(e_taken, 1)
                        link(dve.tensor_tensor(e_b, e_b, over_blocks(B_1), ALU.add))
                        link(dve.scalar_tensor_tensor(zc[:, s, :], e_t[:, :], 0.1, e_t[:, :], ALU.mult, ALU.max))
                        dve.sem_inc(z_ready, 1)
                        link(dve.tensor_tensor(zsq[:, :], zc[:, s, :], zc[:, s, :], ALU.mult))
                        link(dve.tensor_reduce(sqn[:, ds(j * BPC, BPC)], by_block(zsq[:, :]), X_AX, ALU.add))
                        dve.wait_ge(zT_ready, j + 1)
                        dve.scalar_tensor_tensor(zT[1][:, ds(j * CH, CH)], bank(4 + s), SPLIT,
                                                 zT[0][:, ds(j * CH, CH)], ALU.mult, ALU.subtract)\
                            .then_inc(zT_split, 1)
                        ps = PS[0:JD, 6 * CH:7 * CH]
                        dve.wait_ge(sq_ready, j + 1)
                        link(dve.tensor_copy(sq_h[:, :], ps))
                        link(dve.tensor_tensor(sq_r[:, :], ps, sq_h[:, :], ALU.subtract))
                        link(dve.tensor_copy(sq_m[:, :], sq_r[:, :]))
                        link(dve.tensor_tensor(sq_r[:, :], sq_r[:, :], sq_m[:, :], ALU.subtract))
                        link(dve.tensor_scalar(sq_c[:, :], sq_h[:, :], ident[0:JD, 0:1], None, ALU.mult))
                        link(dve.scalar_tensor_tensor(sq_c[:, :], sq_m[:, :], ident[0:JD, 1:2], sq_c[:, :],
                                                      ALU.mult, ALU.add))
                        dve.scalar_tensor_tensor(sq3[:, ds(j * CH, CH)], sq_r[:, :], ident[0:JD, 2:3],
                                                 sq_c[:, :], ALU.mult, ALU.add).then_inc(sq_split, 1)
                    elif k == K_AGG2:
                        link(dve.tensor_tensor(e_b, eps, over_features(rdeg2[:, ds(j * BPC, BPC)]), ALU.mult))
                        dve.sem_inc(e_taken, 1)
                        link(dve.tensor_tensor(e_b, e_b, over_blocks(B_2), ALU.add))
                        link(dve.tensor_tensor(e_b, e_b, x_b, ALU.add))
                        layernorm(j, s, k, j + 1)
                        link(dve.tensor_tensor(x_b, by_block(e_c[:, :]), over_features(e_std[:, :]), ALU.mult))
                    elif k in (K_HOP1, K_HOP2):
                        n_sw = 0 if k == K_HOP1 else NCH
                        dve.tensor_tensor(e_b, eps, over_blocks(B_H), ALU.add).then_inc(swish_in, 1)
                        dve.wait_ge(swish_exp, j + (n_sw + 1))
                        dve.sem_inc(e_taken, 1)
                        link(dve.tensor_scalar(e_exp[:, :], e_exp[:, :], 1.0, None, ALU.add))
                        link(dve.reciprocal(e_exp[:, :], e_exp[:, :]))
                        if k == K_HOP1:
                            link(dve.tensor_tensor(e_t[:, :], e_t[:, :], e_exp[:, :], ALU.mult))
                            split(K_HOP2, j, e_t[:, :])
                        else:
                            link(dve.tensor_tensor(e_t[:, :], e_t[:, :], e_exp[:, :], ALU.mult))
                            link(dve.tensor_tensor(e_b, e_b, x_b, ALU.add))
                            layernorm(j, s, k, j + (NCH + 1))
                            link(dve.tensor_tensor(x_b, by_block(e_c[:, :]), over_features(e_std[:, :]),
                                                   ALU.mult))
                            split(K_FRM1, j, xres[:, ds(j * CH, CH)])
                    elif k == K_FRM1:
                        link(dve.tensor_tensor(e_b, eps, over_features(fscale[:, ds(j * BPC, BPC)]), ALU.mult))
                        dve.sem_inc(e_taken, 1)
                        split(K_FRM2, j, e_t[:, :])
                    else:
                        link(dve.tensor_tensor(e_b, eps, over_blocks(B_F), ALU.add))
                        dve.sem_inc(e_taken, 1)
                        link(dve.tensor_tensor(e_b, e_b, x_b, ALU.add))
                        layernorm(j, s, k, j + (2 * NCH + 1))
                        dve.tensor_tensor(by_block(oc[:, s, :]), by_block(e_c[:, :]),
                                          over_features(e_std[:, :]), ALU.mult).then_inc(out_ready, 1)

                def sum_near(j, s):
                    for b in range(BPC):
                        r = b % 2
                        dve.wait_ge(rows_gathered[r], j * (2 * 16 * K_NEAR) + 16 * K_NEAR * (b // 2 + 1))
                        u = near_u[:, s * BPC + b, :]
                        w0 = (j * BPC + b) * K_NEAR
                        link(dve.tensor_scalar(u, gat[:, r, 0, :], near_s[:, ds(w0, 1)], None, ALU.mult))
                        for n in range(1, K_NEAR):
                            ins = dve.scalar_tensor_tensor(u, gat[:, r, n, :], near_s[:, ds(w0 + n, 1)], u,
                                                           ALU.mult, ALU.add)
                            if n < K_NEAR - 1:
                                link(ins)
                        ins.then_inc(u_ready, 1)

                per = {K_AGG1: 11, K_AGG2: 9 + 12, K_HOP1: 4, K_HOP2: 11, K_FRM1: 2, K_FRM2: 7}[k]

                if k == K_AGG2:
                    sum_near(0, 0)
                    sum_near(1, 1)
                    epilogue(0, 0)
                    n0 = chain.base + chain.n
                    with dve.Fori(1, NCH // 2) as i:
                        chain.enter(i, 1, 2 * per)
                        sum_near(i * 2, 0)
                        epilogue(i * 2 - 1, 1)
                        sum_near(i * 2 + 1, 1)
                        epilogue(i * 2, 0)
                    chain.leave(NCH // 2 - 1)
                    epilogue(NCH - 1, 1)
                    dve.sem_inc(att_done, 1)
                elif k == K_FRM2:
                    epilogue(0, 0)
                    epilogue(1, 1)
                    with dve.Fori(1, NCH // 2) as i:
                        chain.enter(i, 1, 2 * per)
                        for s in range(2):
                            dve.wait_ge(out_stored[s], i * 16)
                            epilogue(i * 2 + s, s)
                    chain.leave(NCH // 2 - 1)
                else:
                    with dve.Fori(0, NCH // 2) as i:
                        chain.enter(i, 0, 2 * per)
                        for s in range(2):
                            epilogue(i * 2 + s, s)
                    chain.leave(NCH // 2)

            product(K_AGG1)

            def search(b, s):
                dve.wait_ge(keys_copied, b * NG + NG)
                apart(dve)
                link(dve.max(top8[:, s, :], key_rows[s]))
                apart(dve)
                dve.max_index(idx8[:, s, :], top8[:, s, :], key_rows[s]).then_inc(near_found, 1)
                dve.tensor_copy(near_key[:, ds(b * K_NEAR, K_NEAR)], top8[:, s, 0:K_NEAR])
                dve.wait_ge(near_found, b + 1)
                link(dve.tensor_copy(near_idx[:, ds(b * K_NEAR, K_NEAR)], idx8[:, s, 0:K_NEAR]))

            with dve.Fori(0, NB // 2) as i:
                chain.enter(i, 0, 4)
                search(i * 2, 0)
                search(i * 2 + 1, 1)
            chain.leave(NB // 2)

            nk = near_key[:, :].rearrange("p (b n) -> p b n", n=K_NEAR)
            ns = near_s[:, :].rearrange("p (b n) -> p b n", n=K_NEAR)
            link(dve.scalar_tensor_tensor(ns, nk, -2.0 / SPLIT ** 2, over_features(sqn[:, :], NB, K_NEAR), ALU.mult, ALU.add))
            dve.tensor_scalar(near_s[:, :], near_s[:, :], 0.0, 1e-10, ALU.max, ALU.add).then_inc(d_near, 1)
            dve.wait_ge(s_near, 2)
            link(dve.tensor_reduce(rdeg2[:, :], ns, X_AX, ALU.add))
            dve.tensor_tensor(rdeg2[:, :], rdeg2[:, :], rowsum[:, :], ALU.add).then_inc(deg2_ready, 1)
            link(dve.tensor_scalar(near_s[:, :], near_s[:, :], SPLIT ** 2, None, ALU.mult))
            dve.wait_ge(deg2_root, 1)
            link(dve.reciprocal(rdeg2[:, :], deg[:, :]))
            scale_x(K_AGG2, rdeg2)

            product(K_AGG2)

            khi = maskb[:, 0, 0:2 * CH].bitcast(f16).rearrange("p (r n) -> p r n", r=2)

            def stage_chunk(j, s):
                dve.tensor_copy(oc[:, s, :], xres[:, ds(j * CH, CH)]).then_inc(kx_staged, 1)

            def kv_chunk(j, s, nxt):
                if nxt:
                    dve.wait_ge(kx_turned, j + 1)
                    stage_chunk(j + 2, s)
                dve.wait_ge(v_ready, j + 1)
                dve.tensor_tensor(by_block(V[:, ds(j * CH, CH)]), by_block(bank(6 + s)), over_blocks(B_V),
                                  ALU.add).then_inc(v_taken, 1)
                for h in range(HEADS):
                    dve.wait_ge(k_halved, j * HEADS + (h + 1))
                    dve.scalar_tensor_tensor(kst[:, h, ds(j * CH, CH)], khi[:, h % 2, :], lo_k[:, :],
                                             pts[h % 2], ALU.mult, ALU.add).then_inc(k_stacked, 1)

            stage_chunk(0, 0)
            stage_chunk(1, 1)
            with dve.Fori(0, NCH // 2 - 1) as i:
                kv_chunk(i * 2, 0, True)
                kv_chunk(i * 2 + 1, 1, True)
            kv_chunk(NCH - 2, 0, False)
            kv_chunk(NCH - 1, 1, False)
            dve.wait_ge(k_stacked, NCH * HEADS)

            def take_scores(v, s, h, t):
                dve.wait_ge(s_ready, v * STEPS + (t + 1))
                apart(dve)
                dve.tensor_tensor_reduce(
                    out=att_w[h][:, t * CH:(t + 1) * CH], in0=bank(t % S_RING),
                    in1=maskb[:, s, t * CH:(t + 1) * CH], scale=1.0, scalar=-3.0e38, op0=ALU.add,
                    op1=ALU.max, accum_out=mx_part[:, h % 2, t:t + 1]).then_inc(s_taken, 1)

            def row_max(v, s, h):
                dve.wait_ge(s_taken, v * STEPS + STEPS)
                mark(dve.tensor_reduce(mx4[:, s, h:h + 1], mx_part[:, h % 2, :], X_AX, ALU.max))

            def bias_exp(h, s):
                settle()
                dve.tensor_scalar(nbias[:, h:h + 1], mx4[:, s, h:h + 1], -ATT_SCALE / SPLIT ** 2, None,
                                  ALU.mult).then_inc(max_ready, 1)

            def stack_queries(b, s, pr):
                dve.wait_ge(q_halved, b * 2 + (pr + 1))
                dve.scalar_tensor_tensor(qst[:, s, 2 * pr:2 * pr + 2, :], q_hi[:, :, :], lo_q[:, :],
                                         q_full[:, :, :], ALU.mult, ALU.add).then_inc(q_stacked, 1)

            def take_xr(b, m):
                dve.wait_ge(q_ready, b * 2 + 1)
                dve.tensor_tensor(xr_new[:, :], bank(m)[:, 0:F], B_S, ALU.add).then_inc(xr_taken, 1)

            def keep_xr(b, s):
                dve.wait_ge(xr_taken, b + 1)
                mark(dve.tensor_copy(cat[:, s, F:2 * F], xr_new[:, :]))

            def copy_turned(v, t):
                dve.wait_ge(pt_ready, v * STEPS + (t + 1))
                dve.tensor_copy(pts[t % T_RING], bank(S_RING + t % T_RING)).then_inc(pt_by_dve, 1)

            def weigh_heads(b, s, part):
                if part == 0:
                    dve.wait_ge(exp_done, b * (HEADS * N // EXP) + (HEADS * N // EXP))
                    mark(dve.tensor_reduce(den4[:, :], den[:, s, :, :], X_AX, ALU.add))
                elif part == 1:
                    settle()
                    mark(dve.reciprocal(rden4[:, :], den4[:, :]))
                else:
                    settle()
                    mark(dve.scalar_tensor_tensor(rden4[:, :], mx4[:, s, :], MASKED / 10, rden4[:, :],
                                                  ALU.is_gt, ALU.mult))

            def normalise(b, s, m, part):
                if part == 0:
                    dve.wait_ge(o_turned, b + 1)
                    mark(dve.tensor_reduce(o_sum[:, :].rearrange("p (h c) -> p h c", h=HEADS),
                                           bank(m).rearrange("p (h r c) -> p h c r", h=HEADS, r=4),
                                           X_AX, ALU.add))
                elif part == 1:
                    settle()
                    mark(dve.tensor_tensor(cat[:, s, 0:F].rearrange("p (c h) -> p h c", h=HEADS),
                                           o_sum[:, :].rearrange("p (h c) -> p h c", h=HEADS),
                                           over_features(rden4[:, :], HEADS, C), ALU.mult))
                elif part == 2:
                    settle()
                    mark(dve.tensor_tensor(cat[:, s, 2 * F:3 * F], cat[:, s, 0:F], cat[:, s, F:2 * F],
                                           ALU.subtract))
                else:
                    settle()
                    apart(dve)
                    dve.tensor_tensor_reduce(out=cat_t[:, :], in0=cat[:, s, :], in1=wb_sb[:, :],
                                             scale=1.0, scalar=0.0, op0=ALU.mult, op1=ALU.add,
                                             accum_out=gate_z[:, :]).then_inc(gate_in, 1)

            def blend(b, s, part):
                if part == 0:
                    dve.wait_ge(gate_exp, b + 1)
                    mark(dve.tensor_scalar(gate_b[:, :], gate_e[:, :], -1.0, -1.0, ALU.mult, ALU.add))
                elif part == 1:
                    settle()
                    mark(dve.reciprocal(gate_b[:, :], gate_b[:, :]))
                elif part == 2:
                    settle()
                    mark(dve.scalar_tensor_tensor(att[:, :], cat[:, s, 2 * F:3 * F], gate_b[:, :],
                                                  cat[:, s, 0:F], ALU.mult, ALU.add))
                elif part == 3:
                    settle()
                    mark(dve.tensor_tensor(att[:, :], att[:, :], xres[:, ds(b * F, F)], ALU.add))
                elif part == 4:
                    settle()
                    mark(dve.bn_stats(st6[:, :], att[:, :]))
                elif part == 5:
                    settle()
                    apart(dve)
                    dve.tensor_copy(xres[:, ds(b * F, F)], att[:, :]).then_inc(att_kept, 1)
                    apart(dve)
                    mark(dve.bn_aggr(mv[:, :], st6[:, :]))
                else:
                    settle()
                    dve.wait_ge(att_kept, b + 1)
                    apart(dve)
                    dve.tensor_copy(mv_all[:, ds(b, 1), :], mv[:, :].unsqueeze(1)).then_inc(avar_ready, 1)

            def finish():
                dve.wait_ge(avar_ready, NB)
                dve.wait_ge(astd_ready, 1)
                link(dve.reciprocal(a_rstd[:, :], a_std[:, :]))
                for b in range(NB):
                    dve.tensor_scalar(xres[:, b * F:(b + 1) * F], xres[:, b * F:(b + 1) * F],
                                      mv_all[:, b, 0:1], a_rstd[:, b:b + 1],
                                      ALU.subtract, ALU.mult).then_inc(att_done, 1)

            def phase(b, s, h, prev, nxt):
                v = b * HEADS + h
                for t in range(STEPS):
                    if t in DVE_STEPS:
                        copy_turned(v, t)
                    if h < 2 or nxt:
                        if h == 2 and t == 0:
                            dve.wait_ge(mask_ready, b + 2)
                        take_scores(v + 2, s if h < 2 else 1 - s, (h + 2) % HEADS, t)
                    if h < 3 or nxt:
                        if t == 0:
                            row_max(v + 1, s if h < 3 else 1 - s, (h + 1) % HEADS)
                        if t == 1:
                            bias_exp((h + 1) % HEADS, s if h < 3 else 1 - s)
                    if h == 0 and prev and t < 3:
                        weigh_heads(b - 1, 1 - s, t)
                    if h == 1 and nxt:
                        if t == 1:
                            take_xr(b + 1, 7 - s)
                        if t in (4, 7):
                            stack_queries(b + 1, 1 - s, t // 5)
                    if h == 2 and prev and 2 <= t < 6:
                        normalise(b - 1, 1 - s, 7 - s, t - 2)
                    if h == 3 and prev:
                        if 1 <= t:
                            blend(b - 1, 1 - s, t - 1)
                    if h == 3 and nxt and t == 6:
                        keep_xr(b + 1, 1 - s)

            dve.wait_ge(mask_rows_in, 16)
            dve.tensor_scalar(maskb[:, 0, :], adj_rows[:, :], 0.0, MASKED, ALU.is_equal, ALU.mult)\
                .then_inc(mask_ready, 1)
            take_xr(0, 7)
            stack_queries(0, 0, 0)
            stack_queries(0, 0, 1)
            keep_xr(0, 0)
            dve.wait_ge(mask_ready, 1)
            for v in range(2):
                for t in range(STEPS):
                    take_scores(v, 0, v, t)
                if v == 0:
                    row_max(0, 0, 0)
                    bias_exp(0, 0)
            for s in range(2):
                for h in range(HEADS):
                    phase(s, s, h, s > 0, True)
            with dve.Fori(1, NB // 2 - 1) as i:
                chain.enter(i, 1, 2 * (4 + 3 + 3 + 6 + 1))
                for s in range(2):
                    for h in range(HEADS):
                        phase(i * 2 + s, s, h, True, True)
            chain.leave(NB // 2 - 2)
            for s in range(2):
                for h in range(HEADS):
                    phase(NB - 2 + s, s, h, True, s == 0)
            settle()
            for part in range(3):
                weigh_heads(NB - 1, 1, part)
            for part in range(4):
                normalise(NB - 1, 1, 7, part)
            for part in range(7):
                blend(NB - 1, 1, part)
            finish()
            for j in range(NCH):
                dve.wait_ge(att_done, (j + 1) * BPC + 1)
                split(K_HOP1, j, xres[:, j * CH:(j + 1) * CH])

            for k in (K_HOP1, K_HOP2, K_FRM1, K_FRM2):
                product(k)


_INS = ['x', 'adj', 'L0_gnn_W1', 'L0_gnn_b1', 'L0_gnn_W2', 'L0_gnn_b2', 'L1_gnn_Wq', 'L1_gnn_bq',
        'L1_gnn_Wk', 'L1_gnn_bk', 'L1_gnn_Wv', 'L1_gnn_bv', 'L1_gnn_Ws', 'L1_gnn_bs', 'L1_gnn_Wb',
        'L2_gnn_W', 'L2_gnn_b', 'L3_gnn_d_list', 'L3_gnn_weight', 'L3_gnn_filt', 'L3_gnn_bias']
_OUTS = [((4096, 128), 'float32')]


def kernel(**inputs):
    import numpy as _np
    import concourse.bacc as _bacc
    from concourse import mybir as _mybir
    from concourse.bass_utils import run_bass_kernel_spmd as _run

    nc = _bacc.Bacc("TRN2", target_bir_lowering=False, num_devices=1)
    arrays, args = {}, []
    for name in _INS:
        a = _np.ascontiguousarray(inputs[name])
        arrays[f"in_{name}_dram"] = a
        args.append(nc.dram_tensor(f"in_{name}_dram", a.shape, _mybir.dt.from_np(a.dtype), kind="ExternalInput").ap())
    for i, (shape, dtype) in enumerate(_OUTS):
        dt = _mybir.dt.from_np(_np.dtype(dtype))
        args.append(nc.dram_tensor(f"out_{i}_dram", shape, dt, kind="ExternalOutput").ap())
    graph_layers_kernel(nc, *args)
    r = _run(nc, [arrays], core_ids=[0])
    got = tuple(r.results[0][f"out_{i}_dram"] for i in range(len(_OUTS)))
    return got[0]
```

```python
from contextlib import ExitStack

import concourse.bass as bass
from concourse import mybir
from concourse.alu_op_type import AluOpType as ALU

ds = bass.ds
N, F, P = 4096, 128, 128
NB = N // P
CH = 512
BPC = CH // P
NCH = N // CH
TQ = 4
TC = NB // TQ
K_NEAR = 4
HEADS, C = 4, 32
JD = 3
LN_EPS = 1e-5
SPLIT = 64.0
MASKED = -1e30
ATT_SCALE = 1.0 / float(C) ** 0.5
GRP = 1024
NG = N // GRP
EXP = 1024
STEPS = NB // 4
DVE_STEPS = [2, 5]
ACT_STEPS = [t for t in range(STEPS) if t not in DVE_STEPS]
EXP_STEPS = [2, 4, 6]
S_RING = 2
T_RING = 4
LAG = 3

K_AGG1, K_AGG2, K_HOP1, K_HOP2, K_FRM1, K_FRM2 = range(6)


class Count:

    def __init__(self, eng, sem):
        self.eng, self.sem, self.base, self.turn, self.n = eng, sem, 0, None, 0

    def link(self, ins):
        self.n += 1
        ins.then_inc(self.sem, 1)
        self.eng.wait_ge(self.sem, self.value())

    def mark(self, ins):
        self.n += 1
        return ins.then_inc(self.sem, 1)

    def settle(self):
        self.eng.wait_ge(self.sem, self.value())

    def value(self):
        if self.turn is None:
            return self.base + self.n
        i, first, per_turn = self.turn
        return i * per_turn + (self.base + self.n - first * per_turn)

    def enter(self, i, first, per_turn):
        self.base, self.n, self.turn = self.base + self.n, 0, (i, first, per_turn)

    def leave(self, turns):
        _, _, per_turn = self.turn
        assert self.n == per_turn, (self.n, per_turn)
        self.base, self.n, self.turn = self.base + turns * per_turn, 0, None


def graph_layers_kernel(nc, x, adj, W1, b1, W2, b2, Wq, bq, Wk, bk, Wv, bv, Ws, bs, Wb, Wh, bh,
                        d_list, Wf, filt, bf, out):
    f32, bf16, f16, u32 = mybir.dt.float32, mybir.dt.bfloat16, mybir.dt.float16, mybir.dt.uint32
    ACT = mybir.ActivationFunctionType
    X_AX = mybir.AxisListType.X

    adjT = nc.dram_tensor("adjT_tiles", (NCH * TQ * P, 2 * TC * CH), f16).ap()
    gtab = nc.dram_tensor("scaled_x_rows", (N, F), f32).ap()

    ctx = ExitStack()
    with ctx:
        def sb(name, shape, dt=f32):
            return ctx.enter_context(nc.sbuf_tensor(name, shape, dt))

        def sem(name):
            return ctx.enter_context(nc.semaphore(name))

        RES = TQ - 1
        xres = sb("xres", [P, NB * F])
        XA = sb("XA", [P, NB * F])
        tiles = sb("tiles", [P, 4, TC * CH])
        R2 = sb("R2", [P, 2 * N])
        adj_rows = sb("adj_rows", [P, N])
        maskb = sb("maskb", [P, 2, N], bf16)
        yT_sb = sb("yT_sb", [P, 2, CH])
        ident = sb("ident", [P, P])
        w_sb = sb("w_sb", [P, 8, F])
        tiles16 = tiles[:, :, :].rearrange("p s n -> p (s n)").bitcast(f16)\
            .rearrange("p (s a c n) -> p s a c n", s=4, a=2, c=TC)
        wq4 = sb("wq4", [P, HEADS, 4, C])
        wk4 = sb("wk4", [P, HEADS, 4, C])
        bq4 = sb("bq4", [P, HEADS])
        bk4 = sb("bk4", [P, HEADS])
        bq4_lo = sb("bq4_lo", [P, HEADS])
        bk4_lo = sb("bk4_lo", [P, HEADS])
        bias_sb = sb("bias_sb", [P, 6, F])
        wb_sb = sb("wb_sb", [P, 3 * F])
        eps_ln = sb("eps_ln", [P, 1])
        zero1 = sb("zero1", [P, 1])
        neg_half = sb("neg_half", [P, JD])
        lo_q = sb("lo_q", [P, 1])
        lo_k = sb("lo_k", [P, 1])
        frm = adj_rows[0:NB, 0:2 * JD * P].rearrange("b (a i p) -> b a i p", a=2, i=JD)
        frm_t = adj_rows[0:NB, 2 * JD * P:3 * JD * P].rearrange("b (i p) -> b i p", i=JD)
        fscale = sb("fscale", [P, NB])
        rs_part = sb("rs_part", [P, TQ, NB])
        rowsum = sb("rowsum", [P, NB])
        deg = sb("deg", [P, NB])
        rdeg = sb("rdeg", [P, NB])
        zc = adj_rows[:, 0:2 * CH].rearrange("p (s n) -> p s n", s=2)
        zsq = adj_rows[:, 2 * CH:3 * CH]
        sqn = sb("sqn", [P, NB])
        sqz = adj_rows[:, 3 * CH:5 * CH].rearrange("p (s n) -> p s n", s=2)
        sq_h = sb("sq_h", [JD, CH], bf16)
        sq_m = sb("sq_m", [JD, CH], bf16)
        sq_r = adj_rows[0:JD, 5 * CH:6 * CH]
        sq_c = adj_rows[0:JD, 6 * CH:7 * CH]
        sq3 = maskb[0:JD, 0, :]
        ones3 = sb("ones3", [JD, P], bf16)
        top8 = sb("top8", [P, 2, 8])
        idx8 = sb("idx8", [P, 2, 8], u32)
        near_key = sb("near_key", [P, NB * K_NEAR])
        near_idx = sb("near_idx", [P, NB * K_NEAR], u32)
        near_s = sb("near_s", [P, NB * K_NEAR])
        near_t = sb("near_t", [P, NB * K_NEAR])
        rdeg2 = sb("rdeg2", [P, NB])
        idx_st = sb("idx_st", [P, BPC, K_NEAR], u32)
        gat = adj_rows[:, 0:4 * CH].rearrange("p (s n f) -> p s n f", s=BPC, n=K_NEAR)
        near_u = adj_rows[:, 4 * CH:6 * CH].rearrange("p (b f) -> p b f", f=F)
        e_tx = sb("e_tx", [P, 2 * CH])
        e_t, e_exp = e_tx[:, 0:CH], e_tx[:, CH:2 * CH]
        e_cq = sb("e_cq", [P, 2 * CH])
        e_c, e_q = e_cq[:, 0:CH], e_cq[:, CH:2 * CH]
        e_sum = sb("e_sum", [P, BPC])
        e_var = sb("e_var", [P, BPC])
        e_std = sb("e_std", [P, BPC])
        oc = sb("oc", [P, 2, CH])
        xst = sb("xst", [P, 2, F])
        xTst = sb("xTst", [P, 2, P])
        q_hi = sb("q_hi", [P, 2, P], f16)
        qst = sb("qst", [P, 2, HEADS, P], f16)
        pts = [e_c, e_q, yT_sb[:, 0, :], yT_sb[:, 1, :]]
        mx_part = sb("mx_part", [P, 2, STEPS])
        mx4 = sb("mx4", [P, 2, HEADS])
        nbias = sb("nbias", [P, HEADS])
        den = sb("den", [P, 2, HEADS, N // EXP])
        den4 = sb("den4", [P, HEADS])
        rden4 = sb("rden4", [P, HEADS])
        oTs = sb("oTs", [P, HEADS, P])
        cat = e_tx[:, 0:6 * F].rearrange("p (s n) -> p s n", s=2)
        cat_t = oc[:, 0, 0:3 * F]
        gate_z = sb("gate_z", [P, 1])
        gate_e = sb("gate_e", [P, 1])
        gate_b = sb("gate_b", [P, 1])
        att = sb("att", [P, F])
        xr_new = oc[:, 1, 0:F]
        o_sum = oc[:, 1, F:2 * F]
        st6 = sb("st6", [P, 6])
        mv = sb("mv", [P, 2])
        mv_all = sb("mv_all", [P, NB, 2])
        a_std = sb("a_std", [P, NB])
        a_rstd = sb("a_rstd", [P, NB])

        PS = ctx.enter_context(nc.psum_tensor("PS", [P, 8 * CH], f32))

        def bank(b):
            return PS[:, b * CH:(b + 1) * CH]

        R2h = R2[:, :].bitcast(f16)
        zT = [R2h[:, 0:N], R2h[:, N:2 * N]]
        scaled_x = R2[:, N:2 * N]
        XA16 = XA[:, :].bitcast(f16)
        XB16 = maskb[:, :, :].rearrange("p s n -> p (s n)").bitcast(f16)
        op_A = [XA16[:, 0:N], XA16[:, N:2 * N]]
        op_B = [XB16[:, 0:N], XB16[:, N:2 * N]]
        kept = [t.bitcast(f16).rearrange("p (a c n) -> p a c n", a=2, c=TC)
                for t in (adj_rows[:, :], R2[:, 0:N], R2[:, N:2 * N])]
        part_y = maskb[:, :, :].rearrange("p s n -> p (s n)").bitcast(f32)
        kst = R2[:, :].bitcast(f16).rearrange("p (h n) -> p h n", h=HEADS)
        key_rows = [tiles[:, 2, :], tiles[:, 3, :]]
        att_w = [tiles[:, h, :] for h in range(HEADS)]
        V = XA
        W_1, W_2, W_H, W_F, W_Q, W_K, W_V, W_S = (w_sb[:, i, :] for i in range(8))
        B_1, B_2, B_H, B_F, B_V, B_S = (bias_sb[:, i, :] for i in range(6))
        weight_of = [W_1, W_2, W_H, W_H, W_F, None]
        operand_of = [op_A, op_A, op_A, op_B, op_A, op_B]

        def by_block(ap):
            return ap.rearrange("p (b f) -> p b f", f=F)

        def over_blocks(vec):
            return vec.unsqueeze(1).to_broadcast([P, BPC, F])

        def over_features(vec, n=BPC, f=F):
            return vec.unsqueeze(2).to_broadcast([P, n, f])

        consts_in = sem("consts_in")
        x_in = sem("x_in")
        made = sem("made")
        fs_summed = sem("fs_summed")
        fs_turned = sem("fs_turned")
        rows_in = [sem(f"rows_in{i}") for i in range(2)]
        bank_turned = sem("bank_turned")
        bank_copied = sem("bank_copied")
        bank_split = sem("bank_split")
        rows_summed = sem("rows_summed")
        adjT_out = [sem(f"adjT_out{i}") for i in range(2)]
        deg_ready = sem("deg_ready")
        deg_root = sem("deg_root")
        part_used = sem("part_used")
        part_kept = sem("part_kept")
        x_ready = [sem(f"x_ready{k}") for k in range(6)]
        tile_in = [sem(f"tile_in{q}") for q in range(TQ)]
        tile_used = [sem(f"tile_used{q}") for q in range(TQ)]
        kept_in = [sem(f"kept_in{q}") for q in range(RES)]
        y_ready = sem("y_ready")
        y_copied = sem("y_copied")
        e_ready = sem("e_ready")
        e_taken = sem("e_taken")
        z_ready = sem("z_ready")
        zT_turned = sem("zT_turned")
        zT_ready = sem("zT_ready")
        zT_split = sem("zT_split")
        sq_ready = sem("sq_ready")
        sq_split = sem("sq_split")
        keys_ready = sem("keys_ready")
        keys_copied = sem("keys_copied")
        near_found = sem("near_found")
        d_near = sem("d_near")
        s_near = sem("s_near")
        x_scaled = sem("x_scaled")
        deg2_ready = sem("deg2_ready")
        deg2_root = sem("deg2_root")
        table_out = sem("table_out")
        idx_staged = sem("idx_staged")
        rows_gathered = [sem(f"rows_gathered{i}") for i in range(BPC)]
        u_ready = sem("u_ready")
        var_ready = sem("var_ready")
        std_ready = sem("std_ready")
        swish_in = sem("swish_in")
        swish_exp = sem("swish_exp")
        out_ready = sem("out_ready")
        out_stored = [sem(f"out_stored{i}") for i in range(2)]
        kx_staged = sem("kx_staged")
        kx_turned = sem("kx_turned")
        kx_copied = sem("kx_copied")
        v_ready = sem("v_ready")
        v_taken = sem("v_taken")
        k_ready = sem("k_ready")
        k_halved = sem("k_halved")
        k_stacked = sem("k_stacked")
        mask_rows_in = sem("mask_rows_in")
        mask_ready = sem("mask_ready")
        xst_ready = sem("xst_ready")
        xT_turned = sem("xT_turned")
        xT_copied = sem("xT_copied")
        xr_taken = sem("xr_taken")
        q_ready = sem("q_ready")
        q_halved = sem("q_halved")
        q_stacked = sem("q_stacked")
        s_ready = sem("s_ready")
        s_taken = sem("s_taken")
        max_ready = sem("max_ready")
        exp_done = sem("exp_done")
        pt_ready = sem("pt_ready")
        pt_by_act = sem("pt_by_act")
        pt_by_dve = sem("pt_by_dve")
        o_ready = sem("o_ready")
        o_copied = sem("o_copied")
        o_turned = sem("o_turned")
        gate_in = sem("gate_in")
        gate_exp = sem("gate_exp")
        avar_ready = sem("avar_ready")
        astd_ready = sem("astd_ready")
        att_done = sem("att_done")
        att_kept = sem("att_kept")
        passed = sem("passed")
        act_link = sem("act_link")
        dve_link = sem("dve_link")

        first_tiles = [(j, q) for j in range(NCH) for q in range(j // 2, TQ)]
        FIRST_LOADS = len(first_tiles) // TQ
        first_uses = [sum(q != RES for u, (j, q) in enumerate(first_tiles) if u % TQ == slot)
                      for slot in range(TQ)]

        def uses_before(u):
            return sum(q != RES for v, (j, q) in enumerate(first_tiles[:u]) if v % TQ == u % TQ)

        def later_loads(k, q):
            n = NCH * (k - K_AGG2)
            return n if k <= K_HOP1 or q >= RES else n - (k - K_HOP1)

        def parts_before(j, p):
            return (j - 2 * p) * p + p * (p - 1)

        def is_kept(k, q):
            return k >= K_HOP1 and q < RES

        N_CONSTS = 0
        consts = []

        for i, w in enumerate((W1, W2, Wh, Wf, Wq, Wk, Wv, Ws)):
            consts.append((w_sb[:, i, :], w))
        for i, b in enumerate((b1, b2, bh, bf, bv, bs)):
            consts.append((bias_sb[:, i, :], b.rearrange("(a n) -> a n", a=1).to_broadcast([P, F])))
        consts.append((wb_sb[:, :], Wb.rearrange("n a -> a n").to_broadcast([P, 3 * F])))
        for r in range(4):
            consts.append((bq4[C * r:C * (r + 1), :], bq.rearrange("(h c) -> c h", c=C)))
            consts.append((bk4[C * r:C * (r + 1), :], bk.rearrange("(h c) -> c h", c=C)))
        consts.append((frm[:, 0, :, :], d_list.rearrange("i (b p) -> b i p", p=P)))
        consts.append((frm[:, 1, :, :], filt.rearrange("i (b p) -> b i p", p=P)))
        N_CONSTS = 16 * len(consts)

        N_MADE = 14

        def apart(eng):
            eng.sem_inc(passed, 1)

        block = ctx.enter_context(nc.Block())

        @block.sync
        def _(sp):
            def load_rows(j, q):
                src = adj[ds(j * CH, CH), q * TC * P:(q + 1) * TC * P]
                sp.dma_start(tiles[:, q % 2, :].rearrange("p (b m) -> p b m", b=BPC),
                             src.rearrange("(b p) m -> p b m", p=P)).then_inc(rows_in[q % 2], 16)

            for q in range(TQ):
                if q >= 2:
                    sp.wait_ge(bank_turned, (q - 1) * TC)
                    sp.wait_ge(rows_summed, q - 1)
                load_rows(0, q)
                if q == 0:
                    with nc.allow_non_contiguous_dma(reason="biases by partition, once"):
                        for dst, src in consts[0::2]:
                            sp.dma_start(dst, src).then_inc(consts_in, 16)
                if q == 1:
                    sp.dma_start(by_block(xres[:, :]), x.rearrange("(b p) f -> p b f", p=P)).then_inc(x_in, 16)
            with sp.Fori(1, NCH) as j:
                for q in range(TQ):
                    sp.wait_ge(bank_turned, j * (TQ * TC) + (q - 1) * TC)
                    apart(sp)
                    sp.wait_ge(rows_summed, j * TQ + (q - 1))
                    apart(sp)
                    load_rows(j, q)

            def load_tile(j, q):
                sp.dma_start(tiles16[:, q, :, :, :].rearrange("p a c n -> p (a c n)"),
                             adjT[ds((j * TQ + q) * P, P), :]).then_inc(tile_in[q], 16)

            def load_first(u):
                j, q = first_tiles[u]
                if u >= TQ:
                    j_last, q_last = first_tiles[u - TQ]
                    if q_last == RES:
                        sp.wait_ge(y_ready, j_last + 1)
                    else:
                        sp.wait_ge(tile_used[u % TQ], uses_before(u))
                sp.dma_start(tiles16[:, u % TQ, :, :, :].rearrange("p a c n -> p (a c n)"),
                             adjT[(j * TQ + q) * P:(j * TQ + q + 1) * P, :]).then_inc(tile_in[u % TQ], 16)

            def slot_free(k, j, q):
                if k == K_AGG2 and isinstance(j, int) and j == 0:
                    sp.wait_ge(y_ready, NCH)
                elif q < RES:
                    sp.wait_ge(tile_used[q], j + (first_uses[q] + later_loads(k, q) - (1 if is_kept(k, q) else 0)))
                elif k == K_AGG2:
                    sp.wait_ge(tile_used[q], j + first_uses[q])
                else:
                    sp.wait_ge(y_ready, j + NCH * k)

            def load_rest(k):
                with sp.Fori(1, NCH) as j:
                    for q in range(TQ):
                        slot_free(k, j, q)
                        apart(sp)
                        load_tile(j, q)

            sp.wait_ge(bank_turned, (NCH * TQ - 1) * TC)
            sp.wait_ge(rows_summed, NCH * TQ - 1)
            sp.wait_ge(adjT_out[0], 16)
            load_first(0)
            sp.wait_ge(bank_turned, NCH * TQ * TC)
            sp.wait_ge(rows_summed, NCH * TQ)
            sp.wait_ge(adjT_out[1], 16)
            load_first(1)
            sp.wait_ge(part_used, parts_before(NCH, NCH // 2))
            for i in range(2):
                sp.wait_ge(adjT_out[i], 16 * NCH * TQ // 2)
                load_first(2 + i)
            for u in range(TQ, len(first_tiles)):
                load_first(u)
            for q in range(TQ):
                slot_free(K_AGG2, 0, q)
                if q >= 2:
                    sp.wait_ge(near_found, NB)
                load_tile(0, q)
            load_rest(K_AGG2)

            def load_mask_rows(b):
                sp.dma_start(adj_rows[:, :], adj[ds(b * P, P), :]).then_inc(mask_rows_in, 16)

            sp.wait_ge(att_done, 1)
            load_mask_rows(0)
            with sp.Fori(1, NB) as b:
                sp.wait_ge(mask_ready, b)
                apart(sp)
                load_mask_rows(b)
            def keep_tile(q):
                sp.dma_start(kept[q].rearrange("p a c n -> p (a c n)"), adjT[q * P:(q + 1) * P, :])\
                    .then_inc(kept_in[q], 16)

            sp.wait_ge(mask_ready, NB)
            keep_tile(0)
            sp.wait_ge(s_ready, NB * HEADS * STEPS)
            keep_tile(1)
            keep_tile(2)
            sp.wait_ge(pt_ready, NB * HEADS * STEPS)
            for k in (K_HOP1, K_HOP2, K_FRM1, K_FRM2):
                slot_free(k, 0, RES)
                load_tile(0, RES)
                load_rest(k)
            for s in range(2):
                sp.wait_ge(out_stored[s], 16 * NCH // 2)

        @block.gpsimd
        def _(pool):
            pool.memset(ident[:, :], 0.0).then_inc(made, 1)
            pool.wait_ge(made, 1)
            pool.affine_select(out=ident[:, :], in_=ident[:, :], compare_op=ALU.not_equal, fill=1.0,
                               base=0, pattern=[[-1, P]], channel_multiplier=1).then_inc(made, 1)
            fills = [(eps_ln, LN_EPS), (zero1, 0.0), (neg_half, -0.5 * SPLIT ** 2), (ones3, 1.0)]
            fills += [(lo_q[C * r:C * (r + 1)], -1.0 if r >= 2 else 0.0) for r in range(4)]
            fills += [(lo_k[C * r:C * (r + 1)], -1.0 if r % 2 else 0.0) for r in range(4)]
            for n, (t, value) in enumerate(fills):
                pool.wait_ge(made, n + 2)
                pool.memset(t[:, :], value).then_inc(made, 1)

            pool.wait_ge(table_out, 16)

            def gather(b, s):
                pool.tensor_copy(idx_st[:, s, :], near_idx[:, ds(b * K_NEAR, K_NEAR)])\
                    .then_inc(idx_staged, 1)
                pool.wait_ge(idx_staged, b + 1)
                apart(pool)
                for n in range(K_NEAR):
                    pool.indirect_dma_start(
                        out=gat[:, s, n, :], out_offset=None, in_=gtab[:, :],
                        in_offset=bass.IndirectOffsetOnAxis(ap=idx_st[:, s, n:n + 1], axis=0),
                    ).then_inc(rows_gathered[s], 16)

            for s in range(BPC):
                gather(s, s)
            with pool.Fori(1, NCH) as i:
                for s in range(BPC):
                    b = i * BPC + s
                    pool.wait_ge(u_ready, b - 3)
                    pool.wait_ge(rows_gathered[s], i * (16 * K_NEAR))
                    gather(b, s)

            pool.wait_ge(k_stacked, NCH * HEADS)

            def stage_x(b, s):
                pool.tensor_copy(xst[:, s, :], xres[:, ds(b * F, F)]).then_inc(xst_ready, 1)

            def mask(b, s):
                pool.wait_ge(mask_rows_in, b * 16 + 16)
                apart(pool)
                pool.tensor_scalar(maskb[:, s, :], adj_rows[:, :], 0.0, MASKED, ALU.is_equal, ALU.mult)\
                    .then_inc(mask_ready, 1)

            for s in range(2):
                stage_x(s, s)
            mask(1, 1)
            with pool.Fori(1, NB // 2) as i:
                for s in range(2):
                    b = i * 2 + s
                    pool.wait_ge(xT_turned, b - 1)
                    stage_x(b, s)
                    pool.wait_ge(s_taken, (b - 1) * (HEADS * STEPS))
                    mask(b, s)

        @block.tensor
        def _(pe):
            pe.wait_ge(made, N_MADE)
            pe.wait_ge(fs_summed, 1)
            pe.transpose(PS[:, 0:NB], frm_t[:, 0, :], ident[0:NB, 0:NB]).then_inc(fs_turned, 1)
            pe.wait_ge(deg_ready, 1)

            TURN = 4

            def turn_tile(j, q, first):
                pe.wait_ge(rows_in[q % 2], j * 32 + 16 * (q // 2 + 1))
                for c in range(TC):
                    if not (first and c < TURN):
                        pe.wait_ge(bank_split, j * (TQ * TC) + (q * TC + c + 1 - TURN))
                    for b in range(BPC):
                        src = tiles[:, q % 2, (b * TC + c) * P:(b * TC + c + 1) * P]
                        ins = pe.transpose(bank(c % TURN)[:, b * P:(b + 1) * P], src, ident[:, :])
                    ins.then_inc(bank_turned, 1)

            def times_block(y, X, m, tile, c, start, stop):
                x_hi, x_lo = (part[:, m * F:(m + 1) * F] for part in X)
                t_hi, t_lo = tile[:, 0, c, :], tile[:, 1, c, :]
                pe.matmul(y, x_hi, t_hi, start=start, stop=False, skip_group_check=True)
                pe.matmul(y, x_hi, t_lo, start=False, stop=False, skip_group_check=True)
                return pe.matmul(y, x_lo, t_hi, start=False, stop=stop, skip_group_check=True)

            def add_part(j, p, q):
                pe.wait_ge(x_ready[K_AGG1], 2 * q + 2)
                pe.wait_ge(bank_split, j * (TQ * TC) + (q + 1) * TC)
                for c in range(TC):
                    ins = times_block(bank(7), op_A, q * TC + c, tiles16[:, 2 + q % 2], c,
                                      q == 0 and c == 0, q == p - 1 and c == TC - 1)
                ins.then_inc(part_used, 1)

            def turn_chunk(j, p, first):
                for q in range(TQ):
                    turn_tile(j, q, first and q == 0)
                    if 1 <= q <= p:
                        add_part(j, p, q - 1)
                if p > 0:
                    pe.wait_ge(part_kept, j - 1)

            turn_chunk(0, 0, True)
            turn_chunk(1, 0, False)
            for p in range(1, NCH // 2):
                with pe.Fori(2 * p, 2 * p + 2) as j:
                    turn_chunk(j, p, False)
            pe.wait_ge(bank_split, NCH * TQ * TC)

            def product(k):
                X = operand_of[k]
                first_c = NCH * k

                def quarter(j, s, q, head):
                    if head:
                        pe.wait_ge(x_ready[k], 2 * q + 2)
                    if head and is_kept(k, q):
                        pe.wait_ge(kept_in[q], 16)
                        tile = kept[q]
                    elif k == K_AGG1:
                        u = first_tiles.index((j, q))
                        pe.wait_ge(tile_in[u % TQ], 16 * (u // TQ + 1))
                        tile = tiles16[:, u % TQ]
                    else:
                        n = FIRST_LOADS + later_loads(k, q) + (0 if is_kept(k, q) else 1)
                        pe.wait_ge(tile_in[q], j * 16 + 16 * n)
                        tile = tiles16[:, q]
                    for c in range(TC):
                        m = q * TC + c
                        ins = times_block(bank(s), X, m, tile, c, m == 0,
                                          m == NB - 1 and k != K_AGG2)
                    if q == RES and k != K_AGG2:
                        ins.then_inc(y_ready, 1)
                    elif k == K_AGG1:
                        ins.then_inc(tile_used[u % TQ], 1)
                    elif not (head and is_kept(k, q)):
                        ins.then_inc(tile_used[q], 1)

                def weigh(j, s, fresh=False):
                    if not fresh:
                        pe.wait_ge(e_taken, j + first_c)
                    pe.wait_ge(y_copied, j + (first_c + 1))
                    for b in range(BPC):
                        y, e = yT_sb[:, s, b * P:(b + 1) * P], bank(2 + s)[:, b * P:(b + 1) * P]
                        if weight_of[k] is None:
                            ins = pe.transpose(e, y, ident[:, :])
                        else:
                            ins = pe.matmul(e, y, weight_of[k], start=True, stop=True)
                    ins.then_inc(e_ready, 1)

                def turn_z(j, s):
                    pe.wait_ge(z_ready, j + 1)
                    for b in range(BPC):
                        ins = pe.transpose(bank(4 + s)[:, b * P:(b + 1) * P],
                                           zc[:, s, b * P:(b + 1) * P], ident[:, :])
                    ins.then_inc(zT_turned, 1)

                def sum_z(j, s):
                    pe.wait_ge(zT_ready, j + 1)
                    pe.matmul(PS[0:JD, 6 * CH:7 * CH], neg_half[:, :], sqz[:, s, :], start=True,
                              stop=True).then_inc(sq_ready, 1)

                def add_near(j, s):
                    pe.wait_ge(u_ready, j * BPC + BPC)
                    for b in range(BPC):
                        ins = pe.matmul(bank(s)[:, b * P:(b + 1) * P], near_u[:, s * BPC + b, :],
                                        ident[:, :], start=False, stop=(b == BPC - 1),
                                        skip_group_check=True)
                    ins.then_inc(y_ready, 1)

                def chunk(j, s, head, after, head_next=False):
                    q0 = j // 2 if k == K_AGG1 else 0
                    if q0 > 0:
                        pe.matmul(bank(s), ident[:, :], part_y[:, j * CH:(j + 1) * CH], start=True,
                                  stop=False, skip_group_check=True)
                    if q0 == RES:
                        weigh(j - 1, 1 - s)
                    for q in range(q0, TQ):
                        quarter(j, s, q, head)
                        if after and q == q0 and q0 < RES and k != K_AGG2:
                            weigh(j - 1, 1 - s, k == K_AGG1 and head_next)
                        if after and q == max(2, q0) and k == K_AGG1:
                            turn_z(j - 1, 1 - s)
                        if after and q == 2 and k == K_AGG2:
                            add_near(j - 1, 1 - s)
                    if k == K_AGG2 and after:
                        weigh(j - 1, 1 - s)
                    if k == K_AGG1 and after:
                        sum_z(j - 1, 1 - s)

                chunk(0, 0, True, False)
                chunk(1, 1, False, True, True)
                if k == K_AGG1:
                    for j in range(2, NCH):
                        chunk(j, j % 2, False, True)
                else:
                    with pe.Fori(1, NCH // 2) as i:
                        chunk(i * 2, 0, False, True)
                        chunk(i * 2 + 1, 1, False, True)
                if k == K_AGG2:
                    add_near(NCH - 1, 1)
                weigh(NCH - 1, 1)
                if k == K_AGG1:
                    turn_z(NCH - 1, 1)
                    sum_z(NCH - 1, 1)

            product(K_AGG1)

            pe.wait_ge(sq_split, NCH)
            pe.wait_ge(zT_split, NCH)
            pe.wait_ge(e_taken, NCH)

            def keys(b, first):
                z_hi, z_lo = (part[:, ds(b * P, P)] for part in zT)
                for g in range(NG):
                    if not first:
                        pe.wait_ge(keys_copied, b * NG + (g + 1 - NG))
                    for h in range(GRP // CH):
                        o = g * GRP + h * CH
                        hi, lo = (part[:, o:o + CH] for part in zT)
                        pe.matmul(PS[:, o:o + CH], z_hi, hi, start=True, stop=False)
                        pe.matmul(PS[:, o:o + CH], z_hi, lo, start=False, stop=False)
                        pe.matmul(PS[:, o:o + CH], z_lo, hi, start=False, stop=False)
                        ins = pe.matmul(PS[:, o:o + CH], ones3[:, :], sq3[:, o:o + CH], start=False,
                                        stop=True)
                    ins.then_inc(keys_ready, 1)

            keys(0, True)
            with pe.Fori(1, NB) as b:
                keys(b, False)
            pe.wait_ge(keys_copied, NB * NG)

            product(K_AGG2)

            def turn_kx(j, s):
                pe.wait_ge(kx_staged, j + 1)
                for b in range(BPC):
                    ins = pe.transpose(bank(4 + s)[:, b * P:(b + 1) * P], oc[:, s, b * P:(b + 1) * P],
                                       ident[:, :])
                ins.then_inc(kx_turned, 1)

            def kv_chunk(j, s, first, nxt):
                pe.wait_ge(kx_copied, j + 1)
                if not first:
                    pe.wait_ge(v_taken, j - 1)
                for b in range(BPC):
                    ins = pe.matmul(bank(6 + s)[:, b * P:(b + 1) * P], yT_sb[:, s, b * P:(b + 1) * P],
                                    W_V, start=True, stop=True)
                ins.then_inc(v_ready, 1)
                if nxt:
                    turn_kx(j + 1, 1 - s)
                for h in range(HEADS):
                    if not (first and s == 0):
                        pe.wait_ge(k_stacked, j * HEADS + (h + 1 - HEADS))
                    elif h == 2:
                        pe.wait_ge(e_taken, 2 * NCH)
                    pe.matmul(bank(h), wk4[:, h, :, :].rearrange("p r c -> p (r c)"), yT_sb[:, s, :],
                              start=True, stop=True).then_inc(k_ready, 1)

            turn_kx(0, 0)
            kv_chunk(0, 0, True, True)
            kv_chunk(1, 1, True, True)
            with pe.Fori(1, NCH // 2 - 1) as i:
                kv_chunk(i * 2, 0, False, True)
                kv_chunk(i * 2 + 1, 1, False, True)
            kv_chunk(NCH - 2, 0, False, True)
            kv_chunk(NCH - 1, 1, False, False)
            pe.wait_ge(k_stacked, NCH * HEADS)
            pe.wait_ge(v_taken, NCH)

            def turn_x(b, s, m):
                pe.wait_ge(xst_ready, b + 1)
                pe.transpose(bank(m)[:, 0:P], xst[:, s, :], ident[:, :]).then_inc(xT_turned, 1)

            def queries(b, s, pr, m):
                if pr == 0:
                    pe.wait_ge(xT_copied, b + 1)
                    pe.matmul(bank(m)[:, 0:F], xTst[:, s, :], W_S, start=True, stop=True)
                else:
                    pe.wait_ge(q_stacked, b * 2 + 1)
                for hh in range(2):
                    o = P + hh * P
                    ins = pe.matmul(bank(m)[:, o:o + P],
                                    wq4[:, 2 * pr + hh, :, :].rearrange("p r c -> p (r c)"),
                                    xTst[:, s, :], start=True, stop=True)
                ins.then_inc(q_ready, 1)

            def scores(v, qb, s, h, t, first):
                if t == 0 and h % 2 == 0:
                    pe.wait_ge(q_stacked, qb * 2 + (h // 2 + 1))
                if not (first and t < S_RING):
                    pe.wait_ge(s_taken, v * STEPS + (t - S_RING + 1))
                pe.matmul(bank(t % S_RING), qst[:, s, h, :], kst[:, h, t * CH:(t + 1) * CH],
                          start=True, stop=True).then_inc(s_ready, 1)

            def turn_weights(v, h, t):
                if t % (EXP // CH) == 0:
                    pe.wait_ge(exp_done, v * (N // EXP) + (t // (EXP // CH) + 1))
                for r in range(4):
                    col = (4 * t + r) * P
                    ins = pe.transpose(bank(S_RING + t % T_RING)[:, r * P:(r + 1) * P],
                                       att_w[h][:, col:col + P], ident[:, :])
                ins.then_inc(pt_ready, 1)

            def weigh_values(b, s, v, h, t, prev, prevprev):
                if t in ACT_STEPS:
                    pe.wait_ge(pt_by_act, v * len(ACT_STEPS) + (ACT_STEPS.index(t) + 1))
                else:
                    pe.wait_ge(pt_by_dve, v * len(DVE_STEPS) + (DVE_STEPS.index(t) + 1))
                if t == 0 and h == 0 and prev:
                    if prevprev:
                        pe.wait_ge(gate_in, b - 1)
                    else:
                        pe.wait_ge(q_stacked, 4)
                for r in range(4):
                    m = 4 * t + r
                    ins = pe.matmul(bank(6 + s)[C * r:C * (r + 1), h * P:(h + 1) * P],
                                    V[:, m * F + C * h:m * F + C * (h + 1)],
                                    pts[t % T_RING][:, r * P:(r + 1) * P], start=(t == 0),
                                    stop=(t == STEPS - 1), skip_group_check=True,
                                    tile_position=(0, C * r))
                if t == STEPS - 1 and h == HEADS - 1:
                    ins.then_inc(o_ready, 1)

            def turn_out(b, m, asked):
                pe.wait_ge(o_copied, b + 1)
                if asked:
                    pe.wait_ge(q_stacked, b * 2 + 6)
                for h in range(HEADS):
                    ins = pe.transpose(bank(m)[:, h * P:(h + 1) * P], oTs[:, h, :], ident[:, :])
                ins.then_inc(o_turned, 1)

            def phase(b, s, h, prev, prevprev, nxt):
                v = b * HEADS + h
                for t in range(STEPS):
                    if t >= LAG:
                        weigh_values(b, s, v, h, t - LAG, prev, prevprev)
                    elif h > 0:
                        weigh_values(b, s, v - 1, h - 1, STEPS + t - LAG, prev, prevprev)
                    elif prev:
                        weigh_values(b - 1, 1 - s, v - 1, HEADS - 1, STEPS + t - LAG, True, True)
                    turn_weights(v, h, t)
                    if h < 2 or nxt:
                        scores(v + 2, b if h < 2 else b + 1, s if h < 2 else 1 - s, (h + 2) % HEADS,
                               t, False)
                    if nxt and h == 0 and t == 5:
                        if prev:
                            pe.wait_ge(o_copied, b)
                        else:
                            pe.wait_ge(q_stacked, 2)
                        turn_x(b + 1, 1 - s, 7 - s)
                    if nxt and h == 1 and t in (0, 5):
                        queries(b + 1, 1 - s, t // 5, 7 - s)
                    if prev and h == 2 and t == 1:
                        turn_out(b - 1, 7 - s, nxt)

            turn_x(0, 0, 7)
            queries(0, 0, 0, 7)
            queries(0, 0, 1, 7)
            for v in range(2):
                for t in range(STEPS):
                    scores(v, 0, 0, v, t, v == 0)
            for s in range(2):
                for h in range(HEADS):
                    phase(s, s, h, s > 0, False, True)
            with pe.Fori(1, NB // 2 - 1) as i:
                for s in range(2):
                    for h in range(HEADS):
                        phase(i * 2 + s, s, h, True, True, True)
            for s in range(2):
                for h in range(HEADS):
                    phase(NB - 2 + s, s, h, True, True, s == 0)
            for t in range(STEPS - LAG, STEPS):
                weigh_values(NB - 1, 1, NB * HEADS - 1, HEADS - 1, t, True, True)
            turn_out(NB - 1, 7, False)

            for k in (K_HOP1, K_HOP2, K_FRM1, K_FRM2):
                product(k)

        @block.scalar
        def _(act):
            chain = Count(act, act_link)
            with nc.allow_non_contiguous_dma(reason="biases by partition, once"):
                for dst, src in consts[1::2]:
                    act.dma_start(dst, src).then_inc(consts_in, 16)
            act.wait_ge(made, N_MADE)

            def store_tile(t, q):
                act.wait_ge(bank_split, t * TC + TC)
                act.dma_start(adjT[ds(t * P, P), :],
                              tiles16[:, 2 + q % 2, :, :, :].rearrange("p a c n -> p (a c n)"))\
                    .then_inc(adjT_out[q % 2], 16)

            def copy_tile(j, p, q, first, fresh):
                if not fresh:
                    act.wait_ge(adjT_out[q % 2], j * 32 + 16 * (q // 2))
                if q >= 2 and q - 2 < p:
                    act.wait_ge(part_used, parts_before(j, p) + (q - 1))
                elif q == 0 and p == NCH // 2 - 1:
                    act.wait_ge(part_used, parts_before(j, p))
                for c in range(TC):
                    act.wait_ge(bank_turned, j * (TQ * TC) + (q * TC + c + 1))
                    act.activation(tiles16[:, 2 + q % 2, 0, c, :], bank(c % 4), ACT.Copy, scale=SPLIT)\
                        .then_inc(bank_copied, 1)
                    if c == TC // 2 and not first:
                        store_tile(j * TQ + (q - 1), q - 1)

            def root_degrees(j):
                act.wait_ge(deg_ready, j + 2)
                act.activation(deg[:, ds(j * BPC, BPC)], rowsum[:, ds(j * BPC, BPC)], ACT.Sqrt,
                               bias=zero1[:, :]).then_inc(deg_root, 1)

            def copy_chunk(j, p, first):
                for q in range(TQ):
                    copy_tile(j, p, q, first and q < 1, first and q < 2)
                    if q == 0 and not first:
                        root_degrees(j - 1)
                    if q == p and p > 0:
                        act.wait_ge(part_used, parts_before(j, p) + p)
                        act.activation(part_y[:, ds(j * CH, CH)], bank(7), ACT.Copy).then_inc(part_kept, 1)

            copy_chunk(0, 0, True)
            copy_chunk(1, 0, False)
            for p in range(1, NCH // 2):
                with act.Fori(2 * p, 2 * p + 2) as j:
                    copy_chunk(j, p, False)
            store_tile(NCH * TQ - 1, TQ - 1)
            root_degrees(NCH - 1)

            def product(k):
                first_c = NCH * k

                def chunk(j, s, n_ln, n_sw):
                    act.wait_ge(y_ready, j + (first_c + 1))
                    act.activation(yT_sb[:, s, :], bank(s), ACT.Copy, scale=1.0 / SPLIT ** 2)\
                        .then_inc(y_copied, 1)
                    if k == K_AGG1:
                        act.wait_ge(zT_turned, j + 1)
                        act.activation(zT[0][:, ds(j * CH, CH)], bank(4 + s), ACT.Copy, scale=SPLIT)\
                            .then_inc(act_link, 1)
                        act.activation(sqz[:, s, :], bank(4 + s), ACT.Square, bias=zero1[:, :])\
                            .then_inc(act_link, 1)
                        act.wait_ge(act_link, j * 2 + 2)
                        act.sem_inc(zT_ready, 1)
                    if k in (K_HOP1, K_HOP2):
                        act.wait_ge(swish_in, j + (n_sw + 1))
                        act.activation(e_exp[:, :], e_t[:, :], ACT.Exp, scale=-1.0, bias=zero1[:, :])\
                            .then_inc(swish_exp, 1)
                    if k in (K_AGG2, K_HOP2, K_FRM2):
                        act.wait_ge(var_ready, j + (n_ln + 1))
                        act.activation(e_std[:, :], e_var[:, :], ACT.Sqrt, scale=1.0 / F,
                                       bias=eps_ln[:, :]).then_inc(std_ready, 1)
                    if k == K_FRM2:
                        act.wait_ge(out_ready, j + 1)
                        act.dma_start(out[ds(j * CH, CH), :].rearrange("(b p) f -> p b f", p=P),
                                      by_block(oc[:, s, :])).then_inc(out_stored[s], 16)

                n_ln = {K_AGG2: 0, K_HOP2: NCH, K_FRM2: 2 * NCH}.get(k)
                n_sw = {K_HOP1: 0, K_HOP2: NCH}.get(k)
                with act.Fori(0, NCH // 2) as i:
                    for s in range(2):
                        chunk(i * 2 + s, s, n_ln, n_sw)

            product(K_AGG1)

            def keys(b, s, first):
                if not first:
                    act.wait_ge(near_found, b - 1)
                for g in range(NG):
                    act.wait_ge(keys_ready, b * NG + (g + 1))
                    act.activation(key_rows[s][:, g * GRP:(g + 1) * GRP], PS[:, g * GRP:(g + 1) * GRP],
                                   ACT.Copy).then_inc(keys_copied, 1)

            act.wait_ge(y_ready, NCH)
            act.wait_ge(y_copied, NCH)
            keys(0, 0, True)
            keys(1, 1, True)
            with act.Fori(1, NB // 2) as i:
                keys(i * 2, 0, False)
                keys(i * 2 + 1, 1, False)

            act.wait_ge(d_near, 1)
            act.activation(near_t[:, :], near_s[:, :], ACT.Sqrt, bias=zero1[:, :]).then_inc(s_near, 1)
            act.wait_ge(s_near, 1)
            act.activation(near_s[:, :], near_t[:, :], ACT.Exp, scale=-0.5, bias=zero1[:, :])\
                .then_inc(s_near, 1)
            act.wait_ge(deg2_ready, 1)
            act.activation(deg[:, :], rdeg2[:, :], ACT.Sqrt, bias=zero1[:, :]).then_inc(deg2_root, 1)
            act.wait_ge(x_scaled, 1)
            act.dma_start(gtab.rearrange("(b p) f -> p b f", p=P), by_block(scaled_x))\
                .then_inc(table_out, 16)

            product(K_AGG2)

            khi = maskb[:, 0, 0:2 * CH].bitcast(f16).rearrange("p (r n) -> p r n", r=2)

            def copy_kx(j, s, fresh):
                act.wait_ge(kx_turned, j + 1)
                if not fresh:
                    act.wait_ge(k_ready, j * HEADS - HEADS)
                act.activation(yT_sb[:, s, :], bank(4 + s), ACT.Copy).then_inc(kx_copied, 1)

            def kv_chunk(j, s, first, nxt):
                if nxt:
                    copy_kx(j + 1, 1 - s, first and s == 0)
                for h in range(HEADS):
                    r = h % 2
                    act.wait_ge(k_ready, j * HEADS + (h + 1))
                    if not (first and s == 0 and h < 2):
                        act.wait_ge(k_stacked, j * HEADS + (h - 1))
                    act.activation(khi[:, r, :], bank(h), ACT.Identity, bias=bk4_lo[:, h:h + 1],
                                   scale=lo_k[:, 0:1]).then_inc(k_halved, 1)

            copy_kx(0, 0, True)
            kv_chunk(0, 0, True, True)
            kv_chunk(1, 1, True, True)
            with act.Fori(1, NCH // 2 - 1) as i:
                kv_chunk(i * 2, 0, False, True)
                kv_chunk(i * 2 + 1, 1, False, True)
            kv_chunk(NCH - 2, 0, False, True)
            kv_chunk(NCH - 1, 1, False, False)

            def copy_xT(b, s, m):
                act.wait_ge(xT_turned, b + 1)
                act.activation(xTst[:, s, :], bank(m)[:, 0:P], ACT.Copy).then_inc(xT_copied, 1)

            def halve_queries(b, s, pr, m, first):
                act.wait_ge(q_ready, b * 2 + (pr + 1))
                if pr == 0:
                    act.wait_ge(xr_taken, b + 1)
                if not (first and pr == 0):
                    act.wait_ge(q_stacked, b * 2 + pr)
                for hh in range(2):
                    h = 2 * pr + hh
                    ins = act.activation(q_hi[:, hh, :], bank(m)[:, P + hh * P:P + (hh + 1) * P],
                                         ACT.Identity, bias=bq4_lo[:, h:h + 1], scale=lo_q[:, 0:1])
                ins.then_inc(q_halved, 1)

            def exponentials(v, s, h, i):
                if i == 0:
                    act.wait_ge(max_ready, v + 1)
                w = att_w[h][:, i * EXP:(i + 1) * EXP]
                act.activation(w, w, ACT.Exp, bias=nbias[:, h:h + 1], scale=ATT_SCALE / SPLIT ** 2,
                               accum_out=den[:, s, h, i:i + 1]).then_inc(exp_done, 1)

            def copy_turned(v, t):
                act.wait_ge(pt_ready, v * STEPS + (t + 1))
                act.activation(pts[t % T_RING], bank(S_RING + t % T_RING), ACT.Copy).then_inc(pt_by_act, 1)

            def copy_out(b, m):
                act.wait_ge(o_ready, b + 1)
                act.activation(oTs[:, :, :].rearrange("p r n -> p (r n)"), bank(m), ACT.Copy)\
                    .then_inc(o_copied, 1)

            def gate(b):
                act.wait_ge(gate_in, b + 1)
                act.activation(gate_e[:, :], gate_z[:, :], ACT.Exp, scale=-1.0, bias=zero1[:, :])\
                    .then_inc(gate_exp, 1)

            def root(b0, b1):
                act.wait_ge(avar_ready, b1)
                act.activation(a_std[:, b0:b1], mv_all[:, b0:b1, 1], ACT.Sqrt, bias=eps_ln[:, :])\
                    .then_inc(astd_ready, 1)

            def phase(b, s, h, prev, nxt):
                v = b * HEADS + h
                for t in range(STEPS):
                    if prev and h == 0 and t == LAG:
                        copy_out(b - 1, 7 - s)
                    if t in ACT_STEPS:
                        copy_turned(v, t)
                    if nxt and h == 0 and t == 6:
                        copy_xT(b + 1, 1 - s, 7 - s)
                    if nxt and h == 1 and t % 4 == 2:
                        halve_queries(b + 1, 1 - s, t // 4, 7 - s, False)
                    if prev and h == 3 and t == 0:
                        gate(b - 1)
                    if t == 0:
                        exponentials(v, s, h, N // EXP - 1)
                    elif t in EXP_STEPS and (h < HEADS - 1 or nxt):
                        exponentials(v + 1, s if h < HEADS - 1 else 1 - s, (h + 1) % HEADS,
                                     EXP_STEPS.index(t))

            copy_xT(0, 0, 7)
            halve_queries(0, 0, 0, 7, True)
            halve_queries(0, 0, 1, 7, True)
            for i in range(N // EXP - 1):
                exponentials(0, 0, 0, i)
            for s in range(2):
                for h in range(HEADS):
                    phase(s, s, h, s > 0, True)
            with act.Fori(1, NB // 2 - 1) as i:
                for s in range(2):
                    for h in range(HEADS):
                        phase(i * 2 + s, s, h, True, True)
            for s in range(2):
                for h in range(HEADS):
                    phase(NB - 2 + s, s, h, True, s == 0)
            root(0, NB - BPC)
            copy_out(NB - 1, 7)
            gate(NB - 1)
            root(NB - BPC, NB)

            for k in (K_HOP1, K_HOP2, K_FRM1, K_FRM2):
                product(k)

        @block.vector
        def _(dve):
            chain = Count(dve, dve_link)
            link = chain.link
            mark, settle = chain.mark, chain.settle

            dve.wait_ge(consts_in, N_CONSTS)
            dve.wait_ge(made, N_MADE)
            link(dve.tensor_tensor(frm_t[:, :, :], frm[:, 0, :, :], frm[:, 1, :, :], ALU.mult))
            link(dve.tensor_tensor(frm_t[:, :, :], frm_t[:, :, :], frm[:, 0, :, :], ALU.mult))
            link(dve.tensor_tensor(frm_t[:, 0, :], frm_t[:, 0, :], frm_t[:, 1, :], ALU.add))
            dve.tensor_tensor(frm_t[:, 0, :], frm_t[:, 0, :], frm_t[:, 2, :], ALU.add).then_inc(fs_summed, 1)
            dve.wait_ge(fs_turned, 1)
            dve.tensor_copy(fscale[:, :], PS[:, 0:NB]).then_inc(deg_ready, 1)

            def split_tile(j, q):
                for c in range(TC):
                    dve.wait_ge(bank_copied, j * (TQ * TC) + (q * TC + c + 1))
                    dve.scalar_tensor_tensor(tiles16[:, 2 + q % 2, 1, c, :], bank(c % 4), SPLIT,
                                             tiles16[:, 2 + q % 2, 0, c, :], ALU.mult, ALU.subtract)\
                        .then_inc(bank_split, 1)

            def sum_rows(j, q):
                dve.wait_ge(rows_in[q % 2], j * 32 + 16 * (q // 2 + 1))
                dve.tensor_reduce(rs_part[:, q, ds(j * BPC, BPC)],
                                  tiles[:, q % 2, :].rearrange("p (b m) -> p b m", b=BPC),
                                  X_AX, ALU.add).then_inc(rows_summed, 1)

            def split(k, j, src):
                hi, lo = (part[:, ds(j * CH, CH)] for part in operand_of[k])
                link(dve.tensor_scalar(hi, src, SPLIT, None, ALU.mult))
                dve.scalar_tensor_tensor(lo, src, SPLIT, hi, ALU.mult, ALU.subtract).then_inc(x_ready[k], 1)
                dve.wait_ge(x_ready[k], j + 1)

            def scale_x(k, r):
                def scale(j):
                    return dve.tensor_tensor(by_block(scaled_x[:, j * CH:(j + 1) * CH]),
                                             by_block(xres[:, j * CH:(j + 1) * CH]),
                                             over_features(r[:, j * BPC:(j + 1) * BPC]), ALU.mult)

                for j in range(2):
                    link(scale(j))
                    split(k, j, scaled_x[:, j * CH:(j + 1) * CH])
                for j in range(2, NCH):
                    mark(scale(j))
                settle()
                dve.sem_inc(x_scaled, 1)
                for j in range(2, NCH):
                    split(k, j, scaled_x[:, j * CH:(j + 1) * CH])

            def sum_chunk(j):
                dve.wait_ge(rows_summed, j * TQ + TQ)
                dve.tensor_reduce(rowsum[:, ds(j * BPC, BPC)],
                                  rs_part[:, :, ds(j * BPC, BPC)].rearrange("p q n -> p n q"), X_AX,
                                  ALU.add).then_inc(deg_ready, 1)

            def scale_chunk(j):
                dve.wait_ge(deg_root, j + 1)
                link(dve.reciprocal(rdeg[:, ds(j * BPC, BPC)], deg[:, ds(j * BPC, BPC)]))
                link(dve.tensor_tensor(by_block(scaled_x[:, ds(j * CH, CH)]), by_block(xres[:, ds(j * CH, CH)]),
                                       over_features(rdeg[:, ds(j * BPC, BPC)]), ALU.mult))
                split(K_AGG1, j, scaled_x[:, ds(j * CH, CH)])

            for q in range(TQ):
                sum_rows(0, q)
                split_tile(0, q)
            for h in range(HEADS):
                for w4, w in ((wq4, W_Q), (wk4, W_K)):
                    link(dve.tensor_copy(w4[:, h, :, :], w[:, C * h:C * (h + 1)].unsqueeze(1)
                                         .to_broadcast([P, 4, C])))
            for t in (wq4[:, :, :, :].rearrange("p h r c -> p (h r c)"),
                      wk4[:, :, :, :].rearrange("p h r c -> p (h r c)"), bq4[:, :], bk4[:, :]):
                link(dve.tensor_scalar(t, t, SPLIT, None, ALU.mult))
            link(dve.tensor_scalar(bq4_lo[:, :], bq4[:, :], lo_q[:, :], None, ALU.mult))
            link(dve.tensor_scalar(bk4_lo[:, :], bk4[:, :], lo_k[:, :], None, ALU.mult))
            dve.wait_ge(x_in, 16)
            with dve.Fori(1, NCH) as j:
                chain.enter(j, 1, 3)
                for q in range(TQ):
                    sum_rows(j, q)
                    split_tile(j, q)
                    if q == 0:
                        sum_chunk(j - 1)
                    if q == 1:
                        scale_chunk(j - 1)
            chain.leave(NCH - 1)
            sum_chunk(NCH - 1)
            scale_chunk(NCH - 1)


            def layernorm(j, s, k, count):
                link(dve.tensor_reduce(e_sum[:, :], by_block(e_t[:, :]), X_AX, ALU.add))
                link(dve.tensor_scalar(e_sum[:, :], e_sum[:, :], 1.0 / F, None, ALU.mult))
                link(dve.tensor_tensor(by_block(e_c[:, :]), by_block(e_t[:, :]),
                                       over_features(e_sum[:, :]), ALU.subtract))
                link(dve.tensor_tensor(e_q[:, :], e_c[:, :], e_c[:, :], ALU.mult))
                dve.tensor_reduce(e_var[:, :], by_block(e_q[:, :]), X_AX, ALU.add).then_inc(var_ready, 1)
                dve.wait_ge(std_ready, count)
                link(dve.reciprocal(e_std[:, :], e_std[:, :]))

            def product(k):
                first_c = NCH * k

                def epilogue(j, s):
                    eps = by_block(bank(2 + s))
                    e_b, x_b = by_block(e_t[:, :]), by_block(xres[:, ds(j * CH, CH)])
                    dve.wait_ge(e_ready, j + (first_c + 1))
                    if k == K_AGG1:
                        link(dve.tensor_tensor(e_b, eps, over_features(rdeg[:, ds(j * BPC, BPC)]), ALU.mult))
                        dve.sem_inc(e_taken, 1)
                        link(dve.tensor_tensor(e_b, e_b, over_blocks(B_1), ALU.add))
                        link(dve.scalar_tensor_tensor(zc[:, s, :], e_t[:, :], 0.1, e_t[:, :], ALU.mult, ALU.max))
                        dve.sem_inc(z_ready, 1)
                        link(dve.tensor_tensor(zsq[:, :], zc[:, s, :], zc[:, s, :], ALU.mult))
                        link(dve.tensor_reduce(sqn[:, ds(j * BPC, BPC)], by_block(zsq[:, :]), X_AX, ALU.add))
                        dve.wait_ge(zT_ready, j + 1)
                        dve.scalar_tensor_tensor(zT[1][:, ds(j * CH, CH)], bank(4 + s), SPLIT,
                                                 zT[0][:, ds(j * CH, CH)], ALU.mult, ALU.subtract)\
                            .then_inc(zT_split, 1)
                        ps = PS[0:JD, 6 * CH:7 * CH]
                        dve.wait_ge(sq_ready, j + 1)
                        link(dve.tensor_copy(sq_h[:, :], ps))
                        link(dve.tensor_tensor(sq_r[:, :], ps, sq_h[:, :], ALU.subtract))
                        link(dve.tensor_copy(sq_m[:, :], sq_r[:, :]))
                        link(dve.tensor_tensor(sq_r[:, :], sq_r[:, :], sq_m[:, :], ALU.subtract))
                        link(dve.tensor_scalar(sq_c[:, :], sq_h[:, :], ident[0:JD, 0:1], None, ALU.mult))
                        link(dve.scalar_tensor_tensor(sq_c[:, :], sq_m[:, :], ident[0:JD, 1:2], sq_c[:, :],
                                                      ALU.mult, ALU.add))
                        dve.scalar_tensor_tensor(sq3[:, ds(j * CH, CH)], sq_r[:, :], ident[0:JD, 2:3],
                                                 sq_c[:, :], ALU.mult, ALU.add).then_inc(sq_split, 1)
                    elif k == K_AGG2:
                        link(dve.tensor_tensor(e_b, eps, over_features(rdeg2[:, ds(j * BPC, BPC)]), ALU.mult))
                        dve.sem_inc(e_taken, 1)
                        link(dve.tensor_tensor(e_b, e_b, over_blocks(B_2), ALU.add))
                        link(dve.tensor_tensor(e_b, e_b, x_b, ALU.add))
                        layernorm(j, s, k, j + 1)
                        link(dve.tensor_tensor(x_b, by_block(e_c[:, :]), over_features(e_std[:, :]), ALU.mult))
                    elif k in (K_HOP1, K_HOP2):
                        n_sw = 0 if k == K_HOP1 else NCH
                        dve.tensor_tensor(e_b, eps, over_blocks(B_H), ALU.add).then_inc(swish_in, 1)
                        dve.wait_ge(swish_exp, j + (n_sw + 1))
                        dve.sem_inc(e_taken, 1)
                        link(dve.tensor_scalar(e_exp[:, :], e_exp[:, :], 1.0, None, ALU.add))
                        link(dve.reciprocal(e_exp[:, :], e_exp[:, :]))
                        if k == K_HOP1:
                            link(dve.tensor_tensor(e_t[:, :], e_t[:, :], e_exp[:, :], ALU.mult))
                            split(K_HOP2, j, e_t[:, :])
                        else:
                            link(dve.tensor_tensor(e_t[:, :], e_t[:, :], e_exp[:, :], ALU.mult))
                            link(dve.tensor_tensor(e_b, e_b, x_b, ALU.add))
                            layernorm(j, s, k, j + (NCH + 1))
                            link(dve.tensor_tensor(x_b, by_block(e_c[:, :]), over_features(e_std[:, :]),
                                                   ALU.mult))
                            split(K_FRM1, j, xres[:, ds(j * CH, CH)])
                    elif k == K_FRM1:
                        link(dve.tensor_tensor(e_b, eps, over_features(fscale[:, ds(j * BPC, BPC)]), ALU.mult))
                        dve.sem_inc(e_taken, 1)
                        split(K_FRM2, j, e_t[:, :])
                    else:
                        link(dve.tensor_tensor(e_b, eps, over_blocks(B_F), ALU.add))
                        dve.sem_inc(e_taken, 1)
                        link(dve.tensor_tensor(e_b, e_b, x_b, ALU.add))
                        layernorm(j, s, k, j + (2 * NCH + 1))
                        dve.tensor_tensor(by_block(oc[:, s, :]), by_block(e_c[:, :]),
                                          over_features(e_std[:, :]), ALU.mult).then_inc(out_ready, 1)

                def sum_near(j, s):
                    for b in range(BPC):
                        dve.wait_ge(rows_gathered[b], j * (16 * K_NEAR) + 16 * K_NEAR)
                        u = near_u[:, s * BPC + b, :]
                        w0 = (j * BPC + b) * K_NEAR
                        link(dve.tensor_scalar(u, gat[:, b, 0, :], near_s[:, ds(w0, 1)], None, ALU.mult))
                        for n in range(1, K_NEAR):
                            ins = dve.scalar_tensor_tensor(u, gat[:, b, n, :], near_s[:, ds(w0 + n, 1)], u,
                                                           ALU.mult, ALU.add)
                            if n < K_NEAR - 1:
                                link(ins)
                        ins.then_inc(u_ready, 1)

                per = {K_AGG1: 11, K_AGG2: 9 + 12, K_HOP1: 4, K_HOP2: 11, K_FRM1: 2, K_FRM2: 7}[k]

                if k == K_AGG2:
                    sum_near(0, 0)
                    sum_near(1, 1)
                    epilogue(0, 0)
                    n0 = chain.base + chain.n
                    with dve.Fori(1, NCH // 2) as i:
                        chain.enter(i, 1, 2 * per)
                        sum_near(i * 2, 0)
                        epilogue(i * 2 - 1, 1)
                        sum_near(i * 2 + 1, 1)
                        epilogue(i * 2, 0)
                    chain.leave(NCH // 2 - 1)
                    stage_chunk(0, 0)
                    stage_chunk(1, 1)
                    epilogue(NCH - 1, 1)
                    dve.sem_inc(att_done, 1)
                elif k == K_FRM2:
                    epilogue(0, 0)
                    epilogue(1, 1)
                    with dve.Fori(1, NCH // 2) as i:
                        chain.enter(i, 1, 2 * per)
                        for s in range(2):
                            dve.wait_ge(out_stored[s], i * 16)
                            epilogue(i * 2 + s, s)
                    chain.leave(NCH // 2 - 1)
                else:
                    with dve.Fori(0, NCH // 2) as i:
                        chain.enter(i, 0, 2 * per)
                        for s in range(2):
                            epilogue(i * 2 + s, s)
                    chain.leave(NCH // 2)

            def stage_chunk(j, s):
                dve.tensor_copy(oc[:, s, :], xres[:, ds(j * CH, CH)]).then_inc(kx_staged, 1)

            product(K_AGG1)

            def keep_places(b, s):
                dve.wait_ge(near_found, b + 1)
                mark(dve.tensor_copy(near_idx[:, ds(b * K_NEAR, K_NEAR)], idx8[:, s, 0:K_NEAR]))

            def search(b, s, first):
                dve.wait_ge(keys_copied, b * NG + NG)
                apart(dve)
                mark(dve.max(top8[:, s, :], key_rows[s]))
                if not first:
                    keep_places(b - 1, 1 - s)
                settle()
                apart(dve)
                dve.max_index(idx8[:, s, :], top8[:, s, :], key_rows[s]).then_inc(near_found, 1)
                mark(dve.tensor_copy(near_key[:, ds(b * K_NEAR, K_NEAR)], top8[:, s, 0:K_NEAR]))

            search(0, 0, True)
            search(1, 1, False)
            with dve.Fori(1, NB // 2) as i:
                chain.enter(i, 1, 6)
                search(i * 2, 0, False)
                search(i * 2 + 1, 1, False)
            chain.leave(NB // 2 - 1)
            keep_places(NB - 1, 1)
            settle()

            nk = near_key[:, :].rearrange("p (b n) -> p b n", n=K_NEAR)
            ns = near_s[:, :].rearrange("p (b n) -> p b n", n=K_NEAR)
            link(dve.scalar_tensor_tensor(ns, nk, -2.0 / SPLIT ** 2, over_features(sqn[:, :], NB, K_NEAR), ALU.mult, ALU.add))
            dve.tensor_scalar(near_s[:, :], near_s[:, :], 0.0, 1e-10, ALU.max, ALU.add).then_inc(d_near, 1)
            dve.wait_ge(s_near, 2)
            link(dve.tensor_reduce(rdeg2[:, :], ns, X_AX, ALU.add))
            dve.tensor_tensor(rdeg2[:, :], rdeg2[:, :], rowsum[:, :], ALU.add).then_inc(deg2_ready, 1)
            link(dve.tensor_scalar(near_s[:, :], near_s[:, :], SPLIT ** 2, None, ALU.mult))
            dve.wait_ge(deg2_root, 1)
            link(dve.reciprocal(rdeg2[:, :], deg[:, :]))
            scale_x(K_AGG2, rdeg2)

            product(K_AGG2)

            khi = maskb[:, 0, 0:2 * CH].bitcast(f16).rearrange("p (r n) -> p r n", r=2)

            def kv_chunk(j, s, nxt):
                if nxt:
                    dve.wait_ge(kx_turned, j + 1)
                    stage_chunk(j + 2, s)
                dve.wait_ge(v_ready, j + 1)
                dve.tensor_tensor(by_block(V[:, ds(j * CH, CH)]), by_block(bank(6 + s)), over_blocks(B_V),
                                  ALU.add).then_inc(v_taken, 1)
                for h in range(HEADS):
                    dve.wait_ge(k_halved, j * HEADS + (h + 1))
                    dve.scalar_tensor_tensor(kst[:, h, ds(j * CH, CH)], bank(h), bk4[:, h:h + 1],
                                             khi[:, h % 2, :], ALU.add, ALU.add).then_inc(k_stacked, 1)

            with dve.Fori(0, NCH // 2 - 1) as i:
                kv_chunk(i * 2, 0, True)
                kv_chunk(i * 2 + 1, 1, True)
            kv_chunk(NCH - 2, 0, False)
            kv_chunk(NCH - 1, 1, False)
            dve.wait_ge(k_stacked, NCH * HEADS)

            def take_scores(v, s, h, t):
                dve.wait_ge(s_ready, v * STEPS + (t + 1))
                apart(dve)
                dve.tensor_tensor_reduce(
                    out=att_w[h][:, t * CH:(t + 1) * CH], in0=bank(t % S_RING),
                    in1=maskb[:, s, t * CH:(t + 1) * CH], scale=1.0, scalar=-3.0e38, op0=ALU.add,
                    op1=ALU.max, accum_out=mx_part[:, h % 2, t:t + 1]).then_inc(s_taken, 1)

            def row_max(v, s, h):
                dve.wait_ge(s_taken, v * STEPS + STEPS)
                mark(dve.tensor_reduce(mx4[:, s, h:h + 1], mx_part[:, h % 2, :], X_AX, ALU.max))

            def bias_exp(h, s):
                settle()
                dve.tensor_scalar(nbias[:, h:h + 1], mx4[:, s, h:h + 1], -ATT_SCALE / SPLIT ** 2, None,
                                  ALU.mult).then_inc(max_ready, 1)

            def stack_queries(b, s, pr, m):
                dve.wait_ge(q_halved, b * 2 + (pr + 1))
                for hh in range(2):
                    h = 2 * pr + hh
                    ins = dve.scalar_tensor_tensor(qst[:, s, h, :], bank(m)[:, P + hh * P:P + (hh + 1) * P],
                                                   bq4[:, h:h + 1], q_hi[:, hh, :], ALU.add, ALU.add)
                ins.then_inc(q_stacked, 1)

            def take_xr(b, m):
                dve.wait_ge(q_ready, b * 2 + 1)
                dve.tensor_tensor(xr_new[:, :], bank(m)[:, 0:F], B_S, ALU.add).then_inc(xr_taken, 1)

            def keep_xr(b, s):
                dve.wait_ge(xr_taken, b + 1)
                mark(dve.tensor_copy(cat[:, s, F:2 * F], xr_new[:, :]))

            def copy_turned(v, t):
                dve.wait_ge(pt_ready, v * STEPS + (t + 1))
                dve.tensor_copy(pts[t % T_RING], bank(S_RING + t % T_RING)).then_inc(pt_by_dve, 1)

            def weigh_heads(b, s, part):
                if part == 0:
                    dve.wait_ge(exp_done, b * (HEADS * N // EXP) + (HEADS * N // EXP))
                    mark(dve.tensor_reduce(den4[:, :], den[:, s, :, :], X_AX, ALU.add))
                elif part == 1:
                    settle()
                    mark(dve.reciprocal(rden4[:, :], den4[:, :]))
                else:
                    settle()
                    mark(dve.scalar_tensor_tensor(rden4[:, :], mx4[:, s, :], MASKED / 10, rden4[:, :],
                                                  ALU.is_gt, ALU.mult))

            def normalise(b, s, m, part):
                if part == 0:
                    dve.wait_ge(o_turned, b + 1)
                    mark(dve.tensor_reduce(o_sum[:, :].rearrange("p (h c) -> p h c", h=HEADS),
                                           bank(m).rearrange("p (h r c) -> p h c r", h=HEADS, r=4),
                                           X_AX, ALU.add))
                elif part == 1:
                    settle()
                    mark(dve.tensor_tensor(cat[:, s, 0:F].rearrange("p (c h) -> p h c", h=HEADS),
                                           o_sum[:, :].rearrange("p (h c) -> p h c", h=HEADS),
                                           over_features(rden4[:, :], HEADS, C), ALU.mult))
                elif part == 2:
                    settle()
                    mark(dve.tensor_tensor(cat[:, s, 2 * F:3 * F], cat[:, s, 0:F], cat[:, s, F:2 * F],
                                           ALU.subtract))
                else:
                    settle()
                    apart(dve)
                    dve.tensor_tensor_reduce(out=cat_t[:, :], in0=cat[:, s, :], in1=wb_sb[:, :],
                                             scale=1.0, scalar=0.0, op0=ALU.mult, op1=ALU.add,
                                             accum_out=gate_z[:, :]).then_inc(gate_in, 1)

            def blend(b, s, part):
                if part == 0:
                    dve.wait_ge(gate_exp, b + 1)
                    mark(dve.tensor_scalar(gate_b[:, :], gate_e[:, :], -1.0, -1.0, ALU.mult, ALU.add))
                elif part == 1:
                    settle()
                    mark(dve.reciprocal(gate_b[:, :], gate_b[:, :]))
                elif part == 2:
                    settle()
                    mark(dve.scalar_tensor_tensor(att[:, :], cat[:, s, 2 * F:3 * F], gate_b[:, :],
                                                  cat[:, s, 0:F], ALU.mult, ALU.add))
                elif part == 3:
                    settle()
                    mark(dve.tensor_tensor(att[:, :], att[:, :], xres[:, ds(b * F, F)], ALU.add))
                elif part == 4:
                    settle()
                    mark(dve.bn_stats(st6[:, :], att[:, :]))
                elif part == 5:
                    settle()
                    apart(dve)
                    dve.tensor_copy(xres[:, ds(b * F, F)], att[:, :]).then_inc(att_kept, 1)
                    apart(dve)
                    mark(dve.bn_aggr(mv[:, :], st6[:, :]))
                else:
                    settle()
                    dve.wait_ge(att_kept, b + 1)
                    apart(dve)
                    dve.tensor_copy(mv_all[:, ds(b, 1), :], mv[:, :].unsqueeze(1)).then_inc(avar_ready, 1)

            def finish(j):
                for b in range(j * BPC, (j + 1) * BPC):
                    dve.tensor_scalar(xres[:, b * F:(b + 1) * F], xres[:, b * F:(b + 1) * F],
                                      mv_all[:, b, 0:1], a_rstd[:, b:b + 1],
                                      ALU.subtract, ALU.mult).then_inc(att_done, 1)
                dve.wait_ge(att_done, (j + 1) * BPC + 1)
                split(K_HOP1, j, xres[:, j * CH:(j + 1) * CH])

            def phase(b, s, h, prev, nxt):
                v = b * HEADS + h
                for t in range(STEPS):
                    if t in DVE_STEPS:
                        copy_turned(v, t)
                    if h < 2 or nxt:
                        if h == 2 and t == 0:
                            dve.wait_ge(mask_ready, b + 2)
                        take_scores(v + 2, s if h < 2 else 1 - s, (h + 2) % HEADS, t)
                    if h < 3 or nxt:
                        if t == 0:
                            row_max(v + 1, s if h < 3 else 1 - s, (h + 1) % HEADS)
                        if t == 1:
                            bias_exp((h + 1) % HEADS, s if h < 3 else 1 - s)
                    if h == 0 and prev and t < 3:
                        weigh_heads(b - 1, 1 - s, t)
                    if h == 1 and nxt:
                        if t == 1:
                            take_xr(b + 1, 7 - s)
                        if t in (4, 7):
                            stack_queries(b + 1, 1 - s, t // 5, 7 - s)
                    if h == 2 and prev and 3 <= t < 7:
                        normalise(b - 1, 1 - s, 7 - s, t - 3)
                    if h == 3 and prev:
                        if 1 <= t:
                            blend(b - 1, 1 - s, t - 1)
                    if h == 3 and nxt and t == 6:
                        keep_xr(b + 1, 1 - s)

            dve.wait_ge(mask_rows_in, 16)
            dve.tensor_scalar(maskb[:, 0, :], adj_rows[:, :], 0.0, MASKED, ALU.is_equal, ALU.mult)\
                .then_inc(mask_ready, 1)
            take_xr(0, 7)
            stack_queries(0, 0, 0, 7)
            stack_queries(0, 0, 1, 7)
            keep_xr(0, 0)
            dve.wait_ge(mask_ready, 1)
            for v in range(2):
                for t in range(STEPS):
                    take_scores(v, 0, v, t)
                if v == 0:
                    row_max(0, 0, 0)
                    bias_exp(0, 0)
            for s in range(2):
                for h in range(HEADS):
                    phase(s, s, h, s > 0, True)
            with dve.Fori(1, NB // 2 - 1) as i:
                chain.enter(i, 1, 2 * (4 + 3 + 3 + 6 + 1))
                for s in range(2):
                    for h in range(HEADS):
                        phase(i * 2 + s, s, h, True, True)
            chain.leave(NB // 2 - 2)
            for s in range(2):
                for h in range(HEADS):
                    phase(NB - 2 + s, s, h, True, s == 0)
            settle()
            dve.wait_ge(astd_ready, 1)
            link(dve.reciprocal(a_rstd[:, 0:NB - BPC], a_std[:, 0:NB - BPC]))
            dve.wait_ge(o_ready, NB)
            for j in range(NCH - 1):
                finish(j)
            for part in range(3):
                weigh_heads(NB - 1, 1, part)
            for part in range(4):
                normalise(NB - 1, 1, 7, part)
            for part in range(7):
                blend(NB - 1, 1, part)
            dve.wait_ge(astd_ready, 2)
            link(dve.reciprocal(a_rstd[:, NB - BPC:NB], a_std[:, NB - BPC:NB]))
            finish(NCH - 1)

            for k in (K_HOP1, K_HOP2, K_FRM1, K_FRM2):
                product(k)


_INS = ['x', 'adj', 'L0_gnn_W1', 'L0_gnn_b1', 'L0_gnn_W2', 'L0_gnn_b2', 'L1_gnn_Wq', 'L1_gnn_bq',
        'L1_gnn_Wk', 'L1_gnn_bk', 'L1_gnn_Wv', 'L1_gnn_bv', 'L1_gnn_Ws', 'L1_gnn_bs', 'L1_gnn_Wb',
        'L2_gnn_W', 'L2_gnn_b', 'L3_gnn_d_list', 'L3_gnn_weight', 'L3_gnn_filt', 'L3_gnn_bias']
_OUTS = [((4096, 128), 'float32')]


def kernel(**inputs):
    import numpy as _np
    import concourse.bacc as _bacc
    from concourse import mybir as _mybir
    from concourse.bass_utils import run_bass_kernel_spmd as _run

    nc = _bacc.Bacc("TRN2", target_bir_lowering=False, num_devices=1)
    arrays, args = {}, []
    for name in _INS:
        a = _np.ascontiguousarray(inputs[name])
        arrays[f"in_{name}_dram"] = a
        args.append(nc.dram_tensor(f"in_{name}_dram", a.shape, _mybir.dt.from_np(a.dtype), kind="ExternalInput").ap())
    for i, (shape, dtype) in enumerate(_OUTS):
        dt = _mybir.dt.from_np(_np.dtype(dtype))
        args.append(nc.dram_tensor(f"out_{i}_dram", shape, dt, kind="ExternalOutput").ap())
    graph_layers_kernel(nc, *args)
    r = _run(nc, [arrays], core_ids=[0])
    got = tuple(r.results[0][f"out_{i}_dram"] for i in range(len(_OUTS)))
    return got[0]
```
